# Optimizing a Trainium2 kernel written in Bass

```python
import numpy as np
import jax
import jax.numpy as jnp

def _softmax(x, axis=-1):
    return jax.nn.softmax(x, axis=axis)

def _gelu(x):
    return jax.nn.gelu(x, approximate=True)

def _silu(x):
    return jax.nn.silu(x)

def _sigmoid(x):
    return jax.nn.sigmoid(x)

def _layernorm(x, axis=-1, eps=1e-05):
    m = jnp.mean(x, axis=axis, keepdims=True)
    v = jnp.var(x, axis=axis, keepdims=True)
    return (x - m) / jnp.sqrt(v + eps)

def _scatter_add(tgt, idx, src, axis=0):
    return tgt.at[idx].add(src)

def _segment_sum(src, seg, n):
    return jax.ops.segment_sum(src, seg, n)
kernel_name = 'mk_prb_d2_jaxref_r8_22b6f9'

def setup_inputs(seed: int=0):
    np.random.seed(seed)
    _w = jnp.asarray

    def _L0_attn_setup():
        import jax, jax.numpy as jnp
        import numpy as np
        from math import log2, floor
        HEADS = 16
        DIM_HEAD = 64
        SCALE = DIM_HEAD ** (-0.5)

        def _get_slopes(heads):

            def pow2_slopes(n):
                start = 2 ** (-2 ** (-(log2(n) - 3)))
                return [start * start ** i for i in range(n)]
            if log2(heads).is_integer():
                return pow2_slopes(heads)
            c = 2 ** floor(log2(heads))
            return pow2_slopes(c) + pow2_slopes(2 * c)[0::2][:heads - c]
        key = jax.random.key(seed)
        k1, k2, k3 = jax.random.split(key, 3)
        b, n, dim = (2, 256, 128)
        inner = HEADS * DIM_HEAD
        x = jax.random.normal(k1, (b, n, dim), dtype=jnp.float32)
        w_qkv = jax.random.normal(k2, (dim, 3 * inner), dtype=jnp.float32) * dim ** (-0.5)
        w_out = jax.random.normal(k3, (inner, dim), dtype=jnp.float32) * inner ** (-0.5)
        b_out = jnp.zeros((dim,), dtype=jnp.float32)
        return {'x': x, 'w_qkv': w_qkv, 'w_out': w_out, 'b_out': b_out}
    _L0_attn_in = _L0_attn_setup()

    def _L0_ffn_setup():
        import jax, jax.numpy as jnp
        import numpy as np
        B, S, H, F, G = (8, 256, 128, 512, 128)
        EPS = 1e-05

        def _dequant(q, scales, g):
            K, N = q.shape
            w = (q.astype(jnp.float32) - 128.0).reshape(K // g, g, N) * scales[:, None, :]
            return w.reshape(K, N)
        key = jax.random.key(seed)
        ks = jax.random.split(key, 8)
        x = jax.random.normal(ks[0], (B, S, H), dtype=jnp.float32)
        ln_gamma = jnp.ones((H,), jnp.float32)
        ln_beta = jnp.zeros((H,), jnp.float32)
        fc1_q = jax.random.randint(ks[1], (H, F), 0, 32, dtype=jnp.int32)
        fc2_q = jax.random.randint(ks[2], (F, H), 0, 32, dtype=jnp.int32)
        fc1_scales = jax.random.uniform(ks[3], (H // G, F), jnp.float32) * 0.02 + 0.001
        fc2_scales = jax.random.uniform(ks[4], (F // G, H), jnp.float32) * 0.02 + 0.001
        fc1_bias = jax.random.normal(ks[5], (F,), jnp.float32) * 0.02
        fc2_bias = jax.random.normal(ks[6], (H,), jnp.float32) * 0.02
        return {'x': x, 'ln_gamma': ln_gamma, 'ln_beta': ln_beta, 'fc1_q': fc1_q, 'fc1_scales': fc1_scales, 'fc1_bias': fc1_bias, 'fc2_q': fc2_q, 'fc2_scales': fc2_scales, 'fc2_bias': fc2_bias}
    _L0_ffn_in = _L0_ffn_setup()

    def _L1_attn_setup():
        import math
        import jax, jax.numpy as jnp
        import numpy as np
        EMBED_DIM = 128
        NUM_HEADS = 8
        HEAD_DIM = EMBED_DIM // NUM_HEADS // 2
        DEPTH = 12
        LAMBDA_INIT = 0.8 - 0.6 * math.exp(-0.3 * DEPTH)
        B, S = (2, 256)
        ROPE_THETA = 10000.0
        EPS = 1e-08

        def rope_rotate(x):
            d = x.shape[-1]
            inv_freq = 1.0 / ROPE_THETA ** (jnp.arange(0, d, 2, dtype=jnp.float32) / d)
            t = jnp.arange(x.shape[1], dtype=jnp.float32)
            freqs = t[:, None] * inv_freq[None, :]
            freqs = jnp.repeat(freqs, 2, axis=-1)
            cos = jnp.cos(freqs)[None, :, None, :].astype(x.dtype)
            sin = jnp.sin(freqs)[None, :, None, :].astype(x.dtype)
            xr = x.reshape(*x.shape[:-1], d // 2, 2)
            x1, x2 = (xr[..., 0], xr[..., 1])
            rot = jnp.stack([-x2, x1], axis=-1).reshape(x.shape)
            return x * cos + rot * sin

        def sdpa(q, k, v):
            d = q.shape[-1]
            scores = jnp.einsum('bshd,bthd->bhst', q, k) * d ** (-0.25)
            w = jax.nn.softmax(scores, axis=-1)
            return jnp.einsum('bhst,bthd->bshd', w, v)
        key = jax.random.key(seed)
        ks = jax.random.split(key, 10)
        scale = 1.0 / math.sqrt(EMBED_DIM)
        return {'x': jax.random.normal(ks[0], (B, S, EMBED_DIM), jnp.float32), 'Wq': jax.random.normal(ks[1], (EMBED_DIM, EMBED_DIM), jnp.float32) * scale, 'Wk': jax.random.normal(ks[2], (EMBED_DIM, EMBED_DIM), jnp.float32) * scale, 'Wv': jax.random.normal(ks[3], (EMBED_DIM, EMBED_DIM), jnp.float32) * scale, 'Wo': jax.random.normal(ks[4], (EMBED_DIM, EMBED_DIM), jnp.float32) * scale, 'lambda_q1': jax.random.normal(ks[5], (HEAD_DIM,), jnp.float32) * 0.1, 'lambda_k1': jax.random.normal(ks[6], (HEAD_DIM,), jnp.float32) * 0.1, 'lambda_q2': jax.random.normal(ks[7], (HEAD_DIM,), jnp.float32) * 0.1, 'lambda_k2': jax.random.normal(ks[8], (HEAD_DIM,), jnp.float32) * 0.1, 'ln_w': jnp.ones((2 * HEAD_DIM,), jnp.float32), 'ln_b': jnp.zeros((2 * HEAD_DIM,), jnp.float32)}
    _L1_attn_in = _L1_attn_setup()

    def _L1_ffn_setup():
        import jax, jax.numpy as jnp
        import numpy as np
        B, S, H, F, G = (8, 256, 128, 512, 128)
        EPS = 1e-05

        def _dequant(q, scales, g):
            K, N = q.shape
            w = (q.astype(jnp.float32) - 128.0).reshape(K // g, g, N) * scales[:, None, :]
            return w.reshape(K, N)
        key = jax.random.key(seed)
        ks = jax.random.split(key, 8)
        x = jax.random.normal(ks[0], (B, S, H), dtype=jnp.float32)
        ln_gamma = jnp.ones((H,), jnp.float32)
        ln_beta = jnp.zeros((H,), jnp.float32)
        fc1_q = jax.random.randint(ks[1], (H, F), 0, 32, dtype=jnp.int32)
        fc2_q = jax.random.randint(ks[2], (F, H), 0, 32, dtype=jnp.int32)
        fc1_scales = jax.random.uniform(ks[3], (H // G, F), jnp.float32) * 0.02 + 0.001
        fc2_scales = jax.random.uniform(ks[4], (F // G, H), jnp.float32) * 0.02 + 0.001
        fc1_bias = jax.random.normal(ks[5], (F,), jnp.float32) * 0.02
        fc2_bias = jax.random.normal(ks[6], (H,), jnp.float32) * 0.02
        return {'x': x, 'ln_gamma': ln_gamma, 'ln_beta': ln_beta, 'fc1_q': fc1_q, 'fc1_scales': fc1_scales, 'fc1_bias': fc1_bias, 'fc2_q': fc2_q, 'fc2_scales': fc2_scales, 'fc2_bias': fc2_bias}
    _L1_ffn_in = _L1_ffn_setup()
    _d = {'L0_attn_x': _L0_attn_in['x'], 'L0_attn_w_qkv': _L0_attn_in['w_qkv'], 'L0_attn_w_out': _L0_attn_in['w_out'], 'L0_attn_b_out': _L0_attn_in['b_out'], 'L0_ffn_ln_gamma': _L0_ffn_in['ln_gamma'], 'L0_ffn_ln_beta': _L0_ffn_in['ln_beta'], 'L0_ffn_fc1_q': _L0_ffn_in['fc1_q'], 'L0_ffn_fc1_scales': _L0_ffn_in['fc1_scales'], 'L0_ffn_fc1_bias': _L0_ffn_in['fc1_bias'], 'L0_ffn_fc2_q': _L0_ffn_in['fc2_q'], 'L0_ffn_fc2_scales': _L0_ffn_in['fc2_scales'], 'L0_ffn_fc2_bias': _L0_ffn_in['fc2_bias'], 'L1_attn_Wq': _L1_attn_in['Wq'], 'L1_attn_Wk': _L1_attn_in['Wk'], 'L1_attn_Wv': _L1_attn_in['Wv'], 'L1_attn_Wo': _L1_attn_in['Wo'], 'L1_attn_lambda_q1': _L1_attn_in['lambda_q1'], 'L1_attn_lambda_k1': _L1_attn_in['lambda_k1'], 'L1_attn_lambda_q2': _L1_attn_in['lambda_q2'], 'L1_attn_lambda_k2': _L1_attn_in['lambda_k2'], 'L1_attn_ln_w': _L1_attn_in['ln_w'], 'L1_attn_ln_b': _L1_attn_in['ln_b'], 'L1_ffn_ln_gamma': _L1_ffn_in['ln_gamma'], 'L1_ffn_ln_beta': _L1_ffn_in['ln_beta'], 'L1_ffn_fc1_q': _L1_ffn_in['fc1_q'], 'L1_ffn_fc1_scales': _L1_ffn_in['fc1_scales'], 'L1_ffn_fc1_bias': _L1_ffn_in['fc1_bias'], 'L1_ffn_fc2_q': _L1_ffn_in['fc2_q'], 'L1_ffn_fc2_scales': _L1_ffn_in['fc2_scales'], 'L1_ffn_fc2_bias': _L1_ffn_in['fc2_bias']}
    _x0 = _d['L0_attn_x']
    _d['L0_attn_x'] = jax.random.normal(jax.random.fold_in(jax.random.key(seed), 1), (16, 512, 128), dtype=_x0.dtype)
    del _x0
    return _d

def reference(L0_attn_x, L0_attn_w_qkv, L0_attn_w_out, L0_attn_b_out, L0_ffn_ln_gamma, L0_ffn_ln_beta, L0_ffn_fc1_q, L0_ffn_fc1_scales, L0_ffn_fc1_bias, L0_ffn_fc2_q, L0_ffn_fc2_scales, L0_ffn_fc2_bias, L1_attn_Wq, L1_attn_Wk, L1_attn_Wv, L1_attn_Wo, L1_attn_lambda_q1, L1_attn_lambda_k1, L1_attn_lambda_q2, L1_attn_lambda_k2, L1_attn_ln_w, L1_attn_ln_b, L1_ffn_ln_gamma, L1_ffn_ln_beta, L1_ffn_fc1_q, L1_ffn_fc1_scales, L1_ffn_fc1_bias, L1_ffn_fc2_q, L1_ffn_fc2_scales, L1_ffn_fc2_bias):

    def _L0_attn_ref(x, w_qkv, w_out, b_out):
        import jax, jax.numpy as jnp
        import numpy as np
        from math import log2, floor
        HEADS = 16
        DIM_HEAD = 64
        SCALE = DIM_HEAD ** (-0.5)

        def _get_slopes(heads):

            def pow2_slopes(n):
                start = 2 ** (-2 ** (-(log2(n) - 3)))
                return [start * start ** i for i in range(n)]
            if log2(heads).is_integer():
                return pow2_slopes(heads)
            c = 2 ** floor(log2(heads))
            return pow2_slopes(c) + pow2_slopes(2 * c)[0::2][:heads - c]
        b, n, _ = x.shape
        qkv = x @ w_qkv
        q, k, v = jnp.split(qkv, 3, axis=-1)

        def to_heads(t):
            return t.reshape(b, n, HEADS, DIM_HEAD).transpose(0, 2, 1, 3)
        q, k, v = map(to_heads, (q, k, v))
        q = q * SCALE
        sim = jnp.einsum('bhid,bhjd->bhij', q, k)
        slopes = jnp.asarray(_get_slopes(HEADS), dtype=sim.dtype)[:, None, None]
        i = jnp.arange(n)
        rel = -jnp.abs(i[None, :] - i[:, None]).astype(sim.dtype)
        sim = sim + rel[None, :, :] * slopes
        causal = jnp.triu(jnp.ones((n, n), dtype=bool), 1)
        mask_value = -jnp.finfo(sim.dtype).max
        sim = jnp.where(causal, mask_value, sim)
        attn = jax.nn.softmax(sim, axis=-1)
        out = jnp.einsum('bhij,bhjd->bhid', attn, v)
        out = out.transpose(0, 2, 1, 3).reshape(b, n, HEADS * DIM_HEAD)
        return out @ w_out + b_out

    def _L0_ffn_ref(x, ln_gamma, ln_beta, fc1_q, fc1_scales, fc1_bias, fc2_q, fc2_scales, fc2_bias):
        import jax, jax.numpy as jnp
        import numpy as np
        B, S, H, F, G = (8, 256, 128, 512, 128)
        EPS = 1e-05

        def _dequant(q, scales, g):
            K, N = q.shape
            w = (q.astype(jnp.float32) - 128.0).reshape(K // g, g, N) * scales[:, None, :]
            return w.reshape(K, N)
        residual = x
        mu = jnp.mean(x, axis=-1, keepdims=True)
        var = jnp.mean(jnp.square(x - mu), axis=-1, keepdims=True)
        h = (x - mu) * jax.lax.rsqrt(var + EPS) * ln_gamma + ln_beta
        hf = h.reshape(-1, H)
        w1 = _dequant(fc1_q, fc1_scales, G)
        y = hf @ w1 + fc1_bias
        y = jax.nn.silu(y)
        w2 = _dequant(fc2_q, fc2_scales, G)
        z = y @ w2 + fc2_bias
        return residual + 0.5 * z.reshape(residual.shape)

    def _L1_attn_ref(x, Wq, Wk, Wv, Wo, lambda_q1, lambda_k1, lambda_q2, lambda_k2, ln_w, ln_b):
        import math
        import jax, jax.numpy as jnp
        import numpy as np
        EMBED_DIM = 128
        NUM_HEADS = 8
        HEAD_DIM = EMBED_DIM // NUM_HEADS // 2
        DEPTH = 12
        LAMBDA_INIT = 0.8 - 0.6 * math.exp(-0.3 * DEPTH)
        B, S = (2, 256)
        ROPE_THETA = 10000.0
        EPS = 1e-08

        def rope_rotate(x):
            d = x.shape[-1]
            inv_freq = 1.0 / ROPE_THETA ** (jnp.arange(0, d, 2, dtype=jnp.float32) / d)
            t = jnp.arange(x.shape[1], dtype=jnp.float32)
            freqs = t[:, None] * inv_freq[None, :]
            freqs = jnp.repeat(freqs, 2, axis=-1)
            cos = jnp.cos(freqs)[None, :, None, :].astype(x.dtype)
            sin = jnp.sin(freqs)[None, :, None, :].astype(x.dtype)
            xr = x.reshape(*x.shape[:-1], d // 2, 2)
            x1, x2 = (xr[..., 0], xr[..., 1])
            rot = jnp.stack([-x2, x1], axis=-1).reshape(x.shape)
            return x * cos + rot * sin

        def sdpa(q, k, v):
            d = q.shape[-1]
            scores = jnp.einsum('bshd,bthd->bhst', q, k) * d ** (-0.25)
            w = jax.nn.softmax(scores, axis=-1)
            return jnp.einsum('bhst,bthd->bshd', w, v)
        b, s, e = x.shape
        H, D = (NUM_HEADS, HEAD_DIM)
        q = (x @ Wq.T).reshape(b, s, 2 * H, D)
        k = (x @ Wk.T).reshape(b, s, 2 * H, D)
        v = (x @ Wv.T).reshape(b, s, H, 2, D)
        q = rope_rotate(q).reshape(b, s, H, 2, D)
        k = rope_rotate(k).reshape(b, s, H, 2, D)
        q1, q2 = (q[..., 0, :], q[..., 1, :])
        k1, k2 = (k[..., 0, :], k[..., 1, :])
        v1, v2 = (v[..., 0, :], v[..., 1, :])
        attn1 = sdpa(q1, k1, v1)
        attn2 = sdpa(q2, k2, v2)
        lam = jnp.exp(jnp.sum(lambda_q1 * lambda_k1)) - jnp.exp(jnp.sum(lambda_q2 * lambda_k2)) + LAMBDA_INIT
        diff = jnp.concatenate([attn1, attn2], axis=0)
        a = attn1 - lam * attn2
        a2 = jnp.concatenate([attn1[..., None, :], attn2[..., None, :]], axis=-2)
        a2 = a2[..., 0, :] - lam * a2[..., 1, :]
        attn1f = sdpa(q1, k1, jnp.concatenate([v1, v2], axis=-1) * 0 + jnp.concatenate([v1, v2], axis=-1))
        vfull = jnp.concatenate([v1, v2], axis=-1)
        o1 = sdpa(q1, k1, vfull)
        o2 = sdpa(q2, k2, vfull)
        o = o1 - lam * o2
        ms = jnp.mean(jnp.square(o), axis=-1, keepdims=True)
        o = o * jax.lax.rsqrt(ms + EPS) * ln_w + ln_b
        o = o * (1.0 - LAMBDA_INIT)
        o = o.reshape(b, s, e)
        return o @ Wo.T

    def _L1_ffn_ref(x, ln_gamma, ln_beta, fc1_q, fc1_scales, fc1_bias, fc2_q, fc2_scales, fc2_bias):
        import jax, jax.numpy as jnp
        import numpy as np
        B, S, H, F, G = (8, 256, 128, 512, 128)
        EPS = 1e-05

        def _dequant(q, scales, g):
            K, N = q.shape
            w = (q.astype(jnp.float32) - 128.0).reshape(K // g, g, N) * scales[:, None, :]
            return w.reshape(K, N)
        residual = x
        mu = jnp.mean(x, axis=-1, keepdims=True)
        var = jnp.mean(jnp.square(x - mu), axis=-1, keepdims=True)
        h = (x - mu) * jax.lax.rsqrt(var + EPS) * ln_gamma + ln_beta
        hf = h.reshape(-1, H)
        w1 = _dequant(fc1_q, fc1_scales, G)
        y = hf @ w1 + fc1_bias
        y = jax.nn.silu(y)
        w2 = _dequant(fc2_q, fc2_scales, G)
        z = y @ w2 + fc2_bias
        return residual + 0.5 * z.reshape(residual.shape)
    x = L0_attn_x
    xn = _layernorm(x, axis=-1)
    x = x + _L0_attn_ref(xn, L0_attn_w_qkv, L0_attn_w_out, L0_attn_b_out) + _L0_ffn_ref(xn, L0_ffn_ln_gamma, L0_ffn_ln_beta, L0_ffn_fc1_q, L0_ffn_fc1_scales, L0_ffn_fc1_bias, L0_ffn_fc2_q, L0_ffn_fc2_scales, L0_ffn_fc2_bias)
    xn = _layernorm(x, axis=-1)
    x = x + _L1_attn_ref(xn, L1_attn_Wq, L1_attn_Wk, L1_attn_Wv, L1_attn_Wo, L1_attn_lambda_q1, L1_attn_lambda_k1, L1_attn_lambda_q2, L1_attn_lambda_k2, L1_attn_ln_w, L1_attn_ln_b) + _L1_ffn_ref(xn, L1_ffn_ln_gamma, L1_ffn_ln_beta, L1_ffn_fc1_q, L1_ffn_fc1_scales, L1_ffn_fc1_bias, L1_ffn_fc2_q, L1_ffn_fc2_scales, L1_ffn_fc2_bias)
    return x

_drawn_inputs = setup_inputs


def setup_inputs(seed=0):
    import zlib

    import numpy as np

    out = dict(_drawn_inputs(seed))
    spreads = {'L0_attn_b_out': (0.0, 0.8),
     'L0_ffn_ln_gamma': (1.0, 0.2),
     'L0_ffn_ln_beta': (0.0, 0.1),
     'L1_attn_ln_w': (1.0, 0.6),
     'L1_attn_ln_b': (0.0, 0.8),
     'L1_ffn_ln_gamma': (1.0, 0.2),
     'L1_ffn_ln_beta': (0.0, 0.1)}
    factors = {'L0_attn_w_qkv': 3.358,
     'L0_attn_w_out': 3.276,
     'L0_ffn_fc1_bias': 8.0,
     'L0_ffn_fc2_bias': 8.0,
     'L1_attn_Wq': 8.0,
     'L1_attn_Wk': 8.0,
     'L1_attn_Wv': 8.0,
     'L1_attn_Wo': 8.0,
     'L1_attn_lambda_q1': 8.0,
     'L1_attn_lambda_k1': 8.0,
     'L1_attn_lambda_q2': 8.0,
     'L1_attn_lambda_k2': 8.0,
     'L1_ffn_fc1_scales': 5.689,
     'L1_ffn_fc1_bias': 8.0,
     'L1_ffn_fc2_bias': 8.0}
    for name, (base, spread) in spreads.items():
        noise = np.random.default_rng([zlib.crc32(name.encode()), seed]).standard_normal(out[name].shape)
        drawn = base * np.exp(spread * noise) if base else spread * noise
        out[name] = jnp.asarray(drawn.astype(out[name].dtype))
    for name, factor in factors.items():
        out[name] = (out[name] * factor).astype(out[name].dtype)
    return out
```

```python
import math
from contextlib import ExitStack

import numpy as np
import concourse.bass as bass
from concourse import mybir

F32 = mybir.dt.float32
F32R = mybir.dt.float32r
BF16 = mybir.dt.bfloat16
I32 = mybir.dt.int32
ACT = mybir.ActivationFunctionType
ALU = mybir.AluOpType
AXIS = mybir.AxisListType

NB = 16
T = 512
D = 128
P = 128
NT = T // P
FF = 512
NF = FF // P
H0, DH = 16, 64
NPAIR = H0 // 2
INNER = H0 * DH
H1, DS = 8, 8
NS = 2 * H1
DV = 2 * DS
NG = 4
GS = NS // NG
LN_EPS = 1e-5
RMS_EPS = 1e-8
LAMBDA_INIT = 0.8 - 0.6 * math.exp(-0.3 * 12)
SLOPES = [2.0 ** (-0.5 * (h + 1)) for h in range(H0)]
MASKED = -3.0e38

WIDTH = [T - P * k for k in range(NT)]
OFFS = [sum(WIDTH[:k]) for k in range(NT)]
PT0 = sum(WIDTH)

ROW_KEY = 64
ROW_MAX = 96


def tables():
    half = np.arange(0, DS, 2, dtype=np.float32) / np.float32(DS)
    inv_freq = (np.float32(1.0) / np.power(np.float32(10000.0), half)).astype(np.float32)
    freqs = (np.arange(T, dtype=np.float32)[:, None] * inv_freq[None, :]).astype(np.float32)
    freqs = np.repeat(freqs, 2, axis=-1).astype(np.float64)
    sign = np.where(np.arange(DS) % 2 == 0, -1.0, 1.0)
    cos = np.cos(freqs).T
    sin = np.sin(freqs).T * sign[:, None]
    rope = np.stack([np.tile(cos, (NS, 1)), np.tile(sin, (NS, 1))], 1)
    causal = np.zeros((P, T), np.float32)
    q, k = np.arange(P)[:, None], np.arange(P)[None, :]
    causal[:, T - P:] = np.where(k > q, np.float32(MASKED), np.float32(0))
    qscale = np.zeros((P, NPAIR), np.float32)
    for p in range(NPAIR):
        for j in range(2):
            qscale[DH * j:DH * (j + 1), p] = DH ** -0.5 / SLOPES[2 * p + j]
    return {
        "t_rope": rope.astype(np.float32),
        "t_causal": causal,
        "t_causalT": np.ascontiguousarray(causal[:, T - P:].T),
        "t_qscale": qscale,
        "t_key": np.arange(T, dtype=np.float32)[None, :],
        "t_ident": np.eye(P, dtype=np.float32),
    }


def pj_order():
    order = ["xnT0", "q0", "k0"] + [f"v{n}" for n in range(2 * NT)] + ["hT0"]
    order += [f"ya{f}" for f in range(NF)] + ["fa"]
    for s in range(NPAIR + 2):
        if 1 <= s <= NPAIR:
            order.append(f"m{s - 1}")
        if s + 1 < NPAIR:
            order += [f"q{s + 1}", f"k{s + 1}"]
        if s >= 2 and s % 2 == 1:
            order.append(f"l{(s - 3) // 2}")
    order += ["wo0", "xnT1", "rq", "rqs", "rk", "rks", "vals", "hT1"]
    order += [f"yb{f}" for f in range(NF)] + ["fb"]
    for g in range(NG + 1):
        if g >= 1:
            order.append(f"n{g - 1}")
        if g >= 2:
            order.append(f"o{g - 2}")
    order += [f"o{NG - 1}", "oT", "wo1"]
    return order


N_PSET = 7
N_VSET = 4
N_VPREP = 19
PJ = {name: n for n, name in enumerate(pj_order())}
PJ_USES = len(PJ)
assert PJ_USES % 2 == 0


def build_program(nc, a, out):
    ctx = ExitStack()
    with ctx:
        def sb(name, shape, dt=F32):
            return ctx.enter_context(nc.sbuf_tensor(name, shape, dt))

        def ps(name):
            return ctx.enter_context(nc.psum_tensor(name, [P, T], F32))

        def sem(name):
            return ctx.enter_context(nc.semaphore(name))

        ident = sb("ident", [P, P])
        causal = sb("causal", [P, T])
        rope = sb("rope", [P, 2, T])
        qscale = sb("qscale", [P, NPAIR])
        identb = sb("identb", [P, P], BF16)
        causalb = sb("causalb", [P, P], BF16)
        ones = sb("ones", [P, 32])
        minus_half = sb("minus_half", [P, 16])
        wqkv = sb("wqkv", [P, 3 * INNER])
        wout = sb("wout", [P, NPAIR, D])
        w1 = sb("w1", [P, 2, FF])
        w2 = sb("w2", [P, 2, NF * D])
        b1 = sb("b1", [P, 2, NF])
        b1h = sb("b1h", [P, 2, NF])
        gamma = sb("gamma", [P, 2])
        beta = sb("beta", [P, 2])
        bias = sb("bias", [P, 2, D])
        w_l1 = sb("w_l1", [P, 6, D])
        lam_in = sb("lam_in", [P, 4, DS])
        lam_pr = sb("lam_pr", [P, 2, DS])
        lam_s = sb("lam_s", [P, 2])
        lam_e = sb("lam_e", [P, 2])
        lam_d = sb("lam_d", [P, 1])
        neglam = sb("neglam", [P, 1])
        lnw_in = sb("lnw_in", [P, 2, DV])
        lnw = sb("lnw", [P, 2, DV])

        x_in = sb("x_in", [P, NT, D])
        xacc = sb("xacc", [P, NT, D])
        xb = sb("xb", [P, NT, D])
        stats = sb("stats", [P, 2, NT, 6])
        mv = sb("mv", [P, 2, NT, 2])
        veps = sb("veps", [P, 2, NT])
        rstd = sb("rstd", [P, 2, NT])
        xnT = sb("xnT", [P, T])
        v0 = sb("v0", [P, NT, INNER])
        rawq = sb("rawq", [P, T])
        rawk = sb("rawk", [P, T])
        QA = sb("QA", [P, 3, 2, T], F32R)
        KA = sb("KA", [P, 3, 2, T], F32R)
        QB = sb("QB", [P, 3, 2, T], F32R)
        KB = sb("KB", [P, 3, 2, T], F32R)
        junk = sb("junk", [P, 2, T], BF16)
        mx = sb("mx", [P, 2, 16])
        mrow = sb("mrow", [16, 2, P], F32R)
        pt = sb("pt", [P, 4 * PT0])
        psums = sb("psums", [P, 4, T])
        tanh = psums[:, 0:2, :]
        xn = psums[:, 2, :].rearrange("p (t d) -> p t d", t=NT)
        hn = psums[:, 3, :].rearrange("p (t d) -> p t d", t=NT)
        lsb = sb("lsb", [P, T])
        hT = lsb
        lcol = sb("lcol", [P, 16])
        rcol = sb("rcol", [P, 16])
        rbc = sb("rbc", [P, 2, T])
        big = sb("big", [P, NPAIR * T])
        keyrow = big[ROW_KEY:ROW_KEY + 1, 3 * INNER:3 * INNER + T]
        y = big[:, 0:NF * T].rearrange("p (f t) -> p f t", f=NF)
        att = big[:, :].rearrange("p (h t) -> p h t", h=NPAIR)
        flat = v0[:, :, :].rearrange("p t e -> p (t e)")
        rot = flat[:, 0:T]
        rest = flat[:, T:2 * T]
        parts = flat[:, 2 * T:5 * T].bitcast(BF16).rearrange("p (w c t) -> p w c t", w=2, c=3)
        oraw = flat[:, 5 * T:7 * T].rearrange("p (b t) -> p b t", b=2)
        o1 = flat[:, 7 * T:8 * T].rearrange("p (t d) -> p t d", t=NT)
        QS = sb("QS", [P, NS, T], BF16)
        KS = sb("KS", [P, NS, T], BF16)
        nrow = sb("nrow", [16, 3, P], BF16)
        nrest = sb("nrest", [16, P])
        v1 = sb("v1", [P, NT, H1, 32])
        rinv = sb("rinv", [P, NT, GS, 1])
        onrm = sb("onrm", [P, NT, GS, DV])
        dif = sb("dif", [P, NT, 2, DV])
        sq = sb("sq", [P, NT, 2, DV])
        ms = sb("ms", [P, NT, 2, 1])
        mse = sb("mse", [P, NT, 2, 1])
        rms = sb("rms", [P, NT, 2, 1])
        od = sq
        ow = sb("ow", [P, NT, 2, DV])
        o1T = rest
        yout = sb("yout", [P, NT, D])

        pj = [ps("pj0"), ps("pj1")]
        mxp = [ps("mx0"), ps("mx1")]
        stp = [ps("st0"), ps("st1")]
        op = [ps("op0"), ps("op1")]

        scr_r = nc.dram_tensor("scr_r", (NPAIR // 2, P, 16), F32).ap()
        scr_p = nc.dram_tensor("scr_p", (2, 3, P, T), BF16).ap()

        s_ld = sem("weights_loaded")
        s_pset = sem("pool_constants")
        s_vset = sem("vector_constants")
        s_vprep = sem("vector_prepared")
        s_aprep = sem("act_prepared")
        s_x = sem("x_loaded")
        s_lnv = sem("ln_vector_steps")
        s_lnp = sem("ln_pool_steps")
        s_pjf = [sem("pj0_full"), sem("pj1_full")]
        s_pje = [sem("pj0_free"), sem("pj1_free")]
        s_tanh = sem("tanh_done")
        s_tanh1 = sem("tanh_plus_one")
        s_res = sem("residual_steps")
        s_spa = sem("act_split")
        s_spv = sem("vector_split")
        s_mxf = sem("max_scores_ready")
        s_mxd = sem("row_max_done")
        s_mhi = sem("minus_max_high")
        s_mdma = [sem("max_rows_stored0"), sem("max_rows_stored1")]
        s_st = sem("key_scores_ready")
        s_exp = sem("exp_done")
        s_psum = sem("probs_added")
        s_pv = sem("pv_done")
        s_pv1 = sem("pv1_tile_done")
        s_att = sem("attention_copied")
        s_ldma = sem("sums_spread")
        s_rc = sem("sums_inverted")
        s_rst = sem("inverse_stored")
        s_rb = sem("inverse_broadcast")
        s_nrm = sem("attention_normalised")
        s_rot = sem("rope_steps")
        s_part = sem("parts_ready")
        s_pst = sem("parts_stored")
        s_stk = sem("stacks_filled")
        s_nth = sem("minus_max1_high")
        s_nt = sem("minus_max1_rest")
        s_nd = [sem("max1_rows_stored0"), sem("max1_rows_stored1")]
        s_or = sem("heads_copied")
        s_tl = sem("head_norm_steps")
        s_tlp = sem("head_norm_pool_steps")
        s_out = sem("result_stored")

        def pjn(name):
            return PJ[name] % 2, PJ[name] // 2 + 1

        PB = PJ_USES // 2
        LNV = 2 * 24
        HP = NPAIR // 2
        MXN = 8 * NPAIR + NS * NT
        L0N = 8 * NPAIR
        NSTK = 16 * 12
        stage = {}
        for n in range(4):
            stage[n] = (v0[:, n, 0:FF], v0[:, n, FF:2 * FF])
        b2_in = big[:, 4 * FF:4 * FF + 2 * D].rearrange("p (l d) -> p l d", l=2)
        bo_in = big[:, 4 * FF + 2 * D:4 * FF + 3 * D]

        causal_in = big[:, 3 * INNER + T:3 * INNER + T + P]
        loads = [
            (causal_in, a["t_causalT"]), (ident[:, :], a["t_ident"]), (causal[:, :], a["t_causal"]), (rope[:, :, :], a["t_rope"]),
            (qscale[:, :], a["t_qscale"]), (keyrow, a["t_key"]),
            (wqkv[:, :], a["L0_attn_w_qkv"]),
            (wout[:, :, :], a["L0_attn_w_out"].rearrange("(h p) d -> p h d", p=P)),
            (bo_in, a["L0_attn_b_out"].partition_broadcast(P)),
            (w_l1[:, 0, :], a["t_WqT"]), (w_l1[:, 1, :], a["t_WqsT"]), (w_l1[:, 2, :], a["t_WkT"]),
            (w_l1[:, 3, :], a["t_WksT"]), (w_l1[:, 4, :], a["t_WvT"]), (w_l1[:, 5, :], a["t_WoT"]),
            (lnw_in[:, 0, :], a["L1_attn_ln_w"].partition_broadcast(P)),
            (lnw_in[:, 1, :], a["L1_attn_ln_b"].partition_broadcast(P)),
        ]
        for n, v in enumerate(("q1", "k1", "q2", "k2")):
            loads.append((lam_in[:, n, :], a[f"L1_attn_lambda_{v}"].partition_broadcast(P)))
        for l in range(2):
            f = f"L{l}_ffn_"
            loads += [
                (b1[:, l, :], a[f + "fc1_bias"].rearrange("(f p) -> p f", p=P)),
                (gamma[:, l:l + 1], a[f + "ln_gamma"].rearrange("(p o) -> p o", o=1)),
                (beta[:, l:l + 1], a[f + "ln_beta"].rearrange("(p o) -> p o", o=1)),
                (b2_in[:, l, :], a[f + "fc2_bias"].partition_broadcast(P)),
                (stage[2 * l][0].bitcast(I32), a[f + "fc1_q"]),
                (stage[2 * l][1], a[f + "fc1_scales"].rearrange("g n -> (g n)").partition_broadcast(P)),
                (stage[2 * l + 1][0].rearrange("p (f d) -> p f d", f=NF).bitcast(I32),
                 a[f + "fc2_q"].rearrange("(f p) d -> p f d", p=P)),
                (stage[2 * l + 1][1], a[f + "fc2_scales"].rearrange("g n -> (g n)").partition_broadcast(P)),
            ]
        NLOAD = 16 * len(loads)

        block = ctx.enter_context(nc.Block())

        @block.sync
        def _(sp):
            x_v = a["L0_attn_x"].rearrange("b (t p) d -> b p t d", p=P)
            out_v = out.rearrange("b (t p) d -> b p t d", p=P)
            with nc.allow_non_contiguous_dma(reason="a few hundred biases and gains, once"):
                for dst, src in loads:
                    sp.dma_start(dst, src).then_inc(s_ld, 16)
            sp.dma_start(x_in[:, :, :], x_v[0]).then_inc(s_x, 16)

            def inverse(i, g):
                sp.wait_ge(s_rc, i * HP + g + 1)
                sp.dma_start(scr_r[g], rcol[:, :]).then_inc(s_rst, 16)
                inverse_stored = sp.to_reg(i * (16 * HP) + 16 * (g + 1))
                rbc_used = sp.to_reg(i * NPAIR + 2 * g) if g else 0
                sp.wait_ge(s_ld, NLOAD)
                sp.wait_ge(s_rst, inverse_stored)
                v = scr_r[g].rearrange("(p j c) e -> j p (c e)", p=2, j=2)
                if g:
                    sp.wait_ge(s_nrm, rbc_used)
                for j in range(2):
                    sp.dma_start(rbc[DH * j:DH * (j + 1), :, :], v[j:j + 1].broadcast_to([DH, 2, T])).then_inc(s_rb, 16)

            with sp.Fori(0, NB) as i:
                for s in range(NPAIR + 2):
                    if 1 <= s <= NPAIR:
                        p = s - 1
                        b, u = pjn(f"m{p}")
                        sp.wait_ge(s_pje[b], i * PB + u)
                        for r in range(2):
                            row = QB[ROW_MAX + r:ROW_MAX + r + 1, p % 3, :, :]
                            sp.dma_start(row.bitcast(F32).rearrange("o j (c f) -> o (j c) f", f=P),
                                         mrow[0:8, r, :].bitcast(F32)).then_inc(s_mdma[p % 2], 16)
                    if s >= 4 and s % 2 == 0:
                        inverse(i, (s - 4) // 2)
                    if s >= 3 and s % 2 == 1:
                        b, u = pjn(f"l{(s - 3) // 2}")
                        sp.wait_ge(s_pje[b], i * PB + u)
                        sp.dma_start(lcol[:, :], lsb[0:P:32, :].rearrange("h (c e) -> h c e", e=16)).then_inc(s_ldma, 16)
                inverse(i, HP - 1)
                next_i = sp.snap((i + 1) % NB)
                xn_there = sp.to_reg(i * LNV + 12)
                residual_read = sp.to_reg(i * 4 + 1)
                sp.wait_ge(s_ld, NLOAD)
                sp.wait_ge(s_lnv, xn_there)
                sp.wait_ge(s_res, residual_read)
                sp.dma_start(x_in[:, :, :], x_v[bass.ds(next_i, 1)].rearrange("b p t d -> p (b t) d")).then_inc(s_x, 16)
                sp.wait_ge(s_part, i * 6 + 6)
                for w in range(2):
                    sp.dma_start(scr_p[w].rearrange("c p t -> p c t"), parts[:, w, :, :]).then_inc(s_pst, 16)
                sp.wait_ge(s_pst, i * 32 + 32)
                for w, (dst, order) in enumerate(((QS, (0, 0, 1, 1, 0, 2)), (KS, (0, 1, 0, 1, 2, 0)))):
                    for slot, c in enumerate(order):
                        sp.dma_start(dst[DS * slot:DS * (slot + 1), :, :],
                                     scr_p[w, c].rearrange("(s d) t -> d s t", d=DS)).then_inc(s_stk, 16)
                for g in range(NG):
                    sp.wait_ge(s_nt, i * 2 * NG + 2 * g + 2)
                    for r in range(3):
                        row = QS[ROW_MAX + r:ROW_MAX + r + 1, GS * g:GS * (g + 1), :]
                        sp.dma_start(row.rearrange("o s (c f) -> o (s c) f", f=P), nrow[:, r, :]).then_inc(s_nd[g % 2], 16)
                b, u = pjn("wo1")
                sp.wait_ge(s_pje[b], i * PB + u)
                sp.dma_start(out_v[bass.ds(i, 1)].rearrange("b p t d -> p (b t) d"), yout[:, :, :]).then_inc(s_out, 16)
                stored = sp.to_reg(i * 16 + 16)
                sp.wait_ge(s_ld, NLOAD)
                sp.wait_ge(s_out, stored)
            sp.wait_ge(s_x, 16 * NB + 16)

        @block.gpsimd
        def _(pool):
            pool.memset(ones[:, :], 1.0).then_inc(s_pset, 1)
            pool.memset(minus_half[:, :], -0.5).then_inc(s_pset, 1)
            pool.memset(v1[:, :, :, :], 0.0).then_inc(s_pset, 1)
            pool.memset(QS[:, :, :], 0.0).then_inc(s_pset, 1)
            pool.memset(KS[:, :, :], 0.0).then_inc(s_pset, 1)
            pool.wait_ge(s_pset, 5)
            pool.memset(v1[:, :, :, DV:DV + 1], 1.0).then_inc(s_pset, 1)
            pool.wait_ge(s_pset, 6)
            pool.memset(KS[ROW_MAX:ROW_MAX + 3, :, :], 1.0).then_inc(s_pset, 1)
            pool.wait_ge(s_pset, N_PSET)
            pool.wait_ge(s_vprep, N_VPREP)

            def ln_scale(i, l, part):
                k = 2 * (2 * l + part)
                mv_there = pool.to_reg(i * LNV + 24 * l + (8 if part == 0 else 20))
                pool.wait_ge(s_pset, N_PSET)
                pool.wait_ge(s_lnv, mv_there)
                pool.tensor_scalar(veps[:, part, :], mv[:, part, :, 1], 1.0, LN_EPS, ALU.mult, ALU.add).then_inc(s_lnp, 1)
                pool.wait_ge(s_lnp, i * 8 + k + 1)
                pool.tensor_tensor(rstd[:, part, :], veps[:, part, :], minus_half[:, 0:NT], ALU.pow).then_inc(s_lnp, 1)

            def residual(i, l, src):
                pool.wait_ge(s_lnv, i * LNV + 24 * l + 12)
                pool.tensor_tensor(xb[:, :, :], src[:, :, :], xn[:, :, :], ALU.add).then_inc(s_res, 1)
                pool.wait_ge(s_res, i * 4 + 2 * l + 1)
                pool.tensor_tensor(xb[:, :, :], xb[:, :, :], bias[:, l:l + 1, :].broadcast_to([P, NT, D]), ALU.add).then_inc(s_res, 1)

            def tanh_plus_one(i, l):
                for f in range(NF):
                    tanh_there = pool.to_reg(i * 2 * NF + l * NF + f + 1)
                    pool.wait_ge(s_pset, N_PSET)
                    pool.wait_ge(s_tanh, tanh_there)
                    pool.tensor_scalar(tanh[:, f % 2, :], tanh[:, f % 2, :], 1.0, 1.0, ALU.mult, ALU.add).then_inc(s_tanh1, 1)

            def normalise(i, p):
                pool.wait_ge(s_rb, i * (32 * HP) + 32 * (p // 2 + 1))
                pool.wait_ge(s_att, i * NPAIR + p + 1)
                pool.tensor_tensor(att[:, p, :], att[:, p, :], rbc[:, p % 2, :], ALU.mult).then_inc(s_nrm, 1)

            with pool.Fori(0, NB) as i:
                ln_scale(i, 0, 0)
                ln_scale(i, 0, 1)
                residual(i, 0, x_in)
                tanh_plus_one(i, 0)
                for s in range(1, NPAIR + 2):
                    if s <= NPAIR:
                        p = s - 1
                        if p >= 2 and p % 2 == 0:
                            b, u = pjn(f"l{p // 2 - 1}")
                            pool.wait_ge(s_pjf[b], i * PB + u)
                        for j in range(2):
                            base = (2 * (p % 2) + j) * PT0
                            c = (2 * p + j) % 4
                            for k in range(NT):
                                n = 8 * p + 4 * j + k
                                tile = pt[:, base + OFFS[k]:base + OFFS[k] + WIDTH[k]]
                                tile_there = pool.to_reg(i * MXN + n + 1)
                                if k == 0:
                                    pool.wait_ge(s_pset, N_PSET)
                                pool.wait_ge(s_exp, tile_there)
                                if k == 0:
                                    pool.tensor_copy(psums[:, c, 0:P], tile[:, 0:P]).then_inc(s_psum, 1)
                                    continue
                                so_far = pt[:, base + P:base + T] if k == 1 else psums[:, c, P * k:T]
                                pool.wait_ge(s_psum, i * L0N + n)
                                pool.tensor_tensor(psums[:, c, P * k:T], so_far, tile, ALU.add).then_inc(s_psum, 1)
                    if s >= 5 and s % 2 == 1:
                        normalise(i, s - 5)
                        normalise(i, s - 4)
                normalise(i, NPAIR - 2)
                normalise(i, NPAIR - 1)
                ln_scale(i, 1, 0)
                ln_scale(i, 1, 1)
                residual(i, 1, xacc)
                tanh_plus_one(i, 1)
                for g in range(NG):
                    ms_there = pool.to_reg(i * 7 * NG + 7 * g + 4)
                    pool.wait_ge(s_pset, N_PSET)
                    pool.wait_ge(s_tl, ms_there)
                    pool.tensor_scalar(mse[:, :, :, :], ms[:, :, :, :], 1.0 / DV, RMS_EPS, ALU.mult, ALU.add).then_inc(s_tlp, 1)
                    pool.wait_ge(s_tlp, i * 2 * NG + 2 * g + 1)
                    pool.tensor_tensor(rms[:, :, :, 0].rearrange("p t h -> p (t h)"), mse[:, :, :, 0].rearrange("p t h -> p (t h)"),
                                       minus_half[:, 0:2 * NT], ALU.pow).then_inc(s_tlp, 1)

        @block.scalar
        def _(act):
            act.wait_ge(s_ld, NLOAD)
            act.wait_ge(s_vset, N_VSET)
            for n in range(6):
                act.activation(KB[ROW_KEY:ROW_KEY + 1, n // 2, n % 2, :], keyrow, ACT.Copy).then_inc(s_aprep, 1)
            act.activation(b1h[:, :, :], b1[:, :, :], ACT.Copy, scale=0.5).then_inc(s_aprep, 1)
            act.wait_ge(s_vprep, 2)
            act.activation(lam_e[:, :], lam_s[:, :], ACT.Exp).then_inc(s_aprep, 1)
            act.wait_ge(s_aprep, 8)
            act.wait_ge(s_pset, N_PSET)

            def transposed(i, l, name):
                b, u = pjn(name)
                act.wait_ge(s_pjf[b], i * PB + u)
                if name[0] == "h":
                    act.activation(hT[:, :], pj[b][:, :], ACT.Identity, scale=gamma[:, l:l + 1],
                                   bias=beta[:, l:l + 1]).then_inc(s_pje[b], 1)
                else:
                    act.activation(xnT[:, :], pj[b][:, :], ACT.Copy).then_inc(s_pje[b], 1)

            def ffn_tanh(i, l):
                for f in range(NF):
                    b, u = pjn(f"y{'ab'[l]}{f}")
                    act.wait_ge(s_pjf[b], i * PB + u)
                    if f >= 2:
                        b2, u2 = pjn(f"y{'ab'[l]}{f - 2}")
                        act.wait_ge(s_pje[b2], i * PB + u2)
                    act.activation(tanh[:, f % 2, :], pj[b][:, :], ACT.Tanh, scale=0.5,
                                   bias=b1h[:, l, f:f + 1]).then_inc(s_tanh, 1)

            def split(i, p):
                b = p % 3
                bq, uq = pjn(f"q{p}")
                bk, uk = pjn(f"k{p}")
                if p:
                    act.wait_ge(s_spv, i * L0N + 8 * p)
                    act.wait_ge(s_spa, i * (4 * NPAIR) + 4 * p)
                act.wait_ge(s_pjf[bq], i * PB + uq)
                act.activation(rawq[:, :], pj[bq][:, :], ACT.Copy, scale=qscale[:, p:p + 1]).then_inc(s_pje[bq], 1)
                act.wait_ge(s_pjf[bk], i * PB + uk)
                act.activation(rawk[:, :], pj[bk][:, :], ACT.Copy).then_inc(s_pje[bk], 1)
                if p >= 3:
                    act.wait_ge(s_st, i * MXN + 8 * (p - 2))
                act.wait_ge(s_pje[bq], i * PB + uq)
                for j in range(2):
                    act.activation(QB[0:DH, b, j, :], rawq[DH * j:DH * (j + 1), :], ACT.Copy).then_inc(s_spa, 1)
                act.wait_ge(s_pje[bk], i * PB + uk)
                for j in range(2):
                    act.activation(KA[DH * (1 - j):DH * (2 - j), b, j, :], rawk[DH * j:DH * (j + 1), :],
                                   ACT.Copy).then_inc(s_spa, 1)

            def copy_heads(i, g):
                act.wait_ge(s_pv1, i * NG * NT + NT * (g + 1))
                act.activation(oraw[:, g % 2, :], op[g % 2][:, :], ACT.Copy).then_inc(s_or, 1)

            with act.Fori(0, NB) as i:
                transposed(i, 0, "xnT0")
                split(i, 0)
                for n in range(2 * NT):
                    b, u = pjn(f"v{n}")
                    act.wait_ge(s_pjf[b], i * PB + u)
                    act.activation(v0[:, n // 2, T * (n % 2):T * (n % 2 + 1)], pj[b][:, :], ACT.Copy).then_inc(s_pje[b], 1)
                transposed(i, 0, "hT0")
                ffn_tanh(i, 0)
                for s in range(NPAIR + 2):
                    if 1 <= s <= NPAIR:
                        p = s - 1
                        b, u = pjn(f"m{p}")
                        act.wait_ge(s_pjf[b], i * PB + u)
                        if p:
                            act.wait_ge(s_mdma[(p - 1) % 2], i * (16 * NPAIR) + 32 * ((p - 1) // 2 + 1))
                        act.activation(mrow[0:8, 0, :], pj[b][0:8, 0:P], ACT.Copy, scale=-1.0).then_inc(s_mhi, 1)
                    if s + 1 < NPAIR:
                        split(i, s + 1)
                    if s >= 2:
                        act.wait_ge(s_pv, i * NPAIR + s - 1)
                        act.activation(att[:, s - 2, :], op[s % 2][:, :], ACT.Copy).then_inc(s_att, 1)
                    if 1 <= s <= NPAIR:
                        p = s - 1
                        for j in range(2):
                            base = (2 * (p % 2) + j) * PT0
                            if p >= 2:
                                act.wait_ge(s_pv, i * NPAIR + p - 1)
                                act.wait_ge(s_psum, i * L0N + 8 * (p - 2) + 4 * (j + 1))
                            for k in range(NT):
                                n = 8 * p + 4 * j + k
                                act.wait_ge(s_st, i * MXN + n + 1)
                                c0 = P if k == NT - 1 else 0
                                act.activation(pt[:, base + OFFS[k]:base + OFFS[k] + WIDTH[k]],
                                               stp[n % 2][:, c0:c0 + WIDTH[k]], ACT.Exp,
                                               scale=SLOPES[2 * p + j]).then_inc(s_exp, 1)
                    if s >= 3 and s % 2 == 1:
                        g = (s - 3) // 2
                        b, u = pjn(f"l{g}")
                        act.wait_ge(s_pjf[b], i * PB + u)
                        if g:
                            act.wait_ge(s_ldma, i * (16 * HP) + 16 * g)
                        act.activation(lsb[:, :], pj[b][:, :], ACT.Copy).then_inc(s_pje[b], 1)
                transposed(i, 1, "xnT1")
                b, u = pjn("vals")
                act.wait_ge(s_pjf[b], i * PB + u)
                act.activation(v1[:, :, :, 0:DV], pj[b][:, :].rearrange("p (t h e) -> p t h e", t=NT, h=H1),
                               ACT.Copy).then_inc(s_pje[b], 1)
                transposed(i, 1, "hT1")
                ffn_tanh(i, 1)
                for g in range(NG):
                    b, u = pjn(f"n{g}")
                    act.wait_ge(s_pjf[b], i * PB + u)
                    if g:
                        act.wait_ge(s_nd[(g - 1) % 2], i * 96 + 48 * ((g - 1) // 2 + 1))
                    act.activation(nrow[:, 0, :], pj[b][0:16, 0:P], ACT.Copy, scale=-1.0).then_inc(s_nth, 1)
                    if g:
                        copy_heads(i, g - 1)
                    for k in range(NT):
                        m = NT * g + k
                        if m >= 2:
                            act.wait_ge(s_pv1, i * NG * NT + m - 1)
                        for j in range(GS):
                            n = GS * m + j
                            act.wait_ge(s_st, i * MXN + L0N + n + 1)
                            act.activation(pt[:, (GS * (k % 2) + j) * T:(GS * (k % 2) + j + 1) * T], stp[n % 2][:, :],
                                           ACT.Exp, scale=float(DS) ** -0.25).then_inc(s_exp, 1)
                copy_heads(i, NG - 1)
                b, u = pjn("oT")
                act.wait_ge(s_pjf[b], i * PB + u)
                act.activation(o1T[:, :], pj[b][:, :], ACT.Copy).then_inc(s_pje[b], 1)

        @block.vector
        def _(dve):
            for t in (QB, KB):
                dve.memset(t[DH:P, :, :, :].bitcast(F32), 0.0).then_inc(s_vset, 1)
            dve.wait_ge(s_vset, 2)
            dve.memset(QB[ROW_KEY:ROW_KEY + 1, :, :, :].bitcast(F32), 1.0).then_inc(s_vset, 1)
            dve.memset(KB[ROW_MAX:ROW_MAX + 2, :, :, :].bitcast(F32), 1.0).then_inc(s_vset, 1)
            assert N_VSET == 4
            dve.wait_ge(s_ld, NLOAD)
            dve.tensor_tensor(lam_pr[:, :, :], lam_in[:, 0:4:2, :], lam_in[:, 1:4:2, :], ALU.mult).then_inc(s_vprep, 1)
            dve.wait_ge(s_vprep, 1)
            dve.reduce_sum(lam_s[:, :], lam_pr[:, :, :], AXIS.X).then_inc(s_vprep, 1)
            dve.wait_ge(s_aprep, 8)
            dve.tensor_tensor(lam_d[:, :], lam_e[:, 1:2], lam_e[:, 0:1], ALU.subtract).then_inc(s_vprep, 1)
            dve.wait_ge(s_vprep, 3)
            dve.tensor_scalar(neglam[:, :], lam_d[:, :], -LAMBDA_INIT, None, ALU.add).then_inc(s_vprep, 1)
            dve.tensor_scalar(lnw[:, :, :], lnw_in[:, :, :], 1.0 - LAMBDA_INIT, None, ALU.mult).then_inc(s_vprep, 1)
            n_prep = 5
            for n in range(4):
                l, second = divmod(n, 2)
                asf = big[:, FF * n:FF * (n + 1)]
                dst = (w2 if second else w1)[:, l, :]
                dve.tensor_copy(asf, stage[n][0].bitcast(I32)).then_inc(s_vprep, 1)
                dve.wait_ge(s_vprep, n_prep + 1)
                dve.scalar_tensor_tensor(out=dst, in0=asf, scalar=-128.0, in1=stage[n][1],
                                         op0=ALU.add, op1=ALU.mult).then_inc(s_vprep, 1)
                n_prep += 2
                if second:
                    dve.wait_ge(s_vprep, n_prep)
                    dve.tensor_scalar(dst, dst, 0.25, None, ALU.mult).then_inc(s_vprep, 1)
                    n_prep += 1
            dve.tensor_copy(identb[:, :], ident[:, :]).then_inc(s_vprep, 1)
            dve.tensor_copy(causalb[:, :], causal_in).then_inc(s_vprep, 1)
            n_prep += 2
            dve.tensor_scalar(bias[:, :, :], b2_in, 0.5, None, ALU.mult).then_inc(s_vprep, 1)
            n_prep += 1
            dve.wait_ge(s_vprep, n_prep)
            dve.tensor_tensor(bias[:, 0, :], bias[:, 0, :], bo_in, ALU.add).then_inc(s_vprep, 1)
            n_prep += 1
            assert n_prep == N_VPREP
            dve.wait_ge(s_vprep, n_prep)

            def layer_norm(i, l, src):
                n = i * LNV + 24 * l
                for part, (inp, dst) in enumerate(((src, xn), (xn, hn))):
                    for t in range(NT):
                        dve.bn_stats(stats[:, part, t, :], inp[:, t, :]).then_inc(s_lnv, 1)
                    bn_stats_done = dve.to_reg(n + 12 * part + 4)
                    dve.wait_ge(s_vset, N_VSET)
                    dve.wait_ge(s_lnv, bn_stats_done)
                    for t in range(NT):
                        dve.bn_aggr(mv[:, part, t, :], stats[:, part, t, :]).then_inc(s_lnv, 1)
                    dve.wait_ge(s_lnv, n + 12 * part + 8)
                    dve.wait_ge(s_lnp, i * 8 + 4 * l + 2 * part + 2)
                    for t in range(NT):
                        dve.tensor_scalar(dst[:, t, :], inp[:, t, :], mv[:, part, t, 0:1], rstd[:, part, t:t + 1],
                                          ALU.subtract, ALU.mult).then_inc(s_lnv, 1)
                    dve.wait_ge(s_lnv, n + 12 * part + 12)

            def ffn(i, l):
                for f in range(NF):
                    b, u = pjn(f"y{'ab'[l]}{f}")
                    dve.wait_ge(s_tanh1, i * 2 * NF + l * NF + f + 1)
                    dve.scalar_tensor_tensor(out=y[:, f, :], in0=pj[b][:, :], scalar=b1[:, l, f:f + 1],
                                             in1=tanh[:, f % 2, :], op0=ALU.add, op1=ALU.mult).then_inc(s_pje[b], 1)
                b, u = pjn("f" + "ab"[l])
                dve.wait_ge(s_pjf[b], i * PB + u)
                dve.wait_ge(s_res, i * 4 + 2 * l + 2)
                dve.tensor_tensor(xacc[:, :, :], pj[b][:, :].rearrange("p (t d) -> p t d", t=NT), xb[:, :, :],
                                  ALU.add).then_inc(s_pje[b], 1)

            def split_high(i, p):
                b = p % 3
                bq, uq = pjn(f"q{p}")
                bk, uk = pjn(f"k{p}")
                if p >= 3:
                    dve.wait_ge(s_st, i * MXN + 8 * (p - 2))
                for t, raw, bb, uu in ((QA, rawq, bq, uq), (KA, rawk, bk, uk)):
                    dve.wait_ge(s_pje[bb], i * PB + uu)
                    for j in range(2):
                        r = slice(DH * j, DH * (j + 1))
                        dve.tensor_copy(t[r, b, j, :], raw[r, :]).then_inc(s_spv, 1)

            def split_low(i, p, n):
                b = p % 3
                which, j = divmod(n, 2)
                r = slice(DH * j, DH * (j + 1))
                o = slice(DH * (1 - j), DH * (2 - j))
                dve.wait_ge(s_spv, i * L0N + 8 * p + n + 1)
                if which == 0:
                    dve.tensor_tensor(QA[o, b, j, :], rawq[r, :], QA[r, b, j, :].bitcast(F32), ALU.subtract).then_inc(s_spv, 1)
                else:
                    dve.tensor_tensor(KB[0:DH, b, j, :], rawk[r, :], KA[r, b, j, :].bitcast(F32), ALU.subtract).then_inc(s_spv, 1)

            def inverse_sums(i, g):
                dve.wait_ge(s_ldma, i * (16 * HP) + 16 * (g + 1))
                if g:
                    dve.wait_ge(s_rst, i * (16 * HP) + 16 * g)
                dve.reciprocal(rcol[:, :], lcol[:, :]).then_inc(s_rc, 1)

            def head_norm_a(i, g):
                b, u = pjn(f"o{g}")
                n = i * 7 * NG + 7 * g
                v = pj[b][:, :].rearrange("p (t j e) -> p t j e", t=NT, j=GS)
                dve.wait_ge(s_pjf[b], i * PB + u)
                dve.reciprocal(rinv[:, :, :, :], v[:, :, :, DV:DV + 1]).then_inc(s_tl, 1)
                dve.wait_ge(s_tl, n + 1)
                dve.tensor_tensor(onrm[:, :, :, :], v[:, :, :, 0:DV], rinv[:, :, :, :].broadcast_to([P, NT, GS, DV]),
                                  ALU.mult).then_inc(s_pje[b], 1)
                dve.wait_ge(s_pje[b], i * PB + u)
                dve.scalar_tensor_tensor(out=dif[:, :, :, :], in0=onrm[:, :, 1:GS:2, :], scalar=neglam[:, 0:1],
                                         in1=onrm[:, :, 0:GS:2, :], op0=ALU.mult, op1=ALU.add).then_inc(s_tl, 1)
                dve.wait_ge(s_tl, n + 2)
                dve.tensor_tensor(sq[:, :, :, :], dif[:, :, :, :], dif[:, :, :, :], ALU.mult).then_inc(s_tl, 1)
                dve.wait_ge(s_tl, n + 3)
                dve.reduce_sum(ms[:, :, :, 0], sq[:, :, :, :], AXIS.X).then_inc(s_tl, 1)

            def head_norm_b(i, g):
                n = i * 7 * NG + 7 * g
                dve.wait_ge(s_tlp, i * 2 * NG + 2 * g + 2)
                dve.tensor_tensor(od[:, :, :, :], dif[:, :, :, :], rms[:, :, :, :].broadcast_to([P, NT, 2, DV]),
                                  ALU.mult).then_inc(s_tl, 1)
                wide = lnw[:, :, :].rearrange("p (w a b) e -> p w a b e", a=1, b=1)
                dve.wait_ge(s_tl, n + 5)
                dve.tensor_tensor(ow[:, :, :, :], od[:, :, :, :], wide[:, 0].broadcast_to([P, NT, 2, DV]),
                                  ALU.mult).then_inc(s_tl, 1)
                dve.wait_ge(s_tl, n + 6)
                dve.tensor_tensor(o1[:, :, 2 * DV * g:2 * DV * (g + 1)].rearrange("p t (h e) -> p t h e", e=DV),
                                  ow[:, :, :, :], wide[:, 1].broadcast_to([P, NT, 2, DV]), ALU.add).then_inc(s_tl, 1)

            with dve.Fori(0, NB) as i:
                dve.wait_ge(s_x, i * 16 + 16)
                layer_norm(i, 0, x_in)
                split_high(i, 0)
                for n in range(4):
                    split_low(i, 0, n)
                ffn(i, 0)
                for s in range(NPAIR + 2):
                    if 1 <= s <= NPAIR:
                        p = s - 1
                        b, u = pjn(f"m{p}")
                        dve.wait_ge(s_mhi, i * NPAIR + p + 1)
                        dve.scalar_tensor_tensor(out=mrow[0:8, 1, :], in0=pj[b][0:8, 0:P], scalar=-1.0,
                                                 in1=mrow[0:8, 0, :].bitcast(F32), op0=ALU.mult,
                                                 op1=ALU.subtract).then_inc(s_pje[b], 1)
                    if s >= 4 and s % 2 == 0:
                        inverse_sums(i, (s - 4) // 2)
                    if s + 1 < NPAIR:
                        split_high(i, s + 1)
                    if s < NPAIR:
                        for n in range(8):
                            j, q = divmod(n, NT)
                            m = 8 * s + n
                            width = P * (q + 1)
                            scores_there = dve.to_reg(i * MXN + m + 1)
                            junk_free = dve.to_reg(i * MXN + m - 1) if m >= 2 else 0
                            dve.wait_ge(s_vset, N_VSET)
                            dve.wait_ge(s_mxf, scores_there)
                            if m >= 2:
                                dve.wait_ge(s_mxd, junk_free)
                            dve.tensor_tensor_reduce(out=junk[:, m % 2, 0:width], in0=mxp[m % 2][:, 0:width],
                                                     in1=causal[:, T - width:T], scale=1.0, scalar=MASKED,
                                                     op0=ALU.add, op1=ALU.max,
                                                     accum_out=mx[:, s % 2, n:n + 1]).then_inc(s_mxd, 1)
                            if s + 1 < NPAIR and n < 4:
                                split_low(i, s + 1, n)
                inverse_sums(i, HP - 1)
                b, u = pjn("wo0")
                bf, uf = pjn("fa")
                dve.wait_ge(s_pjf[b], i * PB + u)
                dve.wait_ge(s_pje[bf], i * PB + uf)
                dve.tensor_tensor(xacc[:, :, :], pj[b][:, :].rearrange("p (t d) -> p t d", t=NT), xacc[:, :, :],
                                  ALU.add).then_inc(s_pje[b], 1)
                dve.wait_ge(s_pje[b], i * PB + u)
                layer_norm(i, 1, xacc)
                for w in range(2):
                    n_rot, n_part = i * 4 + 2 * w, i * 6 + 3 * w
                    for tmp, c, name in ((rawq, 0, "rq" if w == 0 else "rk"), (rawk, 1, "rqs" if w == 0 else "rks")):
                        b, u = pjn(name)
                        dve.wait_ge(s_pjf[b], i * PB + u)
                        dve.tensor_tensor(tmp[:, :], pj[b][:, :], rope[:, c, :], ALU.mult).then_inc(s_pje[b], 1)
                    for name in (("rq", "rqs"), ("rk", "rks"))[w]:
                        b, u = pjn(name)
                        dve.wait_ge(s_pje[b], i * PB + u)
                    dve.tensor_tensor(rot[:, :], rawq[:, :], rawk[:, :], ALU.add).then_inc(s_rot, 1)
                    dve.wait_ge(s_rot, n_rot + 1)
                    dve.tensor_copy(parts[:, w, 0, :], rot[:, :]).then_inc(s_part, 1)
                    dve.wait_ge(s_part, n_part + 1)
                    dve.tensor_tensor(rest[:, :], rot[:, :], parts[:, w, 0, :], ALU.subtract).then_inc(s_rot, 1)
                    dve.wait_ge(s_rot, n_rot + 2)
                    dve.tensor_copy(parts[:, w, 1, :], rest[:, :]).then_inc(s_part, 1)
                    dve.wait_ge(s_part, n_part + 2)
                    dve.tensor_tensor(parts[:, w, 2, :], rest[:, :], parts[:, w, 1, :], ALU.subtract).then_inc(s_part, 1)
                ffn(i, 1)
                for g in range(NG + 1):
                    if g >= 1:
                        b, u = pjn(f"n{g - 1}")
                        n = i * 2 * NG + 2 * (g - 1)
                        dve.wait_ge(s_nth, i * NG + g)
                        dve.scalar_tensor_tensor(out=nrest[:, :], in0=pj[b][0:16, 0:P], scalar=-1.0, in1=nrow[:, 0, :],
                                                 op0=ALU.mult, op1=ALU.subtract).then_inc(s_pje[b], 1)
                        dve.wait_ge(s_pje[b], i * PB + u)
                        dve.tensor_copy(nrow[:, 1, :], nrest[:, :]).then_inc(s_nt, 1)
                        dve.wait_ge(s_nt, n + 1)
                        dve.tensor_tensor(nrow[:, 2, :], nrest[:, :], nrow[:, 1, :], ALU.subtract).then_inc(s_nt, 1)
                    for n in range(GS * NT):
                        if g < NG:
                            m = L0N + GS * NT * g + n
                            dve.wait_ge(s_mxf, i * MXN + m + 1)
                            dve.reduce_max(mx[:, g % 2, n:n + 1], mxp[m % 2][:, :], AXIS.X).then_inc(s_mxd, 1)
                        if g >= 2 and n == 1:
                            head_norm_a(i, g - 2)
                        if g >= 2 and n == 8:
                            head_norm_b(i, g - 2)
                head_norm_a(i, NG - 1)
                head_norm_b(i, NG - 1)
                b, u = pjn("wo1")
                dve.wait_ge(s_pjf[b], i * PB + u)
                dve.tensor_tensor(yout[:, :, :], pj[b][:, :].rearrange("p (t d) -> p t d", t=NT), xacc[:, :, :],
                                  ALU.add).then_inc(s_pje[b], 1)

        @block.tensor
        def _(pe):
            pe.wait_ge(s_ld, NLOAD)
            pe.wait_ge(s_pset, N_PSET)
            pe.wait_ge(s_vprep, N_VPREP)
            pe.wait_ge(s_aprep, 8)
            used = []

            def bank(i, name):
                n = PJ[name]
                used.append(name)
                assert n == len(used) - 1, (name, n, len(used) - 1)
                if n >= 2:
                    pe.wait_ge(s_pje[n % 2], i * PB + n // 2)
                return pj[n % 2], s_pjf[n % 2]

            def transpose4(i, name, src):
                t, full = bank(i, name)
                for k in range(NT):
                    last = pe.transpose(t[:, P * k:P * (k + 1)], src(k), ident[:, :])
                last.then_inc(full, 1)

            def project(i, name, w, x, pieces):
                t, full = bank(i, name)
                for k in range(pieces):
                    c = T // pieces
                    last = pe.matmul(t[:, c * k:c * (k + 1)], w(k), x(k), start=True, stop=True)
                last.then_inc(full, 1)

            def ffn(i, l):
                ab = "ab"[l]
                b, u = pjn(f"hT{l}")
                for f in range(NF):
                    if f == 0:
                        pe.wait_ge(s_pje[b], i * PB + u)
                    project(i, f"y{ab}{f}", lambda k: w1[:, l, P * f:P * (f + 1)], lambda k: hT[:, :], 1)
                for f in range(NF):
                    b, u = pjn(f"y{ab}{f}")
                    pe.wait_ge(s_pje[b], i * PB + u)
                t, full = bank(i, "f" + ab)
                for k in range(NT):
                    for f in range(NF):
                        last = pe.matmul(t[:, D * k:D * (k + 1)], y[:, f, P * k:P * (k + 1)], w2[:, l, D * f:D * (f + 1)],
                                         start=f == 0, stop=f == NF - 1)
                last.then_inc(full, 1)

            def project_qk(i, p):
                project(i, f"q{p}", lambda k: wqkv[:, P * p:P * (p + 1)], lambda k: xnT[:, :], 1)
                project(i, f"k{p}", lambda k: wqkv[:, INNER + P * p:INNER + P * (p + 1)], lambda k: xnT[:, :], 1)

            def max_scores0(i, p, n):
                b = p % 3
                j, q = divmod(n, NT)
                m = 8 * p + n
                width = max(P * (q + 1), 2 * P)
                if n == 0:
                    pe.wait_ge(s_spv, i * L0N + 8 * p + 8)
                    pe.wait_ge(s_spa, i * (4 * NPAIR) + 4 * p + 4)
                if m >= 2:
                    pe.wait_ge(s_mxd, i * MXN + m - 1)
                for x, y_, rows, first in ((QA, KA, P, True), (QB, KB, ROW_MAX, False)):
                    last = pe.matmul(mxp[m % 2][:, 0:width], x[0:rows, b, j, P * q:P * (q + 1)],
                                     y_[0:rows, b, j, 0:width], start=first, stop=not first)
                last.then_inc(s_mxf, 1)

            def key_scores0(i, p, n):
                b = p % 3
                j, k = divmod(n, NT)
                m = 8 * p + n
                q0 = min(P * k, T - 2 * P)
                if n == 0:
                    pe.wait_ge(s_mdma[p % 2], i * (16 * NPAIR) + 32 * (p // 2 + 1))
                if m >= 2:
                    pe.wait_ge(s_exp, i * MXN + m - 1)
                for x, y_, rows, first in ((KA, QA, P, True), (KB, QB, ROW_MAX + 2, False)):
                    last = pe.matmul(stp[m % 2][:, 0:T - q0], x[0:rows, b, j, P * k:P * (k + 1)],
                                     y_[0:rows, b, j, q0:T], start=first, stop=False, skip_group_check=True)
                c0 = P * k - q0
                last = pe.matmul(stp[m % 2][:, c0:c0 + P], identb[:, :], causalb[:, :], start=False, stop=True,
                                 skip_group_check=True)
                last.then_inc(s_st, 1)

            def pv0(i, p):
                pe.wait_ge(s_exp, i * MXN + 8 * p + 8)
                if p >= 2:
                    pe.wait_ge(s_att, i * NPAIR + p - 1)
                for k in range(NT):
                    for j in range(2):
                        base = (2 * (p % 2) + j) * PT0 + OFFS[k]
                        last = pe.matmul(op[p % 2][DH * j:DH * (j + 1), P * k:T], v0[:, k, DH * (2 * p + j):DH * (2 * p + j + 1)],
                                         pt[:, base:base + WIDTH[k]], start=k == 0, stop=k == NT - 1)
                last.then_inc(s_pv, 1)

            def pv1(i, g, k):
                pe.wait_ge(s_exp, i * MXN + L0N + GS * (NT * g + k) + GS)
                if k == 0 and g >= 2:
                    pe.wait_ge(s_or, i * NG + g - 1)
                for j in range(GS):
                    last = pe.matmul(op[g % 2][32 * j:32 * (j + 1), :], v1[:, k, (GS * g + j) // 2, :],
                                     pt[:, (GS * (k % 2) + j) * T:(GS * (k % 2) + j + 1) * T], start=k == 0, stop=k == NT - 1)
                last.then_inc(s_pv1, 1)

            with pe.Fori(0, NB) as i:
                used.clear()
                pe.wait_ge(s_lnv, i * LNV + 12)
                transpose4(i, "xnT0", lambda k: xn[:, k, :])
                b, u = pjn("xnT0")
                pe.wait_ge(s_pje[b], i * PB + u)
                project_qk(i, 0)
                for n in range(2 * NT):
                    project(i, f"v{n}", lambda k: xnT[:, P * (n // 2):P * (n // 2 + 1)],
                            lambda k: wqkv[:, 2 * INNER + T * (n % 2):2 * INNER + T * (n % 2 + 1)], 1)
                pe.wait_ge(s_lnv, i * LNV + 24)
                transpose4(i, "hT0", lambda k: hn[:, k, :])
                ffn(i, 0)
                for s in range(NPAIR + 2):
                    if 1 <= s <= NPAIR:
                        pe.wait_ge(s_mxd, i * MXN + 8 * s)
                        t, full = bank(i, f"m{s - 1}")
                        pe.transpose(t[0:8, 0:P], mx[:, (s - 1) % 2, 0:8], ident[:, :]).then_inc(full, 1)
                    if s + 1 < NPAIR:
                        project_qk(i, s + 1)
                    if s >= 2:
                        pv0(i, s - 2)
                    for n in range(8):
                        if s < NPAIR:
                            max_scores0(i, s, n)
                        if 1 <= s <= NPAIR:
                            key_scores0(i, s - 1, n)
                    if s >= 3 and s % 2 == 1:
                        g = (s - 3) // 2
                        t, full = bank(i, f"l{g}")
                        pe.wait_ge(s_psum, i * L0N + 16 * (g + 1))
                        for c in range(4):
                            last = pe.matmul(t[32 * c:32 * (c + 1), :], ones[:, :], psums[:, c, :], start=True, stop=True)
                        last.then_inc(full, 1)
                t, full = bank(i, "wo0")
                for p in range(NPAIR):
                    pe.wait_ge(s_nrm, i * NPAIR + p + 1)
                    for k in range(NT):
                        last = pe.matmul(t[:, D * k:D * (k + 1)], att[:, p, P * k:P * (k + 1)], wout[:, p, :],
                                         start=p == 0 and k == 0, stop=p == NPAIR - 1, skip_group_check=True)
                last.then_inc(full, 1)
                pe.wait_ge(s_lnv, i * LNV + 24 + 12)
                transpose4(i, "xnT1", lambda k: xn[:, k, :])
                b, u = pjn("xnT1")
                pe.wait_ge(s_pje[b], i * PB + u)
                for c, name in enumerate(("rq", "rqs", "rk", "rks")):
                    project(i, name, lambda k: w_l1[:, c, :], lambda k: xnT[:, :], 1)
                project(i, "vals", lambda k: xnT[:, P * k:P * (k + 1)], lambda k: w_l1[:, 4, :], NT)
                pe.wait_ge(s_lnv, i * LNV + 48)
                transpose4(i, "hT1", lambda k: hn[:, k, :])
                ffn(i, 1)
                b, u = pjn("vals")
                pe.wait_ge(s_pje[b], i * PB + u)
                pe.wait_ge(s_stk, i * NSTK + NSTK)
                for g in range(NG + 1):
                    if g >= 1:
                        pe.wait_ge(s_mxd, i * MXN + L0N + 16 * g)
                        t, full = bank(i, f"n{g - 1}")
                        pe.transpose(t[0:16, 0:P], mx[:, (g - 1) % 2, 0:16], ident[:, :]).then_inc(full, 1)
                    if g >= 2:
                        pe.wait_ge(s_or, i * NG + g - 1)
                        transpose4(i, f"o{g - 2}", lambda k: oraw[:, g % 2, P * k:P * (k + 1)])
                    for n in range(NT * GS):
                        if g < NG:
                            j, q = divmod(n, NT)
                            m = L0N + 16 * g + n
                            pe.wait_ge(s_mxd, i * MXN + m - 1)
                            pe.matmul(mxp[m % 2][:, :], QS[0:ROW_MAX, GS * g + j, P * q:P * (q + 1)],
                                      KS[0:ROW_MAX, GS * g + j, :], start=True, stop=True).then_inc(s_mxf, 1)
                        if g >= 1:
                            k, j = divmod(n, GS)
                            m = L0N + 16 * (g - 1) + n
                            if n == 0:
                                pe.wait_ge(s_nd[(g - 1) % 2], i * 96 + 48 * ((g - 1) // 2 + 1))
                            pe.wait_ge(s_exp, i * MXN + m - 1)
                            pe.matmul(stp[m % 2][:, :], KS[0:ROW_MAX + 3, GS * (g - 1) + j, P * k:P * (k + 1)],
                                      QS[0:ROW_MAX + 3, GS * (g - 1) + j, :], start=True, stop=True).then_inc(s_st, 1)
                            if j == GS - 1 and k >= 1:
                                pv1(i, g - 1, k - 1)
                    if g >= 1:
                        pv1(i, g - 1, NT - 1)
                pe.wait_ge(s_or, i * NG + NG)
                transpose4(i, f"o{NG - 1}", lambda k: oraw[:, (NG - 1) % 2, P * k:P * (k + 1)])
                pe.wait_ge(s_tl, i * 7 * NG + 7 * NG)
                transpose4(i, "oT", lambda k: o1[:, k, :])
                b, u = pjn("oT")
                pe.wait_ge(s_pje[b], i * PB + u)
                project(i, "wo1", lambda k: o1T[:, P * k:P * (k + 1)], lambda k: w_l1[:, 5, :], NT)
                assert len(used) == PJ_USES


def kernel(**inputs):
    import concourse.bacc as bacc
    from concourse.bass_utils import run_bass_kernel_spmd

    nc = bacc.Bacc("TRN2", target_bir_lowering=False, num_devices=1)
    data = {k: np.ascontiguousarray(v) for k, v in inputs.items()}
    swap = np.arange(D) ^ 1
    for n in "qkvo":
        w = data.pop(f"L1_attn_W{n}")
        data[f"t_W{n}T"] = np.ascontiguousarray(w.T)
        if n in "qk":
            data[f"t_W{n}sT"] = np.ascontiguousarray(w[swap].T)
    data.update(tables())
    arrays, a = {}, {}
    for name, v in data.items():
        arrays[f"in_{name}"] = v
        a[name] = nc.dram_tensor(f"in_{name}", v.shape, mybir.dt.from_np(v.dtype), kind="ExternalInput").ap()
    out = nc.dram_tensor("out_x", (NB, T, D), F32, kind="ExternalOutput").ap()
    build_program(nc, a, out)
    r = run_bass_kernel_spmd(nc, [arrays], core_ids=[0])
    return r.results[0]["out_x"]
```

```python
import math
from contextlib import ExitStack

import numpy as np
import concourse.bass as bass
from concourse import mybir

F32 = mybir.dt.float32
F32R = mybir.dt.float32r
BF16 = mybir.dt.bfloat16
I32 = mybir.dt.int32
ACT = mybir.ActivationFunctionType
ALU = mybir.AluOpType
AXIS = mybir.AxisListType

NB = 16
T = 512
D = 128
P = 128
NT = T // P
FF = 512
NF = FF // P
H0, DH = 16, 64
NPAIR = H0 // 2
INNER = H0 * DH
H1, DS = 8, 8
NS = 2 * H1
DV = 2 * DS
NG = 4
GS = NS // NG
LN_EPS = 1e-5
RMS_EPS = 1e-8
LAMBDA_INIT = 0.8 - 0.6 * math.exp(-0.3 * 12)
SLOPES = [2.0 ** (-0.5 * (h + 1)) for h in range(H0)]
MASKED = -3.0e38

WIDTH = [T - P * k for k in range(NT)]
OFFS = [sum(WIDTH[:k]) for k in range(NT)]
PT0 = sum(WIDTH)

ROW_KEY = 64
ROW_MAX = 96


def tables():
    half = np.arange(0, DS, 2, dtype=np.float32) / np.float32(DS)
    inv_freq = (np.float32(1.0) / np.power(np.float32(10000.0), half)).astype(np.float32)
    freqs = (np.arange(T, dtype=np.float32)[:, None] * inv_freq[None, :]).astype(np.float32)
    freqs = np.repeat(freqs, 2, axis=-1).astype(np.float64)
    sign = np.where(np.arange(DS) % 2 == 0, -1.0, 1.0)
    cos = np.cos(freqs).T
    sin = np.sin(freqs).T * sign[:, None]
    rope = np.stack([np.tile(cos, (NS, 1)), np.tile(sin, (NS, 1))], 1)
    causal = np.zeros((P, T), np.float32)
    q, k = np.arange(P)[:, None], np.arange(P)[None, :]
    causal[:, T - P:] = np.where(k > q, np.float32(MASKED), np.float32(0))
    qscale = np.zeros((P, NPAIR), np.float32)
    for p in range(NPAIR):
        for j in range(2):
            qscale[DH * j:DH * (j + 1), p] = DH ** -0.5 / SLOPES[2 * p + j]
    return {
        "t_rope": rope.astype(np.float32),
        "t_causal": causal,
        "t_causalT": np.ascontiguousarray(causal[:, T - P:].T),
        "t_qscale": qscale,
        "t_key": np.arange(T, dtype=np.float32)[None, :],
        "t_ident": np.eye(P, dtype=np.float32),
    }


NU = NS * NT
GU = GS * NT
ROWS_AT = 2
KEY_LAG = GU + 10
HEADS_AT = GU + 5
OUT_AT = GU + 8
NORM_LAG = 6


def l1_rows(t):
    g, r = divmod(t - ROWS_AT, GU)
    return g - 1 if r == 0 and 1 <= g <= NG else None


def l1_heads(t, at, last=NG - 1):
    g, r = divmod(t - KEY_LAG - at, GU)
    return g if r == 0 and 0 <= g < last else None


L1_STEPS = NU + KEY_LAG

ENTRY = ["xnT0", "hT0", "q0", "k0"] + [f"v{n}" for n in range(2 * NT)]
ENTRY_ALL = ENTRY + [f"ya{f}" for f in range(NF)] + ["fa"]


def pj_order():
    order = []
    for s in range(NPAIR + 2):
        if 1 <= s <= NPAIR:
            order.append(f"m{s - 1}")
        if s + 1 < NPAIR:
            order += [f"q{s + 1}", f"k{s + 1}"]
        if s >= 2 and s % 2 == 1:
            order.append(f"l{(s - 3) // 2}")
    order += ENTRY + ["wo0", "xnT1", "rq", "rqs", "rk", "rks", "vals", "hT1"]
    order += [f"yb{f}" for f in range(NF)] + ["fb"]
    for t in range(L1_STEPS):
        if (g := l1_rows(t)) is not None:
            order.append(f"n{g}")
        if (g := l1_heads(t, OUT_AT)) is not None:
            order.append(f"o{g}")
    order += ["ya0", "ya1", f"o{NG - 1}", "ya2", "ya3", "oT", "fa", "wo1"]
    return order


N_PSET = 7
N_VSET = 4
N_VPREP = 19
PJ = {name: n for n, name in enumerate(pj_order())}
PJ_USES = len(PJ)
PJ_ENTRY = {name: n for n, name in enumerate(ENTRY_ALL)}
assert PJ_USES % 2 == 0


def build_program(nc, a, out):
    ctx = ExitStack()
    with ctx:
        def sb(name, shape, dt=F32):
            return ctx.enter_context(nc.sbuf_tensor(name, shape, dt))

        def ps(name):
            return ctx.enter_context(nc.psum_tensor(name, [P, T], F32))

        def sem(name):
            return ctx.enter_context(nc.semaphore(name))

        ident = sb("ident", [P, P])
        causal = sb("causal", [P, T])
        rope = sb("rope", [P, 2, T])
        qscale = sb("qscale", [P, NPAIR])
        identb = sb("identb", [P, P], BF16)
        causalb = sb("causalb", [P, P], BF16)
        ones = sb("ones", [P, 32])
        minus_half = sb("minus_half", [P, 16])
        wqkv = sb("wqkv", [P, 3 * INNER])
        wout = sb("wout", [P, NPAIR, D])
        w1 = sb("w1", [P, 2, FF])
        w2 = sb("w2", [P, 2, NF * D])
        b1 = sb("b1", [P, 2, NF])
        b1h = sb("b1h", [P, 2, NF])
        gamma = sb("gamma", [P, 2])
        beta = sb("beta", [P, 2])
        bias = sb("bias", [P, 2, D])
        w_l1 = sb("w_l1", [P, 6, D])
        lam_in = sb("lam_in", [P, 4, DS])
        lam_pr = sb("lam_pr", [P, 2, DS])
        lam_s = sb("lam_s", [P, 2])
        lam_e = sb("lam_e", [P, 2])
        lam_d = sb("lam_d", [P, 1])
        neglam = sb("neglam", [P, 1])
        lnw_in = sb("lnw_in", [P, 2, DV])
        lnw = sb("lnw", [P, 2, DV])

        x_in = sb("x_in", [P, NT, D])
        xacc = sb("xacc", [P, NT, D])
        xb = sb("xb", [P, NT, D])
        stats = sb("stats", [P, 2, NT, 6])
        mv = sb("mv", [P, 2, NT, 2])
        veps = sb("veps", [P, 2, NT])
        rstd = sb("rstd", [P, 2, NT])
        xnT = sb("xnT", [P, T])
        v0 = sb("v0", [P, NT, INNER])
        rawq = sb("rawq", [P, T])
        rawk = sb("rawk", [P, T])
        QA = sb("QA", [P, 3, 2, T], F32R)
        KA = sb("KA", [P, 3, 2, T], F32R)
        QB = sb("QB", [P, 3, 2, T], F32R)
        KB = sb("KB", [P, 3, 2, T], F32R)
        junk = sb("junk", [P, 2, T], BF16)
        mx = sb("mx", [P, 2, 16])
        mrow = sb("mrow", [16, 2, P], F32R)
        pt = sb("pt", [P, 4 * PT0])
        psums = sb("psums", [P, 4, T])
        tanh = psums[:, 0:2, :]
        xn1 = psums[:, 2, :].rearrange("p (t d) -> p t d", t=NT)
        hn1 = psums[:, 3, :].rearrange("p (t d) -> p t d", t=NT)
        xn0 = rawq[:, :].rearrange("p (t d) -> p t d", t=NT)
        hn0 = rawk[:, :].rearrange("p (t d) -> p t d", t=NT)
        lsb = sb("lsb", [P, T])
        xnT1 = sb("xnT1", [P, T])
        hT = [lsb, xnT1]
        lcol = sb("lcol", [P, 16])
        rcol = sb("rcol", [P, 16])
        rbc = sb("rbc", [P, 2, T])
        big = sb("big", [P, NPAIR * T])
        keyrow = big[ROW_KEY:ROW_KEY + 1, 3 * INNER:3 * INNER + T]
        y = big[:, 0:NF * T].rearrange("p (f t) -> p f t", f=NF)
        att = big[:, :].rearrange("p (h t) -> p h t", h=NPAIR)
        rope_a, rope_b, rot, rest = (big[:, T * c:T * (c + 1)] for c in range(NF, 2 * NF))
        rbch = rbc[:, :, :].rearrange("p b t -> p (b t)").bitcast(BF16)
        parts = [[rbch[:, T * c:T * (c + 1)] for c in range(3)], [rbch[:, 3 * T:4 * T], junk[:, 0, :], junk[:, 1, :]]]
        oraw = big[:, 4 * T:6 * T].rearrange("p (b t) -> p b t", b=2)
        o1 = big[:, 6 * T:7 * T].rearrange("p (t d) -> p t d", t=NT)
        o1T = big[:, 7 * T:8 * T]
        QS = sb("QS", [P, NS, T], BF16)
        KS = sb("KS", [P, NS, T], BF16)
        nrow = sb("nrow", [16, 3, P], BF16)
        nrest = sb("nrest", [16, P])
        v1 = sb("v1", [P, NT, H1, 32])
        rinv = sb("rinv", [P, NT, GS, 1])
        onrm = sb("onrm", [P, NT, GS, DV])
        dif = sb("dif", [P, NT, 2, DV])
        sq = sb("sq", [P, NT, 2, DV])
        ms = sb("ms", [P, NT, 2, 1])
        mse = sb("mse", [P, NT, 2, 1])
        rms = sb("rms", [P, NT, 2, 1])
        od = sq
        ow = sb("ow", [P, NT, 2, DV])

        pj = [ps("pj0"), ps("pj1")]
        mxp = [ps("mx0"), ps("mx1")]
        stp = [ps("st0"), ps("st1")]
        op = [ps("op0"), ps("op1")]

        scr_r = nc.dram_tensor("scr_r", (NPAIR // 2, P, 16), F32).ap()
        scr_p = nc.dram_tensor("scr_p", (2, 3, P, T), BF16).ap()

        s_ld = sem("weights_loaded")
        s_pset = sem("pool_constants")
        s_vset = sem("vector_constants")
        s_vprep = sem("vector_prepared")
        s_aprep = sem("act_prepared")
        s_x = sem("x_loaded")
        s_lnv = sem("ln_vector_steps")
        s_lnp = sem("ln_pool_steps")
        s_pjf = [sem("pj0_full"), sem("pj1_full")]
        s_pje = [sem("pj0_free"), sem("pj1_free")]
        s_tanh = sem("tanh_done")
        s_y = sem("ffn_hidden_ready")
        s_res = sem("residual_steps")
        s_spa = sem("act_split")
        s_spv = sem("vector_split")
        s_mxf = sem("max_scores_ready")
        s_mxd = sem("row_max_done")
        s_mhi = sem("minus_max_high")
        s_mdma = [sem("max_rows_stored0"), sem("max_rows_stored1")]
        s_st = sem("key_scores_ready")
        s_exp = sem("exp_done")
        s_psum = sem("probs_added")
        s_pv = sem("pv_done")
        s_pv1 = sem("pv1_tile_done")
        s_att = sem("attention_copied")
        s_ldma = sem("sums_spread")
        s_rc = sem("sums_inverted")
        s_rst = sem("inverse_stored")
        s_rb = sem("inverse_broadcast")
        s_nrm = sem("attention_normalised")
        s_rot = sem("rope_steps")
        s_part = sem("parts_ready")
        s_pst = sem("parts_stored")
        s_stk = sem("stacks_filled")
        s_nth = sem("minus_max1_high")
        s_nt = sem("minus_max1_rest")
        s_nd = [sem("max1_rows_stored0"), sem("max1_rows_stored1")]
        s_or = sem("heads_copied")
        s_tl = sem("head_norm_steps")
        s_tlp = sem("head_norm_pool_steps")
        s_out = sem("result_stored")

        def pjn(name):
            n = len(ENTRY_ALL) + PJ[name]
            return n % 2, n // 2 + 1

        def entry(i, name):
            if i is None:
                return PJ_ENTRY[name] % 2, PJ_ENTRY[name] // 2 + 1
            b, u = pjn(name)
            return b, i * PB + u

        def before(i, l, n):
            if i is None:
                return 0
            return i * (2 * n) + n * (l + 1)

        def ffn_before(i, l):
            if i is None:
                return 0
            return i * (2 * NF) + NF * (2 - l)

        def sequence(i):
            return 0 if i is None else i + 1

        PB = PJ_USES // 2
        HP = NPAIR // 2
        MXN = 8 * NPAIR + NS * NT
        L0N = 8 * NPAIR
        NSTK = 16 * 12
        stage = {}
        for n in range(4):
            stage[n] = (v0[:, n, 0:FF], v0[:, n, FF:2 * FF])
        b2_in = big[:, 4 * FF:4 * FF + 2 * D].rearrange("p (l d) -> p l d", l=2)
        bo_in = big[:, 4 * FF + 2 * D:4 * FF + 3 * D]

        causal_in = big[:, 3 * INNER + T:3 * INNER + T + P]
        loads = [
            (causal_in, a["t_causalT"]), (ident[:, :], a["t_ident"]), (causal[:, :], a["t_causal"]), (rope[:, :, :], a["t_rope"]),
            (qscale[:, :], a["t_qscale"]), (keyrow, a["t_key"]),
            (wqkv[:, :], a["L0_attn_w_qkv"]),
            (wout[:, :, :], a["L0_attn_w_out"].rearrange("(h p) d -> p h d", p=P)),
            (bo_in, a["L0_attn_b_out"].partition_broadcast(P)),
            (w_l1[:, 0, :], a["t_WqT"]), (w_l1[:, 1, :], a["t_WqsT"]), (w_l1[:, 2, :], a["t_WkT"]),
            (w_l1[:, 3, :], a["t_WksT"]), (w_l1[:, 4, :], a["t_WvT"]), (w_l1[:, 5, :], a["t_WoT"]),
            (lnw_in[:, 0, :], a["L1_attn_ln_w"].partition_broadcast(P)),
            (lnw_in[:, 1, :], a["L1_attn_ln_b"].partition_broadcast(P)),
        ]
        for n, v in enumerate(("q1", "k1", "q2", "k2")):
            loads.append((lam_in[:, n, :], a[f"L1_attn_lambda_{v}"].partition_broadcast(P)))
        for l in range(2):
            f = f"L{l}_ffn_"
            loads += [
                (b1[:, l, :], a[f + "fc1_bias"].rearrange("(f p) -> p f", p=P)),
                (gamma[:, l:l + 1], a[f + "ln_gamma"].rearrange("(p o) -> p o", o=1)),
                (beta[:, l:l + 1], a[f + "ln_beta"].rearrange("(p o) -> p o", o=1)),
                (b2_in[:, l, :], a[f + "fc2_bias"].partition_broadcast(P)),
                (stage[2 * l][0].bitcast(I32), a[f + "fc1_q"]),
                (stage[2 * l][1], a[f + "fc1_scales"].rearrange("g n -> (g n)").partition_broadcast(P)),
                (stage[2 * l + 1][0].rearrange("p (f d) -> p f d", f=NF).bitcast(I32),
                 a[f + "fc2_q"].rearrange("(f p) d -> p f d", p=P)),
                (stage[2 * l + 1][1], a[f + "fc2_scales"].rearrange("g n -> (g n)").partition_broadcast(P)),
            ]
        NLOAD = 16 * len(loads)

        block = ctx.enter_context(nc.Block())

        @block.sync
        def _(sp):
            x_v = a["L0_attn_x"].rearrange("b (t p) d -> b p t d", p=P)
            out_v = out.rearrange("b (t p) d -> b p t d", p=P)
            with nc.allow_non_contiguous_dma(reason="a few hundred biases and gains, once"):
                for dst, src in loads:
                    sp.dma_start(dst, src).then_inc(s_ld, 16)
            sp.dma_start(x_in[:, :, :], x_v[0]).then_inc(s_x, 16)

            b, n = entry(None, "fa")
            sp.wait_ge(s_pje[b], n)
            sp.dma_start(x_in[:, :, :], x_v[1 % NB]).then_inc(s_x, 16)

            def inverse(i, g):
                sp.wait_ge(s_rc, i * HP + g + 1)
                sp.dma_start(scr_r[g], rcol[:, :]).then_inc(s_rst, 16)
                inverse_stored = sp.to_reg(i * (16 * HP) + 16 * (g + 1))
                rbc_used = sp.to_reg(i * NPAIR + 2 * g) if g else 0
                sp.wait_ge(s_ld, NLOAD)
                sp.wait_ge(s_rst, inverse_stored)
                v = scr_r[g].rearrange("(p j c) e -> j p (c e)", p=2, j=2)
                if g:
                    sp.wait_ge(s_nrm, rbc_used)
                for j in range(2):
                    sp.dma_start(rbc[DH * j:DH * (j + 1), :, :], v[j:j + 1].broadcast_to([DH, 2, T])).then_inc(s_rb, 16)

            with sp.Fori(0, NB) as i:
                for s in range(NPAIR + 2):
                    if 1 <= s <= NPAIR:
                        p = s - 1
                        b, u = pjn(f"m{p}")
                        sp.wait_ge(s_pje[b], i * PB + u)
                        for r in range(2):
                            row = QB[ROW_MAX + r:ROW_MAX + r + 1, p % 3, :, :]
                            sp.dma_start(row.bitcast(F32).rearrange("o j (c f) -> o (j c) f", f=P),
                                         mrow[0:8, r, :].bitcast(F32)).then_inc(s_mdma[p % 2], 16)
                    if s >= 4 and s % 2 == 0:
                        inverse(i, (s - 4) // 2)
                    if s >= 3 and s % 2 == 1:
                        b, u = pjn(f"l{(s - 3) // 2}")
                        sp.wait_ge(s_pje[b], i * PB + u)
                        sp.dma_start(lcol[:, :], lsb[0:P:32, :].rearrange("h (c e) -> h c e", e=16)).then_inc(s_ldma, 16)
                inverse(i, HP - 1)
                sp.wait_ge(s_part, i * 6 + 6)
                sp.dma_start(scr_p[0].rearrange("c p t -> p c t"), rbch[:, 0:3 * T].rearrange("p (c t) -> p c t", c=3)).then_inc(s_pst, 16)
                sp.dma_start(scr_p[1, 0], parts[1][0]).then_inc(s_pst, 16)
                sp.dma_start(scr_p[1, 1:3].rearrange("c p t -> p c t"), junk[:, :, :]).then_inc(s_pst, 16)
                sp.wait_ge(s_pst, i * 48 + 48)
                for w, (dst, order) in enumerate(((QS, (0, 0, 1, 1, 0, 2)), (KS, (0, 1, 0, 1, 2, 0)))):
                    for slot, c in enumerate(order):
                        sp.dma_start(dst[DS * slot:DS * (slot + 1), :, :],
                                     scr_p[w, c].rearrange("(s d) t -> d s t", d=DS)).then_inc(s_stk, 16)
                for g in range(NG):
                    sp.wait_ge(s_nt, i * 2 * NG + 2 * g + 2)
                    for r in range(3):
                        row = QS[ROW_MAX + r:ROW_MAX + r + 1, GS * g:GS * (g + 1), :]
                        sp.dma_start(row.rearrange("o s (c f) -> o (s c) f", f=P), nrow[:, r, :]).then_inc(s_nd[g % 2], 16)
                x_after = sp.snap((i + 2) % NB)
                b, u = pjn("fa")
                x_used = sp.to_reg(i * PB + u)
                sp.wait_ge(s_ld, NLOAD)
                sp.wait_ge(s_pje[b], x_used)
                sp.dma_start(x_in[:, :, :], x_v[bass.ds(x_after, 1)].rearrange("b p t d -> p (b t) d")).then_inc(s_x, 16)
                b, u = pjn("wo1")
                sp.wait_ge(s_pje[b], i * PB + u)
                sp.dma_start(out_v[bass.ds(i, 1)].rearrange("b p t d -> p (b t) d"), xacc[:, :, :]).then_inc(s_out, 16)
                stored = sp.to_reg(i * 16 + 16)
                sp.wait_ge(s_ld, NLOAD)
                sp.wait_ge(s_out, stored)
            sp.wait_ge(s_x, 16 * NB + 32)

        @block.gpsimd
        def _(pool):
            pool.memset(ones[:, :], 1.0).then_inc(s_pset, 1)
            pool.memset(minus_half[:, :], -0.5).then_inc(s_pset, 1)
            pool.memset(v1[:, :, :, :], 0.0).then_inc(s_pset, 1)
            pool.memset(QS[:, :, :], 0.0).then_inc(s_pset, 1)
            pool.memset(KS[:, :, :], 0.0).then_inc(s_pset, 1)
            pool.wait_ge(s_pset, 5)
            pool.memset(v1[:, :, :, DV:DV + 1], 1.0).then_inc(s_pset, 1)
            pool.wait_ge(s_pset, 6)
            pool.memset(KS[ROW_MAX:ROW_MAX + 3, :, :], 1.0).then_inc(s_pset, 1)
            pool.wait_ge(s_pset, N_PSET)
            pool.wait_ge(s_vprep, N_VPREP)

            def ln_scale(i, l, part):
                n = before(i, l, 4) + 2 * part
                mv_there = before(i, l, 24) + (8 if part == 0 else 20)
                mv_there = mv_there if i is None else pool.to_reg(mv_there)
                pool.wait_ge(s_pset, N_PSET)
                pool.wait_ge(s_lnv, mv_there)
                pool.tensor_scalar(veps[:, part, :], mv[:, part, :, 1], 1.0, LN_EPS, ALU.mult, ALU.add).then_inc(s_lnp, 1)
                pool.wait_ge(s_lnp, n + 1)
                pool.tensor_tensor(rstd[:, part, :], veps[:, part, :], minus_half[:, 0:NT], ALU.pow).then_inc(s_lnp, 1)

            def residual(i, l, x, xn):
                pool.wait_ge(s_lnv, before(i, l, 24) + 12)
                pool.tensor_tensor(x[:, :, :], x[:, :, :], xn, ALU.add).then_inc(s_res, 1)
                pool.wait_ge(s_res, before(i, l, 2) + 1)
                pool.tensor_tensor(x[:, :, :], x[:, :, :], bias[:, l:l + 1, :].broadcast_to([P, NT, D]), ALU.add).then_inc(s_res, 1)

            def normalise(i, p):
                pool.wait_ge(s_rb, i * (32 * HP) + 32 * (p // 2 + 1))
                pool.wait_ge(s_att, i * NPAIR + p + 1)
                pool.tensor_tensor(att[:, p, :], att[:, p, :], rbc[:, p % 2, :], ALU.mult).then_inc(s_nrm, 1)

            ln_scale(None, 0, 0)
            ln_scale(None, 0, 1)
            residual(None, 0, x_in, xn0)
            with pool.Fori(0, NB) as i:
                for s in range(1, NPAIR + 2):
                    if s == NPAIR:
                        ln_scale(i, 0, 0)
                    if s <= NPAIR:
                        p = s - 1
                        if p >= 2 and p % 2 == 0:
                            b, u = pjn(f"l{p // 2 - 1}")
                            pool.wait_ge(s_pjf[b], i * PB + u)
                        for j in range(2):
                            base = (2 * (p % 2) + j) * PT0
                            c = (2 * p + j) % 4
                            for k in range(NT):
                                n = 8 * p + 4 * j + k
                                tile = pt[:, base + OFFS[k]:base + OFFS[k] + WIDTH[k]]
                                tile_there = pool.to_reg(i * MXN + n + 1)
                                if k == 0:
                                    pool.wait_ge(s_pset, N_PSET)
                                pool.wait_ge(s_exp, tile_there)
                                if k == 0:
                                    pool.tensor_copy(psums[:, c, 0:P], tile[:, 0:P]).then_inc(s_psum, 1)
                                    continue
                                so_far = pt[:, base + P:base + T] if k == 1 else psums[:, c, P * k:T]
                                pool.wait_ge(s_psum, i * L0N + n)
                                pool.tensor_tensor(psums[:, c, P * k:T], so_far, tile, ALU.add).then_inc(s_psum, 1)
                    if s >= 5 and s % 2 == 1:
                        normalise(i, s - 5)
                        normalise(i, s - 4)
                    if s == NPAIR:
                        ln_scale(i, 0, 1)
                        residual(i, 0, x_in, xn0)
                normalise(i, NPAIR - 2)
                normalise(i, NPAIR - 1)
                ln_scale(i, 1, 0)
                ln_scale(i, 1, 1)
                residual(i, 1, xacc, xn1)
                for g in range(NG):
                    ms_there = pool.to_reg(i * 7 * NG + 7 * g + 4)
                    pool.wait_ge(s_pset, N_PSET)
                    pool.wait_ge(s_tl, ms_there)
                    pool.tensor_scalar(mse[:, :, :, :], ms[:, :, :, :], 1.0 / DV, RMS_EPS, ALU.mult, ALU.add).then_inc(s_tlp, 1)
                    pool.wait_ge(s_tlp, i * 2 * NG + 2 * g + 1)
                    pool.tensor_tensor(rms[:, :, :, 0].rearrange("p t h -> p (t h)"), mse[:, :, :, 0].rearrange("p t h -> p (t h)"),
                                       minus_half[:, 0:2 * NT], ALU.pow).then_inc(s_tlp, 1)

        @block.scalar
        def _(act):
            act.wait_ge(s_ld, NLOAD)
            act.wait_ge(s_vset, N_VSET)
            for n in range(6):
                act.activation(KB[ROW_KEY:ROW_KEY + 1, n // 2, n % 2, :], keyrow, ACT.Copy).then_inc(s_aprep, 1)
            act.activation(b1h[:, :, :], b1[:, :, :], ACT.Copy, scale=0.5).then_inc(s_aprep, 1)
            act.wait_ge(s_vprep, 2)
            act.activation(lam_e[:, :], lam_s[:, :], ACT.Exp).then_inc(s_aprep, 1)
            act.wait_ge(s_aprep, 8)
            act.wait_ge(s_pset, N_PSET)

            def transposed(b, n, l, name):
                act.wait_ge(s_pjf[b], n)
                if name == "h":
                    act.activation(hT[l][:, :], pj[b][:, :], ACT.Identity, scale=gamma[:, l:l + 1],
                                   bias=beta[:, l:l + 1]).then_inc(s_pje[b], 1)
                else:
                    act.activation((xnT, xnT1)[l][:, :], pj[b][:, :], ACT.Copy).then_inc(s_pje[b], 1)

            def ffn_act(i, l, f):
                b, n = entry(i, f"y{'ab'[l]}{f}")
                act.wait_ge(s_pjf[b], n)
                if f >= 2:
                    act.wait_ge(s_y, ffn_before(i, l) + f - 1)
                act.activation(tanh[:, f % 2, :], pj[b][:, :], ACT.Tanh, scale=0.5,
                               bias=b1h[:, l, f:f + 1]).then_inc(s_tanh, 1)
                act.activation(y[:, f, :], pj[b][:, :], ACT.Identity, bias=b1[:, l, f:f + 1]).then_inc(s_pje[b], 1)

            def values(i):
                for n in range(2 * NT):
                    b, m = entry(i, f"v{n}")
                    act.wait_ge(s_pjf[b], m)
                    act.activation(v0[:, n // 2, T * (n % 2):T * (n % 2 + 1)], pj[b][:, :], ACT.Copy).then_inc(s_pje[b], 1)

            def split(p, seq, q_use, k_use, st_before):
                b = p % 3
                bq, nq = q_use
                bk, nk = k_use
                if p:
                    act.wait_ge(s_spv, seq * L0N + 8 * p)
                    act.wait_ge(s_spa, seq * (4 * NPAIR) + 4 * p)
                act.wait_ge(s_pjf[bq], nq)
                act.activation(rawq[:, :], pj[bq][:, :], ACT.Copy, scale=qscale[:, p:p + 1]).then_inc(s_pje[bq], 1)
                act.wait_ge(s_pjf[bk], nk)
                act.activation(rawk[:, :], pj[bk][:, :], ACT.Copy).then_inc(s_pje[bk], 1)
                if st_before is not None:
                    act.wait_ge(s_st, st_before)
                act.wait_ge(s_pje[bq], nq)
                for j in range(2):
                    act.activation(QB[0:DH, b, j, :], rawq[DH * j:DH * (j + 1), :], ACT.Copy).then_inc(s_spa, 1)
                act.wait_ge(s_pje[bk], nk)
                for j in range(2):
                    act.activation(KA[DH * (1 - j):DH * (2 - j), b, j, :], rawk[DH * j:DH * (j + 1), :],
                                   ACT.Copy).then_inc(s_spa, 1)

            def split_in_loop(i, p):
                split(p, i, entry(i, f"q{p}"), entry(i, f"k{p}"), i * MXN + 8 * (p - 2) if p >= 3 else None)

            def entry_act(i):
                transposed(*entry(i, "xnT0"), 0, "x")
                if i is not None:
                    act.wait_ge(s_ldma, i * (16 * HP) + 16 * HP)
                transposed(*entry(i, "hT0"), 0, "h")
                act.wait_ge(s_res, before(i, 0, 2) + 2)
                split(0, sequence(i), entry(i, "q0"), entry(i, "k0"), None if i is None else i * MXN + 8 * (NPAIR - 1))
                values(i)

            def copy_heads(i, g):
                act.wait_ge(s_pv1, i * NG * NT + NT * (g + 1))
                act.activation(oraw[:, g % 2, :], op[g % 2][:, :], ACT.Copy).then_inc(s_or, 1)

            entry_act(None)
            for f in range(NF):
                ffn_act(None, 0, f)
            with act.Fori(0, NB) as i:
                for s in range(NPAIR + 2):
                    if 1 <= s <= NPAIR:
                        p = s - 1
                        b, u = pjn(f"m{p}")
                        act.wait_ge(s_pjf[b], i * PB + u)
                        if p:
                            act.wait_ge(s_mdma[(p - 1) % 2], i * (16 * NPAIR) + 32 * ((p - 1) // 2 + 1))
                        act.activation(mrow[0:8, 0, :], pj[b][0:8, 0:P], ACT.Copy, scale=-1.0).then_inc(s_mhi, 1)
                    if s + 1 < NPAIR:
                        split_in_loop(i, s + 1)
                    if s >= 2:
                        act.wait_ge(s_pv, i * NPAIR + s - 1)
                        act.activation(att[:, s - 2, :], op[s % 2][:, :], ACT.Copy).then_inc(s_att, 1)
                    if 1 <= s <= NPAIR:
                        p = s - 1
                        for j in range(2):
                            base = (2 * (p % 2) + j) * PT0
                            if p >= 2:
                                act.wait_ge(s_pv, i * NPAIR + p - 1)
                                act.wait_ge(s_psum, i * L0N + 8 * (p - 2) + 4 * (j + 1))
                            for k in range(NT):
                                n = 8 * p + 4 * j + k
                                act.wait_ge(s_st, i * MXN + n + 1)
                                c0 = P if k == NT - 1 else 0
                                act.activation(pt[:, base + OFFS[k]:base + OFFS[k] + WIDTH[k]],
                                               stp[n % 2][:, c0:c0 + WIDTH[k]], ACT.Exp,
                                               scale=SLOPES[2 * p + j]).then_inc(s_exp, 1)
                    if s >= 3 and s % 2 == 1:
                        g = (s - 3) // 2
                        b, u = pjn(f"l{g}")
                        act.wait_ge(s_pjf[b], i * PB + u)
                        if g:
                            act.wait_ge(s_ldma, i * (16 * HP) + 16 * g)
                        act.activation(lsb[:, :], pj[b][:, :], ACT.Copy).then_inc(s_pje[b], 1)
                entry_act(i)
                transposed(*entry(i, "xnT1"), 1, "x")
                b, u = pjn("vals")
                act.wait_ge(s_pjf[b], i * PB + u)
                act.activation(v1[:, :, :, 0:DV], pj[b][:, :].rearrange("p (t h e) -> p t h e", t=NT, h=H1),
                               ACT.Copy).then_inc(s_pje[b], 1)
                transposed(*entry(i, "hT1"), 1, "h")
                for f in range(NF):
                    ffn_act(i, 1, f)
                for t in range(L1_STEPS):
                    if (g := l1_rows(t)) is not None:
                        b, u = pjn(f"n{g}")
                        act.wait_ge(s_pjf[b], i * PB + u)
                        if g:
                            act.wait_ge(s_nd[(g - 1) % 2], i * 96 + 48 * ((g - 1) // 2 + 1))
                        act.activation(nrow[:, 0, :], pj[b][0:16, 0:P], ACT.Copy, scale=-1.0).then_inc(s_nth, 1)
                    if (g := l1_heads(t, HEADS_AT)) is not None:
                        copy_heads(i, g)
                    if (n := t - KEY_LAG) >= 0:
                        m, j = divmod(n, GS)
                        if m >= 2 and j == 0:
                            act.wait_ge(s_pv1, i * NG * NT + m - 1)
                        act.wait_ge(s_st, i * MXN + L0N + n + 1)
                        act.activation(pt[:, (GS * (m % 2) + j) * T:(GS * (m % 2) + j + 1) * T], stp[n % 2][:, :],
                                       ACT.Exp, scale=float(DS) ** -0.25).then_inc(s_exp, 1)
                ffn_act(i, 0, 0)
                copy_heads(i, NG - 1)
                for f in range(1, NF):
                    ffn_act(i, 0, f)
                b, u = pjn("oT")
                act.wait_ge(s_pjf[b], i * PB + u)
                act.activation(o1T[:, :], pj[b][:, :], ACT.Copy).then_inc(s_pje[b], 1)

        @block.vector
        def _(dve):
            for t in (QB, KB):
                dve.memset(t[DH:P, :, :, :].bitcast(F32), 0.0).then_inc(s_vset, 1)
            dve.wait_ge(s_vset, 2)
            dve.memset(QB[ROW_KEY:ROW_KEY + 1, :, :, :].bitcast(F32), 1.0).then_inc(s_vset, 1)
            dve.memset(KB[ROW_MAX:ROW_MAX + 2, :, :, :].bitcast(F32), 1.0).then_inc(s_vset, 1)
            assert N_VSET == 4
            dve.wait_ge(s_ld, NLOAD)
            dve.tensor_tensor(lam_pr[:, :, :], lam_in[:, 0:4:2, :], lam_in[:, 1:4:2, :], ALU.mult).then_inc(s_vprep, 1)
            dve.wait_ge(s_vprep, 1)
            dve.reduce_sum(lam_s[:, :], lam_pr[:, :, :], AXIS.X).then_inc(s_vprep, 1)
            dve.wait_ge(s_aprep, 8)
            dve.tensor_tensor(lam_d[:, :], lam_e[:, 1:2], lam_e[:, 0:1], ALU.subtract).then_inc(s_vprep, 1)
            dve.wait_ge(s_vprep, 3)
            dve.tensor_scalar(neglam[:, :], lam_d[:, :], -LAMBDA_INIT, None, ALU.add).then_inc(s_vprep, 1)
            dve.tensor_scalar(lnw[:, :, :], lnw_in[:, :, :], 1.0 - LAMBDA_INIT, None, ALU.mult).then_inc(s_vprep, 1)
            n_prep = 5
            for n in range(4):
                l, second = divmod(n, 2)
                asf = big[:, FF * n:FF * (n + 1)]
                dst = (w2 if second else w1)[:, l, :]
                dve.tensor_copy(asf, stage[n][0].bitcast(I32)).then_inc(s_vprep, 1)
                dve.wait_ge(s_vprep, n_prep + 1)
                dve.scalar_tensor_tensor(out=dst, in0=asf, scalar=-128.0, in1=stage[n][1],
                                         op0=ALU.add, op1=ALU.mult).then_inc(s_vprep, 1)
                n_prep += 2
                if second:
                    dve.wait_ge(s_vprep, n_prep)
                    dve.tensor_scalar(dst, dst, 0.25, None, ALU.mult).then_inc(s_vprep, 1)
                    n_prep += 1
            dve.tensor_copy(identb[:, :], ident[:, :]).then_inc(s_vprep, 1)
            dve.tensor_copy(causalb[:, :], causal_in).then_inc(s_vprep, 1)
            n_prep += 2
            dve.tensor_scalar(bias[:, :, :], b2_in, 0.5, None, ALU.mult).then_inc(s_vprep, 1)
            n_prep += 1
            dve.wait_ge(s_vprep, n_prep)
            dve.tensor_tensor(bias[:, 0, :], bias[:, 0, :], bo_in, ALU.add).then_inc(s_vprep, 1)
            n_prep += 1
            assert n_prep == N_VPREP
            dve.wait_ge(s_vprep, n_prep)

            def layer_norm(i, l, part, inp, dst):
                n = before(i, l, 24) + 12 * part
                for t in range(NT):
                    dve.bn_stats(stats[:, part, t, :], inp[:, t, :]).then_inc(s_lnv, 1)
                stats_there = n + 4 if i is None else dve.to_reg(n + 4)
                dve.wait_ge(s_vset, N_VSET)
                dve.wait_ge(s_lnv, stats_there)
                for t in range(NT):
                    dve.bn_aggr(mv[:, part, t, :], stats[:, part, t, :]).then_inc(s_lnv, 1)
                dve.wait_ge(s_lnv, n + 8)
                dve.wait_ge(s_lnp, before(i, l, 4) + 2 * part + 2)
                for t in range(NT):
                    dve.tensor_scalar(dst[:, t, :], inp[:, t, :], mv[:, part, t, 0:1], rstd[:, part, t:t + 1],
                                      ALU.subtract, ALU.mult).then_inc(s_lnv, 1)
                dve.wait_ge(s_lnv, n + 12)

            def ffn_dve(i, l, f):
                b, n = entry(i, f"y{'ab'[l]}{f}")
                dve.wait_ge(s_tanh, ffn_before(i, l) + f + 1)
                dve.wait_ge(s_pje[b], n)
                dve.scalar_tensor_tensor(out=y[:, f, :], in0=tanh[:, f % 2, :], scalar=1.0, in1=y[:, f, :],
                                         op0=ALU.add, op1=ALU.mult).then_inc(s_y, 1)

            def ffn_end(i, l, dst, src):
                b, n = entry(i, "f" + "ab"[l])
                dve.wait_ge(s_pjf[b], n)
                dve.wait_ge(s_res, before(i, l, 2) + 2)
                dve.tensor_tensor(dst[:, :, :], pj[b][:, :].rearrange("p (t d) -> p t d", t=NT), src[:, :, :],
                                  ALU.add).then_inc(s_pje[b], 1)

            def split_high(p, q_use, k_use, st_before):
                b = p % 3
                if st_before is not None:
                    dve.wait_ge(s_st, st_before)
                for t, raw, (bb, n) in ((QA, rawq, q_use), (KA, rawk, k_use)):
                    dve.wait_ge(s_pje[bb], n)
                    for j in range(2):
                        r = slice(DH * j, DH * (j + 1))
                        dve.tensor_copy(t[r, b, j, :], raw[r, :]).then_inc(s_spv, 1)

            def split_low(seq, p, n):
                b = p % 3
                which, j = divmod(n, 2)
                r = slice(DH * j, DH * (j + 1))
                o = slice(DH * (1 - j), DH * (2 - j))
                dve.wait_ge(s_spv, seq * L0N + 8 * p + n + 1)
                if which == 0:
                    dve.tensor_tensor(QA[o, b, j, :], rawq[r, :], QA[r, b, j, :].bitcast(F32), ALU.subtract).then_inc(s_spv, 1)
                else:
                    dve.tensor_tensor(KB[0:DH, b, j, :], rawk[r, :], KA[r, b, j, :].bitcast(F32), ALU.subtract).then_inc(s_spv, 1)

            def entry_split(i):
                split_high(0, entry(i, "q0"), entry(i, "k0"), None if i is None else i * MXN + 8 * (NPAIR - 1))
                for n in range(4):
                    split_low(sequence(i), 0, n)

            def inverse_sums(i, g):
                dve.wait_ge(s_ldma, i * (16 * HP) + 16 * (g + 1))
                if g:
                    dve.wait_ge(s_rst, i * (16 * HP) + 16 * g)
                dve.reciprocal(rcol[:, :], lcol[:, :]).then_inc(s_rc, 1)

            def head_norm_a(i, g):
                b, u = pjn(f"o{g}")
                n = i * 7 * NG + 7 * g
                v = pj[b][:, :].rearrange("p (t j e) -> p t j e", t=NT, j=GS)
                dve.wait_ge(s_pjf[b], i * PB + u)
                dve.reciprocal(rinv[:, :, :, :], v[:, :, :, DV:DV + 1]).then_inc(s_tl, 1)
                dve.wait_ge(s_tl, n + 1)
                dve.tensor_tensor(onrm[:, :, :, :], v[:, :, :, 0:DV], rinv[:, :, :, :].broadcast_to([P, NT, GS, DV]),
                                  ALU.mult).then_inc(s_pje[b], 1)
                dve.wait_ge(s_pje[b], i * PB + u)
                dve.scalar_tensor_tensor(out=dif[:, :, :, :], in0=onrm[:, :, 1:GS:2, :], scalar=neglam[:, 0:1],
                                         in1=onrm[:, :, 0:GS:2, :], op0=ALU.mult, op1=ALU.add).then_inc(s_tl, 1)
                dve.wait_ge(s_tl, n + 2)
                dve.tensor_tensor(sq[:, :, :, :], dif[:, :, :, :], dif[:, :, :, :], ALU.mult).then_inc(s_tl, 1)
                dve.wait_ge(s_tl, n + 3)
                dve.reduce_sum(ms[:, :, :, 0], sq[:, :, :, :], AXIS.X).then_inc(s_tl, 1)

            def head_norm_b(i, g):
                n = i * 7 * NG + 7 * g
                dve.wait_ge(s_tlp, i * 2 * NG + 2 * g + 2)
                dve.tensor_tensor(od[:, :, :, :], dif[:, :, :, :], rms[:, :, :, :].broadcast_to([P, NT, 2, DV]),
                                  ALU.mult).then_inc(s_tl, 1)
                wide = lnw[:, :, :].rearrange("p (w a b) e -> p w a b e", a=1, b=1)
                dve.wait_ge(s_tl, n + 5)
                dve.tensor_tensor(ow[:, :, :, :], od[:, :, :, :], wide[:, 0].broadcast_to([P, NT, 2, DV]),
                                  ALU.mult).then_inc(s_tl, 1)
                dve.wait_ge(s_tl, n + 6)
                dve.tensor_tensor(o1[:, :, 2 * DV * g:2 * DV * (g + 1)].rearrange("p t (h e) -> p t h e", e=DV),
                                  ow[:, :, :, :], wide[:, 1].broadcast_to([P, NT, 2, DV]), ALU.add).then_inc(s_tl, 1)

            dve.wait_ge(s_x, 16)
            layer_norm(None, 0, 0, x_in, xn0)
            layer_norm(None, 0, 1, xn0, hn0)
            entry_split(None)
            for f in range(NF):
                ffn_dve(None, 0, f)
            ffn_end(None, 0, xb, x_in)
            with dve.Fori(0, NB) as i:
                for s in range(NPAIR + 2):
                    if 1 <= s <= NPAIR:
                        p = s - 1
                        b, u = pjn(f"m{p}")
                        dve.wait_ge(s_mhi, i * NPAIR + p + 1)
                        dve.scalar_tensor_tensor(out=mrow[0:8, 1, :], in0=pj[b][0:8, 0:P], scalar=-1.0,
                                                 in1=mrow[0:8, 0, :].bitcast(F32), op0=ALU.mult,
                                                 op1=ALU.subtract).then_inc(s_pje[b], 1)
                    if s >= 4 and s % 2 == 0:
                        inverse_sums(i, (s - 4) // 2)
                    if s + 1 < NPAIR:
                        split_high(s + 1, entry(i, f"q{s + 1}"), entry(i, f"k{s + 1}"),
                                   i * MXN + 8 * (s - 1) if s >= 2 else None)
                    if s == NPAIR:
                        dve.wait_ge(s_x, i * 16 + 32)
                        dve.wait_ge(s_spa, i * (4 * NPAIR) + 4 * NPAIR)
                        dve.wait_ge(s_spv, i * L0N + 8 * NPAIR)
                        layer_norm(i, 0, 0, x_in, xn0)
                        layer_norm(i, 0, 1, xn0, hn0)
                    if s < NPAIR:
                        for n in range(8):
                            j, q = divmod(n, NT)
                            m = 8 * s + n
                            width = P * (q + 1)
                            scores_there = dve.to_reg(i * MXN + m + 1)
                            junk_free = dve.to_reg(i * MXN + m - 1) if m >= 2 else 0
                            dve.wait_ge(s_vset, N_VSET)
                            dve.wait_ge(s_mxf, scores_there)
                            if m >= 2:
                                dve.wait_ge(s_mxd, junk_free)
                            dve.tensor_tensor_reduce(out=junk[:, m % 2, 0:width], in0=mxp[m % 2][:, 0:width],
                                                     in1=causal[:, T - width:T], scale=1.0, scalar=MASKED,
                                                     op0=ALU.add, op1=ALU.max,
                                                     accum_out=mx[:, s % 2, n:n + 1]).then_inc(s_mxd, 1)
                            if s + 1 < NPAIR and n < 4:
                                split_low(i, s + 1, n)
                inverse_sums(i, HP - 1)
                b, u = pjn("wo0")
                dve.wait_ge(s_pjf[b], i * PB + u)
                dve.tensor_tensor(xacc[:, :, :], pj[b][:, :].rearrange("p (t d) -> p t d", t=NT), xb[:, :, :],
                                  ALU.add).then_inc(s_pje[b], 1)
                dve.wait_ge(s_pje[b], i * PB + u)
                layer_norm(i, 1, 0, xacc, xn1)
                for w in range(2):
                    n_rot, n_part = i * 4 + 2 * w, i * 6 + 3 * w
                    for tmp, c, name in ((rope_a, 0, "rq" if w == 0 else "rk"), (rope_b, 1, "rqs" if w == 0 else "rks")):
                        b, u = pjn(name)
                        dve.wait_ge(s_pjf[b], i * PB + u)
                        dve.tensor_tensor(tmp, pj[b][:, :], rope[:, c, :], ALU.mult).then_inc(s_pje[b], 1)
                    for name in (("rq", "rqs"), ("rk", "rks"))[w]:
                        b, u = pjn(name)
                        dve.wait_ge(s_pje[b], i * PB + u)
                    dve.tensor_tensor(rot, rope_a, rope_b, ALU.add).then_inc(s_rot, 1)
                    dve.wait_ge(s_rot, n_rot + 1)
                    dve.tensor_copy(parts[w][0], rot).then_inc(s_part, 1)
                    dve.wait_ge(s_part, n_part + 1)
                    dve.tensor_tensor(rest, rot, parts[w][0], ALU.subtract).then_inc(s_rot, 1)
                    dve.wait_ge(s_rot, n_rot + 2)
                    dve.tensor_copy(parts[w][1], rest).then_inc(s_part, 1)
                    dve.wait_ge(s_part, n_part + 2)
                    dve.tensor_tensor(parts[w][2], rest, parts[w][1], ALU.subtract).then_inc(s_part, 1)
                layer_norm(i, 1, 1, xn1, hn1)
                entry_split(i)
                for f in range(NF):
                    ffn_dve(i, 1, f)
                ffn_end(i, 1, xacc, xacc)
                for t in range(L1_STEPS):
                    if (g := l1_rows(t)) is not None:
                        b, u = pjn(f"n{g}")
                        n = i * 2 * NG + 2 * g
                        dve.wait_ge(s_nth, i * NG + g + 1)
                        dve.scalar_tensor_tensor(out=nrest[:, :], in0=pj[b][0:16, 0:P], scalar=-1.0, in1=nrow[:, 0, :],
                                                 op0=ALU.mult, op1=ALU.subtract).then_inc(s_pje[b], 1)
                        dve.wait_ge(s_pje[b], i * PB + u)
                        dve.tensor_copy(nrow[:, 1, :], nrest[:, :]).then_inc(s_nt, 1)
                        dve.wait_ge(s_nt, n + 1)
                        dve.tensor_tensor(nrow[:, 2, :], nrest[:, :], nrow[:, 1, :], ALU.subtract).then_inc(s_nt, 1)
                    if (g := l1_heads(t, OUT_AT)) is not None:
                        head_norm_a(i, g)
                    if (g := l1_heads(t, OUT_AT + NORM_LAG)) is not None:
                        head_norm_b(i, g)
                    if t < NU:
                        g, n = divmod(t, GU)
                        m = L0N + t
                        dve.wait_ge(s_mxf, i * MXN + m + 1)
                        dve.reduce_max(mx[:, g % 2, n:n + 1], mxp[m % 2][:, :], AXIS.X).then_inc(s_mxd, 1)
                ffn_dve(i, 0, 0)
                head_norm_a(i, NG - 1)
                ffn_dve(i, 0, 1)
                head_norm_b(i, NG - 1)
                ffn_dve(i, 0, 2)
                ffn_dve(i, 0, 3)
                ffn_end(i, 0, xb, x_in)
                b, u = pjn("wo1")
                bf, uf = pjn("fb")
                dve.wait_ge(s_pjf[b], i * PB + u)
                dve.wait_ge(s_pje[bf], i * PB + uf)
                dve.tensor_tensor(xacc[:, :, :], pj[b][:, :].rearrange("p (t d) -> p t d", t=NT), xacc[:, :, :],
                                  ALU.add).then_inc(s_pje[b], 1)

        @block.tensor
        def _(pe):
            pe.wait_ge(s_ld, NLOAD)
            pe.wait_ge(s_pset, N_PSET)
            pe.wait_ge(s_vprep, N_VPREP)
            pe.wait_ge(s_aprep, 8)
            used = []

            def bank(i, name):
                used.append(name)
                b, n = entry(i, name)
                if i is not None or PJ_ENTRY[name] >= 2:
                    pe.wait_ge(s_pje[b], n - 1)
                return pj[b], s_pjf[b]

            def transpose4(i, name, src):
                t, full = bank(i, name)
                for k in range(NT):
                    last = pe.transpose(t[:, P * k:P * (k + 1)], src(k), ident[:, :])
                last.then_inc(full, 1)

            def project(i, name, w, x, pieces):
                t, full = bank(i, name)
                for k in range(pieces):
                    c = T // pieces
                    last = pe.matmul(t[:, c * k:c * (k + 1)], w(k), x(k), start=True, stop=True)
                last.then_inc(full, 1)

            def ffn_first(i, l, f):
                if f == 0:
                    b, n = entry(i, f"hT{l}")
                    pe.wait_ge(s_pje[b], n)
                project(i, f"y{'ab'[l]}{f}", lambda k: w1[:, l, P * f:P * (f + 1)], lambda k: hT[l][:, :], 1)

            def ffn_second(i, l):
                pe.wait_ge(s_y, ffn_before(i, l) + NF)
                t, full = bank(i, "f" + "ab"[l])
                for k in range(NT):
                    for f in range(NF):
                        last = pe.matmul(t[:, D * k:D * (k + 1)], y[:, f, P * k:P * (k + 1)], w2[:, l, D * f:D * (f + 1)],
                                         start=f == 0, stop=f == NF - 1)
                last.then_inc(full, 1)

            def project_qk(i, p):
                project(i, f"q{p}", lambda k: wqkv[:, P * p:P * (p + 1)], lambda k: xnT[:, :], 1)
                project(i, f"k{p}", lambda k: wqkv[:, INNER + P * p:INNER + P * (p + 1)], lambda k: xnT[:, :], 1)

            def max_scores0(i, p, n):
                b = p % 3
                j, q = divmod(n, NT)
                m = 8 * p + n
                width = max(P * (q + 1), 2 * P)
                if n == 0:
                    pe.wait_ge(s_spv, i * L0N + 8 * p + 8)
                    pe.wait_ge(s_spa, i * (4 * NPAIR) + 4 * p + 4)
                if m >= 2:
                    pe.wait_ge(s_mxd, i * MXN + m - 1)
                for x, y_, rows, first in ((QA, KA, P, True), (QB, KB, ROW_MAX, False)):
                    last = pe.matmul(mxp[m % 2][:, 0:width], x[0:rows, b, j, P * q:P * (q + 1)],
                                     y_[0:rows, b, j, 0:width], start=first, stop=not first)
                last.then_inc(s_mxf, 1)

            def key_scores0(i, p, n):
                b = p % 3
                j, k = divmod(n, NT)
                m = 8 * p + n
                q0 = min(P * k, T - 2 * P)
                if n == 0:
                    pe.wait_ge(s_mdma[p % 2], i * (16 * NPAIR) + 32 * (p // 2 + 1))
                if m >= 2:
                    pe.wait_ge(s_exp, i * MXN + m - 1)
                for x, y_, rows, first in ((KA, QA, P, True), (KB, QB, ROW_MAX + 2, False)):
                    last = pe.matmul(stp[m % 2][:, 0:T - q0], x[0:rows, b, j, P * k:P * (k + 1)],
                                     y_[0:rows, b, j, q0:T], start=first, stop=False, skip_group_check=True)
                c0 = P * k - q0
                last = pe.matmul(stp[m % 2][:, c0:c0 + P], identb[:, :], causalb[:, :], start=False, stop=True,
                                 skip_group_check=True)
                last.then_inc(s_st, 1)

            def pv0(i, p):
                pe.wait_ge(s_exp, i * MXN + 8 * p + 8)
                if p >= 2:
                    pe.wait_ge(s_att, i * NPAIR + p - 1)
                for k in range(NT):
                    for j in range(2):
                        base = (2 * (p % 2) + j) * PT0 + OFFS[k]
                        last = pe.matmul(op[p % 2][DH * j:DH * (j + 1), P * k:T], v0[:, k, DH * (2 * p + j):DH * (2 * p + j + 1)],
                                         pt[:, base:base + WIDTH[k]], start=k == 0, stop=k == NT - 1)
                last.then_inc(s_pv, 1)

            def pv1(i, g, k):
                pe.wait_ge(s_exp, i * MXN + L0N + GS * (NT * g + k) + GS)
                if k == 0 and g >= 2:
                    pe.wait_ge(s_or, i * NG + g - 1)
                for j in range(GS):
                    last = pe.matmul(op[g % 2][32 * j:32 * (j + 1), :], v1[:, k, (GS * g + j) // 2, :],
                                     pt[:, (GS * (k % 2) + j) * T:(GS * (k % 2) + j + 1) * T], start=k == 0, stop=k == NT - 1)
                last.then_inc(s_pv1, 1)

            def entry_pe(i):
                pe.wait_ge(s_lnv, before(i, 0, 24) + 12)
                transpose4(i, "xnT0", lambda k: xn0[:, k, :])
                pe.wait_ge(s_lnv, before(i, 0, 24) + 24)
                transpose4(i, "hT0", lambda k: hn0[:, k, :])
                b, n = entry(i, "xnT0")
                pe.wait_ge(s_pje[b], n)
                project_qk(i, 0)
                for n in range(2 * NT):
                    project(i, f"v{n}", lambda k: xnT[:, P * (n // 2):P * (n // 2 + 1)],
                            lambda k: wqkv[:, 2 * INNER + T * (n % 2):2 * INNER + T * (n % 2 + 1)], 1)

            entry_pe(None)
            for f in range(NF):
                ffn_first(None, 0, f)
            ffn_second(None, 0)
            assert used == ENTRY_ALL
            with pe.Fori(0, NB) as i:
                used.clear()
                for s in range(NPAIR + 2):
                    if 1 <= s <= NPAIR:
                        pe.wait_ge(s_mxd, i * MXN + 8 * s)
                        t, full = bank(i, f"m{s - 1}")
                        pe.transpose(t[0:8, 0:P], mx[:, (s - 1) % 2, 0:8], ident[:, :]).then_inc(full, 1)
                    if s + 1 < NPAIR:
                        project_qk(i, s + 1)
                    if s >= 2:
                        pv0(i, s - 2)
                    for n in range(8):
                        if s < NPAIR:
                            max_scores0(i, s, n)
                        if 1 <= s <= NPAIR:
                            key_scores0(i, s - 1, n)
                    if s >= 3 and s % 2 == 1:
                        g = (s - 3) // 2
                        t, full = bank(i, f"l{g}")
                        pe.wait_ge(s_psum, i * L0N + 16 * (g + 1))
                        for c in range(4):
                            last = pe.matmul(t[32 * c:32 * (c + 1), :], ones[:, :], psums[:, c, :], start=True, stop=True)
                        last.then_inc(full, 1)
                entry_pe(i)
                t, full = bank(i, "wo0")
                for p in range(NPAIR):
                    pe.wait_ge(s_nrm, i * NPAIR + p + 1)
                    for k in range(NT):
                        last = pe.matmul(t[:, D * k:D * (k + 1)], att[:, p, P * k:P * (k + 1)], wout[:, p, :],
                                         start=p == 0 and k == 0, stop=p == NPAIR - 1, skip_group_check=True)
                last.then_inc(full, 1)
                pe.wait_ge(s_lnv, before(i, 1, 24) + 12)
                transpose4(i, "xnT1", lambda k: xn1[:, k, :])
                b, u = pjn("xnT1")
                pe.wait_ge(s_pje[b], i * PB + u)
                for c, name in enumerate(("rq", "rqs", "rk", "rks")):
                    project(i, name, lambda k: w_l1[:, c, :], lambda k: xnT1[:, :], 1)
                project(i, "vals", lambda k: xnT1[:, P * k:P * (k + 1)], lambda k: w_l1[:, 4, :], NT)
                pe.wait_ge(s_lnv, before(i, 1, 24) + 24)
                transpose4(i, "hT1", lambda k: hn1[:, k, :])
                for f in range(NF):
                    ffn_first(i, 1, f)
                ffn_second(i, 1)
                b, u = pjn("vals")
                pe.wait_ge(s_pje[b], i * PB + u)
                pe.wait_ge(s_stk, i * NSTK + NSTK)
                for t in range(L1_STEPS):
                    if (g := l1_rows(t)) is not None:
                        pe.wait_ge(s_mxd, i * MXN + L0N + GU * (g + 1))
                        rows, full = bank(i, f"n{g}")
                        pe.transpose(rows[0:16, 0:P], mx[:, g % 2, 0:16], ident[:, :]).then_inc(full, 1)
                    if (g := l1_heads(t, OUT_AT)) is not None:
                        pe.wait_ge(s_or, i * NG + g + 1)
                        transpose4(i, f"o{g}", lambda k: oraw[:, g % 2, P * k:P * (k + 1)])
                    if t < NU:
                        j, q = divmod(t, NT)
                        m = L0N + t
                        pe.wait_ge(s_mxd, i * MXN + m - 1)
                        pe.matmul(mxp[m % 2][:, :], QS[0:ROW_MAX, j, P * q:P * (q + 1)],
                                  KS[0:ROW_MAX, j, :], start=True, stop=True).then_inc(s_mxf, 1)
                    if (n := t - KEY_LAG) >= 0:
                        g, r = divmod(n, GU)
                        k, j = divmod(r, GS)
                        if r == 0:
                            pe.wait_ge(s_nd[g % 2], i * 96 + 48 * (g // 2 + 1))
                        pe.wait_ge(s_exp, i * MXN + L0N + n - 1)
                        pe.matmul(stp[n % 2][:, :], KS[0:ROW_MAX + 3, GS * g + j, P * k:P * (k + 1)],
                                  QS[0:ROW_MAX + 3, GS * g + j, :], start=True, stop=True).then_inc(s_st, 1)
                        if j == GS - 1 and n >= GS:
                            pv1(i, *divmod(n // GS - 1, NT))
                ffn_first(i, 0, 0)
                pv1(i, NG - 1, NT - 1)
                ffn_first(i, 0, 1)
                pe.wait_ge(s_or, i * NG + NG)
                transpose4(i, f"o{NG - 1}", lambda k: oraw[:, (NG - 1) % 2, P * k:P * (k + 1)])
                ffn_first(i, 0, 2)
                ffn_first(i, 0, 3)
                pe.wait_ge(s_tl, i * 7 * NG + 7 * NG)
                transpose4(i, "oT", lambda k: o1[:, k, :])
                ffn_second(i, 0)
                b, u = pjn("oT")
                pe.wait_ge(s_pje[b], i * PB + u)
                project(i, "wo1", lambda k: o1T[:, P * k:P * (k + 1)], lambda k: w_l1[:, 5, :], NT)
                assert used == pj_order()


def kernel(**inputs):
    import concourse.bacc as bacc
    from concourse.bass_utils import run_bass_kernel_spmd

    nc = bacc.Bacc("TRN2", target_bir_lowering=False, num_devices=1)
    data = {k: np.ascontiguousarray(v) for k, v in inputs.items()}
    swap = np.arange(D) ^ 1
    for n in "qkvo":
        w = data.pop(f"L1_attn_W{n}")
        data[f"t_W{n}T"] = np.ascontiguousarray(w.T)
        if n in "qk":
            data[f"t_W{n}sT"] = np.ascontiguousarray(w[swap].T)
    data.update(tables())
    arrays, a = {}, {}
    for name, v in data.items():
        arrays[f"in_{name}"] = v
        a[name] = nc.dram_tensor(f"in_{name}", v.shape, mybir.dt.from_np(v.dtype), kind="ExternalInput").ap()
    out = nc.dram_tensor("out_x", (NB, T, D), F32, kind="ExternalOutput").ap()
    build_program(nc, a, out)
    r = run_bass_kernel_spmd(nc, [arrays], core_ids=[0])
    return r.results[0]["out_x"]
```

```python
import math
from contextlib import ExitStack

import numpy as np
import concourse.bass as bass
from concourse import mybir

F32 = mybir.dt.float32
F32R = mybir.dt.float32r
BF16 = mybir.dt.bfloat16
I32 = mybir.dt.int32
ACT = mybir.ActivationFunctionType
ALU = mybir.AluOpType
AXIS = mybir.AxisListType

NB = 16
T = 512
D = 128
P = 128
NT = T // P
FF = 512
NF = FF // P
H0, DH = 16, 64
NPAIR = H0 // 2
INNER = H0 * DH
H1, DS = 8, 8
NS = 2 * H1
DV = 2 * DS
NG = 4
GS = NS // NG
LN_EPS = 1e-5
RMS_EPS = 1e-8
LAMBDA_INIT = 0.8 - 0.6 * math.exp(-0.3 * 12)
SLOPES = [2.0 ** (-0.5 * (h + 1)) for h in range(H0)]
MASKED = -3.0e38

WIDTH = [T - P * k for k in range(NT)]
OFFS = [sum(WIDTH[:k]) for k in range(NT)]
PT0 = sum(WIDTH)

ROW_KEY = 64
ROW_MAX = 96


def tables():
    half = np.arange(0, DS, 2, dtype=np.float32) / np.float32(DS)
    inv_freq = (np.float32(1.0) / np.power(np.float32(10000.0), half)).astype(np.float32)
    freqs = (np.arange(T, dtype=np.float32)[:, None] * inv_freq[None, :]).astype(np.float32)
    freqs = np.repeat(freqs, 2, axis=-1).astype(np.float64)
    sign = np.where(np.arange(DS) % 2 == 0, -1.0, 1.0)
    cos = np.cos(freqs).T
    sin = np.sin(freqs).T * sign[:, None]
    rope = np.stack([np.tile(cos, (NS, 1)), np.tile(sin, (NS, 1))], 1)
    causal = np.zeros((P, T), np.float32)
    q, k = np.arange(P)[:, None], np.arange(P)[None, :]
    causal[:, T - P:] = np.where(k > q, np.float32(MASKED), np.float32(0))
    qscale = np.zeros((P, NPAIR), np.float32)
    for p in range(NPAIR):
        for j in range(2):
            qscale[DH * j:DH * (j + 1), p] = DH ** -0.5 / SLOPES[2 * p + j]
    return {
        "t_rope": rope.astype(np.float32),
        "t_causal": causal,
        "t_causalT": np.ascontiguousarray(causal[:, T - P:].T),
        "t_qscale": qscale,
        "t_key": np.arange(T, dtype=np.float32)[None, :],
        "t_ident": np.eye(P, dtype=np.float32),
    }


NU = NS * NT
GU = GS * NT
ROWS_AT = 2
KEY_LAG = GU + 10
HEADS_AT = GU + 2
OUT_AT = GU + 8
NORM_LAG = 6
PV_AT = 1
LN_AT = 0
HT_AT = 6
SPLIT_AT = NU + 5
MXB = 3
STB = 2


def l1_rows(t):
    g, r = divmod(t - ROWS_AT, GU)
    return g - 1 if r == 0 and 1 <= g <= NG else None


def l1_heads(t, at, last=NG - 1):
    g, r = divmod(t - KEY_LAG - at, GU)
    return g if r == 0 and 0 <= g < last else None


L1_STEPS = NU + KEY_LAG

ENTRY_QK = ["xnT0", "hT0", "q0", "k0"]
ENTRY_V = [f"v{n}" for n in range(2 * NT)]
ENTRY_ALL = ENTRY_QK + ENTRY_V + [f"ya{f}" for f in range(NF)] + ["fa"]


HT0_AT, QK_AT = 3, 7
MAX_EARLY = 1
V_EARLY = 2


def pj_order():
    order = []
    for s in range(NPAIR + 2):
        if 1 <= s <= NPAIR:
            order.append(f"m{s - 1}")
        if s + 1 < NPAIR:
            order += [f"q{s + 1}", f"k{s + 1}"]
        if s == NPAIR:
            order += ENTRY_QK
        if s == NPAIR + 1:
            order += ENTRY_V[:V_EARLY]
        if s >= 2 and s % 2 == 1:
            order.append(f"l{(s - 3) // 2}")
    order += ENTRY_V[V_EARLY:] + ["wo0"] + [f"ya{f}" for f in range(NF)]
    order += ["xnT1", "rq", "rqs", "rk", "rks", "vals", "fa"]
    for t in range(L1_STEPS):
        if (g := l1_rows(t)) is not None:
            order.append(f"n{g}")
        if (g := l1_heads(t, OUT_AT)) is not None:
            order.append(f"o{g}")
        if t == HT_AT:
            order.append("hT1")
    order += ["yb0", "yb1", f"o{NG - 1}", "yb2", "yb3", "oT", "fb", "wo1"]
    return order


N_PSET = 7
N_VSET = 4
N_VPREP = 19
PJ = {name: n for n, name in enumerate(pj_order())}
PJ_USES = len(PJ)
PJ_ENTRY = {name: n for n, name in enumerate(ENTRY_ALL)}
assert PJ_USES % 2 == 0


def build_program(nc, a, out):
    ctx = ExitStack()
    with ctx:
        def sb(name, shape, dt=F32):
            return ctx.enter_context(nc.sbuf_tensor(name, shape, dt))

        def ps(name):
            return ctx.enter_context(nc.psum_tensor(name, [P, T], F32))

        def sem(name):
            return ctx.enter_context(nc.semaphore(name))

        ident = sb("ident", [P, P])
        causal = sb("causal", [P, T])
        rope = sb("rope", [P, 2, T])
        qscale = sb("qscale", [P, NPAIR])
        identb = sb("identb", [P, P], BF16)
        causalb = sb("causalb", [P, P], BF16)
        ones = sb("ones", [P, 32])
        minus_half = sb("minus_half", [P, 16])
        wqkv = sb("wqkv", [P, 3 * INNER])
        wout = sb("wout", [P, NPAIR, D])
        w1 = sb("w1", [P, 2, FF])
        w2 = sb("w2", [P, 2, NF * D])
        b1 = sb("b1", [P, 2, NF])
        b1h = sb("b1h", [P, 2, NF])
        gamma = sb("gamma", [P, 2])
        beta = sb("beta", [P, 2])
        bias = sb("bias", [P, 2, D])
        w_l1 = sb("w_l1", [P, 6, D])
        lam_in = sb("lam_in", [P, 4, DS])
        lam_pr = sb("lam_pr", [P, 2, DS])
        lam_s = sb("lam_s", [P, 2])
        lam_e = sb("lam_e", [P, 2])
        lam_d = sb("lam_d", [P, 1])
        neglam = sb("neglam", [P, 1])
        lnw_in = sb("lnw_in", [P, 2, DV])
        lnw = sb("lnw", [P, 2, DV])

        x_in = sb("x_in", [P, NT, D])
        xacc = sb("xacc", [P, NT, D])
        xb = sb("xb", [P, NT, D])
        stats = sb("stats", [P, 2, NT, 6])
        mv = sb("mv", [P, 2, NT, 2])
        veps = sb("veps", [P, 2, NT])
        rstd = sb("rstd", [P, 2, NT])
        xnT = sb("xnT", [P, T])
        v0 = sb("v0", [P, NT, INNER])
        rawq = sb("rawq", [P, T])
        rawk = sb("rawk", [P, T])
        QA = sb("QA", [P, 3, 2, T], F32R)
        KA = sb("KA", [P, 3, 2, T], F32R)
        QB = sb("QB", [P, 3, 2, T], F32R)
        KB = sb("KB", [P, 3, 2, T], F32R)
        junk = sb("junk", [P, 2, T], BF16)
        mx = sb("mx", [P, 2, 16])
        mrow = sb("mrow", [16, 2, P], F32R)
        pt = sb("pt", [P, 4 * PT0])
        psums = sb("psums", [P, 4, T])
        tanh = psums[:, 0:2, :]
        xn1 = psums[:, 2, :].rearrange("p (t d) -> p t d", t=NT)
        hn1 = psums[:, 3, :].rearrange("p (t d) -> p t d", t=NT)
        xn0 = rawq[:, :].rearrange("p (t d) -> p t d", t=NT)
        hn0 = rawk[:, :].rearrange("p (t d) -> p t d", t=NT)
        hT0 = sb("hT0", [P, T])
        xnT1 = sb("xnT1", [P, T])
        hT = [hT0, xnT1]
        lsb = xnT1
        lcol = sb("lcol", [P, 16])
        rcol = sb("rcol", [P, 16])
        rbc = sb("rbc", [P, 2, T])
        big = sb("big", [P, NPAIR * T])
        keyrow = big[ROW_KEY:ROW_KEY + 1, 3 * INNER:3 * INNER + T]
        y = big[:, 0:NF * T].rearrange("p (f t) -> p f t", f=NF)
        att = big[:, :].rearrange("p (h t) -> p h t", h=NPAIR)
        rope_a, rope_b, rot, rest = (big[:, T * c:T * (c + 1)] for c in range(NF, 2 * NF))
        rbch = rbc[:, :, :].rearrange("p b t -> p (b t)").bitcast(BF16)
        parts = [[rbch[:, T * c:T * (c + 1)] for c in range(3)], [rbch[:, 3 * T:4 * T], junk[:, 0, :], junk[:, 1, :]]]
        oraw = big[:, 4 * T:6 * T].rearrange("p (b t) -> p b t", b=2)
        o1 = big[:, 6 * T:7 * T].rearrange("p (t d) -> p t d", t=NT)
        o1T = big[:, 7 * T:8 * T]
        QS = sb("QS", [P, NS, T], BF16)
        KS = sb("KS", [P, NS, T], BF16)
        nrow = sb("nrow", [16, 3, P], BF16)
        nrest = sb("nrest", [16, P])
        v1 = sb("v1", [P, NT, H1, 32])
        rinv = sb("rinv", [P, NT, GS, 1])
        onrm = sb("onrm", [P, NT, GS, DV])
        dif = sb("dif", [P, NT, 2, DV])
        sq = sb("sq", [P, NT, 2, DV])
        ms = sb("ms", [P, NT, 2, 1])
        mse = sb("mse", [P, NT, 2, 1])
        rms = sb("rms", [P, NT, 2, 1])
        od = sq
        ow = sb("ow", [P, NT, 2, DV])

        pj = [ps("pj0"), ps("pj1")]
        mxp = [ps(f"mx{n}") for n in range(MXB)]
        stp = [ps(f"st{n}") for n in range(STB)]
        op = ps("op")

        scr_r = nc.dram_tensor("scr_r", (NPAIR // 2, P, 16), F32).ap()
        scr_p = nc.dram_tensor("scr_p", (2, 3, DS, NS, T), BF16).ap()

        s_ld = sem("weights_loaded")
        s_pset = sem("pool_constants")
        s_vset = sem("vector_constants")
        s_vprep = sem("vector_prepared")
        s_aprep = sem("act_prepared")
        s_x = sem("x_loaded")
        s_lnv = sem("ln_vector_steps")
        s_lnp = sem("ln_pool_steps")
        s_pjf = [sem("pj0_full"), sem("pj1_full")]
        s_pje = [sem("pj0_free"), sem("pj1_free")]
        s_tanh = sem("tanh_done")
        s_y = sem("ffn_hidden_ready")
        s_res = sem("residual1_steps")
        s_rx = sem("residual0_steps")
        s_spa = sem("act_split")
        s_spv = sem("vector_split")
        s_mxf = sem("max_scores_ready")
        s_mxd = sem("row_max_done")
        s_mhi = sem("minus_max_high")
        s_mdma = [sem("max_rows_stored0"), sem("max_rows_stored1")]
        s_st = sem("key_scores_ready")
        s_exp = sem("exp_done")
        s_psum = sem("probs_added")
        s_psv = sem("probs_added_last_head")
        s_pv = sem("pv_done")
        s_pv1 = sem("pv1_tile_done")
        s_att = sem("attention_copied")
        s_ldma = sem("sums_spread")
        s_rc = sem("sums_inverted")
        s_rst = sem("inverse_stored")
        s_rb = sem("inverse_broadcast")
        s_nrm = sem("attention_normalised")
        s_nrmv = sem("last_pair_normalised")
        s_rot = sem("rope_steps")
        s_part = sem("parts_ready")
        s_pst = sem("parts_stored")
        s_psl = sem("last_part_stored")
        s_stk = sem("stacks_filled")
        s_nth = sem("minus_max1_high")
        s_nt = sem("minus_max1_rest")
        s_nd = [sem("max1_rows_stored0"), sem("max1_rows_stored1")]
        s_or = sem("heads_copied")
        s_tl = sem("head_norm_steps")
        s_tlp = sem("head_norm_pool_steps")
        s_out = sem("result_stored")

        def pjn(name):
            n = len(ENTRY_ALL) + PJ[name]
            return n % 2, n // 2 + 1

        def entry(i, name):
            if i is None:
                return PJ_ENTRY[name] % 2, PJ_ENTRY[name] // 2 + 1
            b, u = pjn(name)
            return b, i * PB + u

        def before(i, l, n):
            if i is None:
                return 0
            return i * (2 * n) + n * (l + 1)

        def sequence(i):
            return 0 if i is None else i + 1

        PB = PJ_USES // 2
        HP = NPAIR // 2
        MXN = 8 * NPAIR + NS * NT
        L0N = 8 * NPAIR
        PSN = L0N - NT
        NSTK = 16 * 7
        stage = {}
        for n in range(4):
            stage[n] = (v0[:, n, 0:FF], v0[:, n, FF:2 * FF])
        b2_in = big[:, 4 * FF:4 * FF + 2 * D].rearrange("p (l d) -> p l d", l=2)
        bo_in = big[:, 4 * FF + 2 * D:4 * FF + 3 * D]

        causal_in = big[:, 3 * INNER + T:3 * INNER + T + P]
        loads = [
            (causal_in, a["t_causalT"]), (ident[:, :], a["t_ident"]), (causal[:, :], a["t_causal"]), (rope[:, :, :], a["t_rope"]),
            (qscale[:, :], a["t_qscale"]), (keyrow, a["t_key"]),
            (wqkv[:, :], a["L0_attn_w_qkv"]),
            (wout[:, :, :], a["L0_attn_w_out"].rearrange("(h p) d -> p h d", p=P)),
            (bo_in, a["L0_attn_b_out"].partition_broadcast(P)),
            (w_l1[:, 0, :], a["t_WqT"]), (w_l1[:, 1, :], a["t_WqsT"]), (w_l1[:, 2, :], a["t_WkT"]),
            (w_l1[:, 3, :], a["t_WksT"]), (w_l1[:, 4, :], a["t_WvT"]), (w_l1[:, 5, :], a["t_WoT"]),
            (lnw_in[:, 0, :], a["L1_attn_ln_w"].partition_broadcast(P)),
            (lnw_in[:, 1, :], a["L1_attn_ln_b"].partition_broadcast(P)),
        ]
        for n, v in enumerate(("q1", "k1", "q2", "k2")):
            loads.append((lam_in[:, n, :], a[f"L1_attn_lambda_{v}"].partition_broadcast(P)))
        for l in range(2):
            f = f"L{l}_ffn_"
            loads += [
                (b1[:, l, :], a[f + "fc1_bias"].rearrange("(f p) -> p f", p=P)),
                (gamma[:, l:l + 1], a[f + "ln_gamma"].rearrange("(p o) -> p o", o=1)),
                (beta[:, l:l + 1], a[f + "ln_beta"].rearrange("(p o) -> p o", o=1)),
                (b2_in[:, l, :], a[f + "fc2_bias"].partition_broadcast(P)),
                (stage[2 * l][0].bitcast(I32), a[f + "fc1_q"]),
                (stage[2 * l][1], a[f + "fc1_scales"].rearrange("g n -> (g n)").partition_broadcast(P)),
                (stage[2 * l + 1][0].rearrange("p (f d) -> p f d", f=NF).bitcast(I32),
                 a[f + "fc2_q"].rearrange("(f p) d -> p f d", p=P)),
                (stage[2 * l + 1][1], a[f + "fc2_scales"].rearrange("g n -> (g n)").partition_broadcast(P)),
            ]
        NLOAD = 16 * len(loads)

        block = ctx.enter_context(nc.Block())

        @block.sync
        def _(sp):
            x_v = a["L0_attn_x"].rearrange("b (t p) d -> b p t d", p=P)
            out_v = out.rearrange("b (t p) d -> b p t d", p=P)
            with nc.allow_non_contiguous_dma(reason="a few hundred biases and gains, once"):
                for dst, src in loads:
                    sp.dma_start(dst, src).then_inc(s_ld, 16)
            sp.dma_start(x_in[:, :, :], x_v[0]).then_inc(s_x, 16)

            b, n = entry(None, "fa")
            sp.wait_ge(s_pje[b], n)
            sp.dma_start(x_in[:, :, :], x_v[1 % NB]).then_inc(s_x, 16)

            def inverse(i, g):
                sp.wait_ge(s_rc, i * HP + g + 1)
                sp.dma_start(scr_r[g], rcol[:, :]).then_inc(s_rst, 16)
                inverse_stored = sp.to_reg(i * (16 * HP) + 16 * (g + 1))
                rbc_used = sp.to_reg(i * (NPAIR - 1) + 2 * g) if g else 0
                sp.wait_ge(s_ld, NLOAD)
                sp.wait_ge(s_rst, inverse_stored)
                v = scr_r[g].rearrange("(p j c) e -> j p (c e)", p=2, j=2)
                if g:
                    sp.wait_ge(s_nrm, rbc_used)
                for j in range(2):
                    sp.dma_start(rbc[DH * j:DH * (j + 1), :, :], v[j:j + 1].broadcast_to([DH, 2, T])).then_inc(s_rb, 16)

            def stack(w, slot, c, n):
                src = scr_p[w].rearrange("c d s t -> c d (s t)")
                src = src[c:c + 1].broadcast_to([n, DS, NS * T]) if w == 0 else src[c:c + n]
                dst = (QS, KS)[w][DS * slot:DS * (slot + n), :, :]
                sp.dma_start(dst.rearrange("r s t -> r (s t)"), src).then_inc(s_stk, 16)

            with sp.Fori(0, NB) as i:
                for s in range(NPAIR + 2):
                    if 1 <= s <= NPAIR:
                        p = s - 1
                        b, u = pjn(f"m{p}")
                        sp.wait_ge(s_pje[b], i * PB + u)
                        for r in range(2):
                            row = QB[ROW_MAX + r:ROW_MAX + r + 1, p % 3, :, :]
                            sp.dma_start(row.bitcast(F32).rearrange("o j (c f) -> o (j c) f", f=P),
                                         mrow[0:8, r, :].bitcast(F32)).then_inc(s_mdma[p % 2], 16)
                    if s >= 4 and s % 2 == 0:
                        inverse(i, (s - 4) // 2)
                    if s >= 3 and s % 2 == 1:
                        b, u = pjn(f"l{(s - 3) // 2}")
                        sp.wait_ge(s_pje[b], i * PB + u)
                        sp.dma_start(lcol[:, :], lsb[0:P:32, :].rearrange("h (c e) -> h c e", e=16)).then_inc(s_ldma, 16)
                inverse(i, HP - 1)
                for w in range(2):
                    for c in range(3):
                        sp.wait_ge(s_part, i * 6 + 3 * w + c + 1)
                        stored = s_pst if (w, c) != (1, 2) else s_psl
                        sp.dma_start(scr_p[w, c].rearrange("d s t -> s d t"), parts[w][c]).then_inc(stored, 16)
                    sp.wait_ge(s_pst, i * 80 + (48, 80)[w])
                    for slot, c, n in ((0, 0, 3), (3, 1, 2), (5, 2, 1)) if w == 0 else ((0, 0, 2), (3, 0, 2), (5, 0, 1)):
                        stack(w, slot, c, n)
                sp.wait_ge(s_psl, i * 16 + 16)
                stack(1, 2, 2, 1)
                for g in range(NG):
                    sp.wait_ge(s_nt, i * 2 * NG + 2 * g + 2)
                    for r in range(3):
                        row = QS[ROW_MAX + r:ROW_MAX + r + 1, GS * g:GS * (g + 1), :]
                        sp.dma_start(row.rearrange("o s (c f) -> o (s c) f", f=P), nrow[:, r, :]).then_inc(s_nd[g % 2], 16)
                x_after = sp.snap((i + 2) % NB)
                b, u = pjn("fa")
                x_used = sp.to_reg(i * PB + u)
                sp.wait_ge(s_ld, NLOAD)
                sp.wait_ge(s_pje[b], x_used)
                sp.dma_start(x_in[:, :, :], x_v[bass.ds(x_after, 1)].rearrange("b p t d -> p (b t) d")).then_inc(s_x, 16)
                b, u = pjn("wo1")
                sp.wait_ge(s_pje[b], i * PB + u)
                sp.dma_start(out_v[bass.ds(i, 1)].rearrange("b p t d -> p (b t) d"), xacc[:, :, :]).then_inc(s_out, 16)
                stored = sp.to_reg(i * 16 + 16)
                sp.wait_ge(s_ld, NLOAD)
                sp.wait_ge(s_out, stored)
            sp.wait_ge(s_x, 16 * NB + 32)

        @block.gpsimd
        def _(pool):
            pool.memset(ones[:, :], 1.0).then_inc(s_pset, 1)
            pool.memset(minus_half[:, :], -0.5).then_inc(s_pset, 1)
            pool.memset(v1[:, :, :, :], 0.0).then_inc(s_pset, 1)
            pool.memset(QS[:, :, :], 0.0).then_inc(s_pset, 1)
            pool.memset(KS[:, :, :], 0.0).then_inc(s_pset, 1)
            pool.wait_ge(s_pset, 5)
            pool.memset(v1[:, :, :, DV:DV + 1], 1.0).then_inc(s_pset, 1)
            pool.wait_ge(s_pset, 6)
            pool.memset(KS[ROW_MAX:ROW_MAX + 3, :, :], 1.0).then_inc(s_pset, 1)
            pool.wait_ge(s_pset, N_PSET)
            pool.wait_ge(s_vprep, N_VPREP)

            def ln_scale(i, l, part):
                n = before(i, l, 4) + 2 * part
                mv_there = before(i, l, 24) + (8 if part == 0 else 20)
                mv_there = mv_there if i is None else pool.to_reg(mv_there)
                pool.wait_ge(s_pset, N_PSET)
                pool.wait_ge(s_lnv, mv_there)
                pool.tensor_scalar(veps[:, part, :], mv[:, part, :, 1], 1.0, LN_EPS, ALU.mult, ALU.add).then_inc(s_lnp, 1)
                pool.wait_ge(s_lnp, n + 1)
                pool.tensor_tensor(rstd[:, part, :], veps[:, part, :], minus_half[:, 0:NT], ALU.pow).then_inc(s_lnp, 1)

            def residual1(i):
                pool.wait_ge(s_lnv, before(i, 1, 24) + 12)
                pool.tensor_tensor(xacc[:, :, :], xacc[:, :, :], xn1, ALU.add).then_inc(s_res, 1)
                pool.wait_ge(s_res, i * 2 + 1)
                pool.tensor_tensor(xacc[:, :, :], xacc[:, :, :], bias[:, 1:2, :].broadcast_to([P, NT, D]), ALU.add).then_inc(s_res, 1)

            def normalise(i, p):
                pool.wait_ge(s_rb, i * (32 * HP) + 32 * (p // 2 + 1))
                pool.wait_ge(s_att, i * NPAIR + p + 1)
                pool.tensor_tensor(att[:, p, :], att[:, p, :], rbc[:, p % 2, :], ALU.mult).then_inc(s_nrm, 1)

            ln_scale(None, 0, 0)
            ln_scale(None, 0, 1)
            with pool.Fori(0, NB) as i:
                for s in range(1, NPAIR + 2):
                    if s == 3:
                        ln_scale(i, 0, 0)
                    if s <= NPAIR:
                        p = s - 1
                        if p >= 2 and p % 2 == 0:
                            b, u = pjn(f"l{p // 2 - 1}")
                            pool.wait_ge(s_pjf[b], i * PB + u)
                        for j in range(2 if p < NPAIR - 1 else 1):
                            base = (2 * (p % 2) + j) * PT0
                            c = (2 * p + j) % 4
                            for k in range(NT):
                                n = 8 * p + 4 * j + k
                                tile = pt[:, base + OFFS[k]:base + OFFS[k] + WIDTH[k]]
                                tile_there = pool.to_reg(i * MXN + n + 1)
                                if k == 0:
                                    pool.wait_ge(s_pset, N_PSET)
                                pool.wait_ge(s_exp, tile_there)
                                if k == 0:
                                    pool.tensor_copy(psums[:, c, 0:P], tile[:, 0:P]).then_inc(s_psum, 1)
                                    continue
                                so_far = pt[:, base + P:base + T] if k == 1 else psums[:, c, P * k:T]
                                pool.wait_ge(s_psum, i * PSN + n)
                                pool.tensor_tensor(psums[:, c, P * k:T], so_far, tile, ALU.add).then_inc(s_psum, 1)
                                if p == NPAIR - 2 and (j, k) == (0, NT - 1):
                                    ln_scale(i, 0, 1)
                    if s >= 5 and s % 2 == 1:
                        normalise(i, s - 5)
                        normalise(i, s - 4)
                normalise(i, NPAIR - 2)
                ln_scale(i, 1, 0)
                residual1(i)
                ln_scale(i, 1, 1)
                for g in range(NG):
                    ms_there = pool.to_reg(i * 7 * NG + 7 * g + 4)
                    pool.wait_ge(s_pset, N_PSET)
                    pool.wait_ge(s_tl, ms_there)
                    pool.tensor_scalar(mse[:, :, :, :], ms[:, :, :, :], 1.0 / DV, RMS_EPS, ALU.mult, ALU.add).then_inc(s_tlp, 1)
                    pool.wait_ge(s_tlp, i * 2 * NG + 2 * g + 1)
                    pool.tensor_tensor(rms[:, :, :, 0].rearrange("p t h -> p (t h)"), mse[:, :, :, 0].rearrange("p t h -> p (t h)"),
                                       minus_half[:, 0:2 * NT], ALU.pow).then_inc(s_tlp, 1)

        @block.scalar
        def _(act):
            act.wait_ge(s_ld, NLOAD)
            act.wait_ge(s_vset, N_VSET)
            for n in range(6):
                act.activation(KB[ROW_KEY:ROW_KEY + 1, n // 2, n % 2, :], keyrow, ACT.Copy).then_inc(s_aprep, 1)
            act.activation(b1h[:, :, :], b1[:, :, :], ACT.Copy, scale=0.5).then_inc(s_aprep, 1)
            act.wait_ge(s_vprep, 2)
            act.activation(lam_e[:, :], lam_s[:, :], ACT.Exp).then_inc(s_aprep, 1)
            act.wait_ge(s_aprep, 8)
            act.wait_ge(s_pset, N_PSET)

            def transposed(b, n, l, name):
                act.wait_ge(s_pjf[b], n)
                if name == "h":
                    act.activation(hT[l][:, :], pj[b][:, :], ACT.Identity, scale=gamma[:, l:l + 1],
                                   bias=beta[:, l:l + 1]).then_inc(s_pje[b], 1)
                else:
                    act.activation((xnT, xnT1)[l][:, :], pj[b][:, :], ACT.Copy).then_inc(s_pje[b], 1)

            def ffn_act(i, l, f):
                b, n = entry(i, f"y{'ab'[l]}{f}")
                act.wait_ge(s_pjf[b], n)
                if f >= 2:
                    act.wait_ge(s_y, before(i, l, NF) + f - 1)
                act.activation(tanh[:, f % 2, :], pj[b][:, :], ACT.Tanh, scale=0.5,
                               bias=b1h[:, l, f:f + 1]).then_inc(s_tanh, 1)
                act.activation(y[:, f, :], pj[b][:, :], ACT.Identity, bias=b1[:, l, f:f + 1]).then_inc(s_pje[b], 1)

            def values(i, lo, hi):
                for n in range(lo, hi):
                    b, m = entry(i, f"v{n}")
                    act.wait_ge(s_pjf[b], m)
                    act.activation(v0[:, n // 2, T * (n % 2):T * (n % 2 + 1)], pj[b][:, :], ACT.Copy).then_inc(s_pje[b], 1)

            def split(p, seq, q_use, k_use, st_before):
                b = p % 3
                bq, nq = q_use
                bk, nk = k_use
                if p:
                    act.wait_ge(s_spv, seq * L0N + 8 * p)
                    act.wait_ge(s_spa, seq * (4 * NPAIR) + 4 * p)
                act.wait_ge(s_pjf[bq], nq)
                act.activation(rawq[:, :], pj[bq][:, :], ACT.Copy, scale=qscale[:, p:p + 1]).then_inc(s_pje[bq], 1)
                act.wait_ge(s_pjf[bk], nk)
                act.activation(rawk[:, :], pj[bk][:, :], ACT.Copy).then_inc(s_pje[bk], 1)
                if st_before is not None:
                    act.wait_ge(s_st, st_before)
                act.wait_ge(s_pje[bq], nq)
                for j in range(2):
                    act.activation(QB[0:DH, b, j, :], rawq[DH * j:DH * (j + 1), :], ACT.Copy).then_inc(s_spa, 1)
                act.wait_ge(s_pje[bk], nk)
                for j in range(2):
                    act.activation(KA[DH * (1 - j):DH * (2 - j), b, j, :], rawk[DH * j:DH * (j + 1), :],
                                   ACT.Copy).then_inc(s_spa, 1)

            def split_in_loop(i, p):
                split(p, i, entry(i, f"q{p}"), entry(i, f"k{p}"), i * MXN + 8 * (p - 2) if p >= 3 else None)

            def entry_transposed(i, part):
                transposed(*entry(i, ("xnT0", "hT0")[part]), 0, "xh"[part])

            def entry_split(i):
                act.wait_ge(s_rx, 2 if i is None else i * 2 + 4)
                split(0, sequence(i), entry(i, "q0"), entry(i, "k0"), None if i is None else i * MXN + 8 * (NPAIR - 1))

            def copy_heads(i, g):
                act.wait_ge(s_pv1, i * NG * NT + NT * (g + 1))
                act.activation(oraw[:, g % 2, :], op[:, :], ACT.Copy).then_inc(s_or, 1)

            entry_transposed(None, 0)
            entry_transposed(None, 1)
            entry_split(None)
            values(None, 0, 2 * NT)
            for f in range(NF):
                ffn_act(None, 0, f)
            with act.Fori(0, NB) as i:
                for s in range(NPAIR + 2):
                    if 1 <= s <= NPAIR:
                        p = s - 1
                        b, u = pjn(f"m{p}")
                        act.wait_ge(s_pjf[b], i * PB + u)
                        if p:
                            act.wait_ge(s_mdma[(p - 1) % 2], i * (16 * NPAIR) + 32 * ((p - 1) // 2 + 1))
                        act.activation(mrow[0:8, 0, :], pj[b][0:8, 0:P], ACT.Copy, scale=-1.0).then_inc(s_mhi, 1)
                    if s + 1 < NPAIR:
                        split_in_loop(i, s + 1)
                    if s >= 2:
                        act.wait_ge(s_pv, i * NPAIR + s - 1)
                        act.activation(att[:, s - 2, :], op[:, :], ACT.Copy).then_inc(s_att, 1)
                    if s == NPAIR:
                        entry_transposed(i, 0)
                    if 1 <= s <= NPAIR:
                        p = s - 1
                        for j in range(2):
                            base = (2 * (p % 2) + j) * PT0
                            if p >= 2:
                                act.wait_ge(s_pv, i * NPAIR + p - 1)
                                act.wait_ge(s_psum, i * PSN + 8 * (p - 2) + 4 * (j + 1))
                            for k in range(NT):
                                n = 8 * p + 4 * j + k
                                act.wait_ge(s_st, i * MXN + n + 1)
                                c0 = P if k == NT - 1 else 0
                                act.activation(pt[:, base + OFFS[k]:base + OFFS[k] + WIDTH[k]],
                                               stp[n % STB][:, c0:c0 + WIDTH[k]], ACT.Exp,
                                               scale=SLOPES[2 * p + j]).then_inc(s_exp, 1)
                                if s == NPAIR and 4 * j + k == HT0_AT:
                                    entry_transposed(i, 1)
                                if s == NPAIR and 4 * j + k == QK_AT:
                                    entry_split(i)
                    if s == NPAIR + 1:
                        values(i, 0, V_EARLY)
                    if s >= 3 and s % 2 == 1:
                        g = (s - 3) // 2
                        b, u = pjn(f"l{g}")
                        act.wait_ge(s_pjf[b], i * PB + u)
                        if g:
                            act.wait_ge(s_ldma, i * (16 * HP) + 16 * g)
                        act.activation(lsb[:, :], pj[b][:, :], ACT.Copy).then_inc(s_pje[b], 1)
                values(i, V_EARLY, 2 * NT)
                for f in range(NF):
                    ffn_act(i, 0, f)
                act.wait_ge(s_ldma, i * (16 * HP) + 16 * HP)
                transposed(*entry(i, "xnT1"), 1, "x")
                b, u = pjn("vals")
                act.wait_ge(s_pjf[b], i * PB + u)
                act.activation(v1[:, :, :, 0:DV], pj[b][:, :].rearrange("p (t h e) -> p t h e", t=NT, h=H1),
                               ACT.Copy).then_inc(s_pje[b], 1)
                for t in range(L1_STEPS):
                    if (g := l1_rows(t)) is not None:
                        b, u = pjn(f"n{g}")
                        act.wait_ge(s_pjf[b], i * PB + u)
                        if g:
                            act.wait_ge(s_nd[(g - 1) % 2], i * 96 + 48 * ((g - 1) // 2 + 1))
                        act.activation(nrow[:, 0, :], pj[b][0:16, 0:P], ACT.Copy, scale=-1.0).then_inc(s_nth, 1)
                    if (g := l1_heads(t, HEADS_AT)) is not None:
                        copy_heads(i, g)
                    if (n := t - KEY_LAG) >= 0:
                        m, j = divmod(n, GS)
                        if m >= 2 and j == 0:
                            act.wait_ge(s_pv1, i * NG * NT + m - 1)
                        act.wait_ge(s_st, i * MXN + L0N + n + 1)
                        act.activation(pt[:, (GS * (m % 2) + j) * T:(GS * (m % 2) + j + 1) * T], stp[(L0N + n) % STB][:, :],
                                       ACT.Exp, scale=float(DS) ** -0.25).then_inc(s_exp, 1)
                    if t == HT_AT:
                        transposed(*entry(i, "hT1"), 1, "h")
                ffn_act(i, 1, 0)
                copy_heads(i, NG - 1)
                for f in range(1, NF):
                    ffn_act(i, 1, f)
                b, u = pjn("oT")
                act.wait_ge(s_pjf[b], i * PB + u)
                act.activation(o1T[:, :], pj[b][:, :], ACT.Copy).then_inc(s_pje[b], 1)

        @block.vector
        def _(dve):
            for t in (QB, KB):
                dve.memset(t[DH:P, :, :, :].bitcast(F32), 0.0).then_inc(s_vset, 1)
            dve.wait_ge(s_vset, 2)
            dve.memset(QB[ROW_KEY:ROW_KEY + 1, :, :, :].bitcast(F32), 1.0).then_inc(s_vset, 1)
            dve.memset(KB[ROW_MAX:ROW_MAX + 2, :, :, :].bitcast(F32), 1.0).then_inc(s_vset, 1)
            assert N_VSET == 4
            dve.wait_ge(s_ld, NLOAD)
            dve.tensor_tensor(lam_pr[:, :, :], lam_in[:, 0:4:2, :], lam_in[:, 1:4:2, :], ALU.mult).then_inc(s_vprep, 1)
            dve.wait_ge(s_vprep, 1)
            dve.reduce_sum(lam_s[:, :], lam_pr[:, :, :], AXIS.X).then_inc(s_vprep, 1)
            dve.wait_ge(s_aprep, 8)
            dve.tensor_tensor(lam_d[:, :], lam_e[:, 1:2], lam_e[:, 0:1], ALU.subtract).then_inc(s_vprep, 1)
            dve.wait_ge(s_vprep, 3)
            dve.tensor_scalar(neglam[:, :], lam_d[:, :], -LAMBDA_INIT, None, ALU.add).then_inc(s_vprep, 1)
            dve.tensor_scalar(lnw[:, :, :], lnw_in[:, :, :], 1.0 - LAMBDA_INIT, None, ALU.mult).then_inc(s_vprep, 1)
            n_prep = 5
            for n in range(4):
                l, second = divmod(n, 2)
                asf = big[:, FF * n:FF * (n + 1)]
                dst = (w2 if second else w1)[:, l, :]
                dve.tensor_copy(asf, stage[n][0].bitcast(I32)).then_inc(s_vprep, 1)
                dve.wait_ge(s_vprep, n_prep + 1)
                dve.scalar_tensor_tensor(out=dst, in0=asf, scalar=-128.0, in1=stage[n][1],
                                         op0=ALU.add, op1=ALU.mult).then_inc(s_vprep, 1)
                n_prep += 2
                if second:
                    dve.wait_ge(s_vprep, n_prep)
                    dve.tensor_scalar(dst, dst, 0.25, None, ALU.mult).then_inc(s_vprep, 1)
                    n_prep += 1
            dve.tensor_copy(identb[:, :], ident[:, :]).then_inc(s_vprep, 1)
            dve.tensor_copy(causalb[:, :], causal_in).then_inc(s_vprep, 1)
            n_prep += 2
            dve.tensor_scalar(bias[:, :, :], b2_in, 0.5, None, ALU.mult).then_inc(s_vprep, 1)
            n_prep += 1
            dve.wait_ge(s_vprep, n_prep)
            dve.tensor_tensor(bias[:, 0, :], bias[:, 0, :], bo_in, ALU.add).then_inc(s_vprep, 1)
            n_prep += 1
            assert n_prep == N_VPREP
            dve.wait_ge(s_vprep, n_prep)

            def ln_stats(i, l, part, inp):
                n = before(i, l, 24) + 12 * part
                for t in range(NT):
                    dve.bn_stats(stats[:, part, t, :], inp[:, t, :]).then_inc(s_lnv, 1)
                stats_there = n + 4 if i is None else dve.to_reg(n + 4)
                dve.wait_ge(s_vset, N_VSET)
                dve.wait_ge(s_lnv, stats_there)
                for t in range(NT):
                    dve.bn_aggr(mv[:, part, t, :], stats[:, part, t, :]).then_inc(s_lnv, 1)

            def ln_apply(i, l, part, inp, dst):
                n = before(i, l, 24) + 12 * part
                dve.wait_ge(s_lnv, n + 8)
                dve.wait_ge(s_lnp, before(i, l, 4) + 2 * part + 2)
                for t in range(NT):
                    dve.tensor_scalar(dst[:, t, :], inp[:, t, :], mv[:, part, t, 0:1], rstd[:, part, t:t + 1],
                                      ALU.subtract, ALU.mult).then_inc(s_lnv, 1)
                dve.wait_ge(s_lnv, n + 12)

            def layer_norm(i, l, part, inp, dst):
                ln_stats(i, l, part, inp)
                ln_apply(i, l, part, inp, dst)

            def add_last_head(i, k):
                base = (2 * ((NPAIR - 1) % 2) + 1) * PT0
                tile = pt[:, base + OFFS[k]:base + OFFS[k] + WIDTH[k]]
                c = (H0 - 1) % 4
                dve.wait_ge(s_exp, i * MXN + L0N - NT + k + 1)
                if k == 0:
                    b, n = entry(i, f"l{HP - 2}")
                    dve.wait_ge(s_pjf[b], n)
                    dve.tensor_copy(psums[:, c, 0:P], tile[:, 0:P]).then_inc(s_psv, 1)
                    return
                dve.wait_ge(s_psv, i * NT + k)
                so_far = pt[:, base + P:base + T] if k == 1 else psums[:, c, P * k:T]
                dve.tensor_tensor(psums[:, c, P * k:T], so_far, tile, ALU.add).then_inc(s_psv, 1)

            def ffn_dve(i, l, f):
                b, n = entry(i, f"y{'ab'[l]}{f}")
                dve.wait_ge(s_tanh, before(i, l, NF) + f + 1)
                dve.wait_ge(s_pje[b], n)
                dve.scalar_tensor_tensor(out=y[:, f, :], in0=tanh[:, f % 2, :], scalar=1.0, in1=y[:, f, :],
                                         op0=ALU.add, op1=ALU.mult).then_inc(s_y, 1)

            def ffn_end(i, l, dst, src):
                b, n = entry(i, "f" + "ab"[l])
                dve.wait_ge(s_pjf[b], n)
                if l == 0:
                    dve.wait_ge(s_rx, 2 * sequence(i) + 2)
                else:
                    dve.wait_ge(s_res, i * 2 + 2)
                dve.tensor_tensor(dst[:, :, :], pj[b][:, :].rearrange("p (t d) -> p t d", t=NT), src[:, :, :],
                                  ALU.add).then_inc(s_pje[b], 1)

            def residual0(i):
                dve.tensor_tensor(x_in[:, :, :], x_in[:, :, :], xn0, ALU.add).then_inc(s_rx, 1)
                dve.wait_ge(s_rx, 2 * sequence(i) + 1)
                dve.tensor_tensor(x_in[:, :, :], x_in[:, :, :], bias[:, 0:1, :].broadcast_to([P, NT, D]), ALU.add).then_inc(s_rx, 1)

            def split_high(p, q_use, k_use, st_before):
                b = p % 3
                if st_before is not None:
                    dve.wait_ge(s_st, st_before)
                for t, raw, (bb, n) in ((QA, rawq, q_use), (KA, rawk, k_use)):
                    dve.wait_ge(s_pje[bb], n)
                    for j in range(2):
                        r = slice(DH * j, DH * (j + 1))
                        dve.tensor_copy(t[r, b, j, :], raw[r, :]).then_inc(s_spv, 1)

            def split_low(seq, p, n):
                b = p % 3
                which, j = divmod(n, 2)
                r = slice(DH * j, DH * (j + 1))
                o = slice(DH * (1 - j), DH * (2 - j))
                dve.wait_ge(s_spv, seq * L0N + 8 * p + n + 1)
                if which == 0:
                    dve.tensor_tensor(QA[o, b, j, :], rawq[r, :], QA[r, b, j, :].bitcast(F32), ALU.subtract).then_inc(s_spv, 1)
                else:
                    dve.tensor_tensor(KB[0:DH, b, j, :], rawk[r, :], KA[r, b, j, :].bitcast(F32), ALU.subtract).then_inc(s_spv, 1)

            def entry_split(i):
                split_high(0, entry(i, "q0"), entry(i, "k0"), None if i is None else i * MXN + 8 * (NPAIR - 1))
                for n in range(4):
                    split_low(sequence(i), 0, n)

            def inverse_sums(i, g):
                dve.wait_ge(s_ldma, i * (16 * HP) + 16 * (g + 1))
                if g:
                    dve.wait_ge(s_rst, i * (16 * HP) + 16 * g)
                dve.reciprocal(rcol[:, :], lcol[:, :]).then_inc(s_rc, 1)

            def head_norm_a(i, g):
                b, u = pjn(f"o{g}")
                n = i * 7 * NG + 7 * g
                v = pj[b][:, :].rearrange("p (t j e) -> p t j e", t=NT, j=GS)
                dve.wait_ge(s_pjf[b], i * PB + u)
                dve.reciprocal(rinv[:, :, :, :], v[:, :, :, DV:DV + 1]).then_inc(s_tl, 1)
                dve.wait_ge(s_tl, n + 1)
                dve.tensor_tensor(onrm[:, :, :, :], v[:, :, :, 0:DV], rinv[:, :, :, :].broadcast_to([P, NT, GS, DV]),
                                  ALU.mult).then_inc(s_pje[b], 1)
                dve.wait_ge(s_pje[b], i * PB + u)
                dve.scalar_tensor_tensor(out=dif[:, :, :, :], in0=onrm[:, :, 1:GS:2, :], scalar=neglam[:, 0:1],
                                         in1=onrm[:, :, 0:GS:2, :], op0=ALU.mult, op1=ALU.add).then_inc(s_tl, 1)
                dve.wait_ge(s_tl, n + 2)
                dve.tensor_tensor(sq[:, :, :, :], dif[:, :, :, :], dif[:, :, :, :], ALU.mult).then_inc(s_tl, 1)
                dve.wait_ge(s_tl, n + 3)
                dve.reduce_sum(ms[:, :, :, 0], sq[:, :, :, :], AXIS.X).then_inc(s_tl, 1)

            def head_norm_b(i, g):
                n = i * 7 * NG + 7 * g
                dve.wait_ge(s_tlp, i * 2 * NG + 2 * g + 2)
                dve.tensor_tensor(od[:, :, :, :], dif[:, :, :, :], rms[:, :, :, :].broadcast_to([P, NT, 2, DV]),
                                  ALU.mult).then_inc(s_tl, 1)
                wide = lnw[:, :, :].rearrange("p (w a b) e -> p w a b e", a=1, b=1)
                dve.wait_ge(s_tl, n + 5)
                dve.tensor_tensor(ow[:, :, :, :], od[:, :, :, :], wide[:, 0].broadcast_to([P, NT, 2, DV]),
                                  ALU.mult).then_inc(s_tl, 1)
                dve.wait_ge(s_tl, n + 6)
                dve.tensor_tensor(o1[:, :, 2 * DV * g:2 * DV * (g + 1)].rearrange("p t (h e) -> p t h e", e=DV),
                                  ow[:, :, :, :], wide[:, 1].broadcast_to([P, NT, 2, DV]), ALU.add).then_inc(s_tl, 1)

            dve.wait_ge(s_x, 16)
            layer_norm(None, 0, 0, x_in, xn0)
            layer_norm(None, 0, 1, xn0, hn0)
            residual0(None)
            entry_split(None)
            for f in range(NF):
                ffn_dve(None, 0, f)
            ffn_end(None, 0, xb, x_in)
            with dve.Fori(0, NB) as i:
                for s in range(NPAIR + 2):
                    if 1 <= s <= NPAIR:
                        p = s - 1
                        b, u = pjn(f"m{p}")
                        dve.wait_ge(s_mhi, i * NPAIR + p + 1)
                        dve.scalar_tensor_tensor(out=mrow[0:8, 1, :], in0=pj[b][0:8, 0:P], scalar=-1.0,
                                                 in1=mrow[0:8, 0, :].bitcast(F32), op0=ALU.mult,
                                                 op1=ALU.subtract).then_inc(s_pje[b], 1)
                    if s >= 4 and s % 2 == 0:
                        inverse_sums(i, (s - 4) // 2)
                    if s == 2:
                        dve.wait_ge(s_x, i * 16 + 32)
                        ln_stats(i, 0, 0, x_in)
                    if s == NPAIR - 1:
                        dve.wait_ge(s_spa, i * (4 * NPAIR) + 4 * NPAIR)
                        dve.wait_ge(s_spv, i * L0N + 8 * NPAIR)
                        ln_apply(i, 0, 0, x_in, xn0)
                        ln_stats(i, 0, 1, xn0)
                    if s == NPAIR:
                        residual0(i)
                        ln_apply(i, 0, 1, xn0, hn0)
                        for k in range(NT):
                            add_last_head(i, k)
                    if s + 1 < NPAIR:
                        split_high(s + 1, entry(i, f"q{s + 1}"), entry(i, f"k{s + 1}"),
                                   i * MXN + 8 * (s - 1) if s >= 2 else None)
                    if s < NPAIR:
                        for n in range(8):
                            j, q = divmod(n, NT)
                            m = 8 * s + n
                            width = P * (q + 1)
                            scores_there = dve.to_reg(i * MXN + m + 1)
                            junk_free = dve.to_reg(i * MXN + m - 1) if m >= 2 else 0
                            dve.wait_ge(s_vset, N_VSET)
                            dve.wait_ge(s_mxf, scores_there)
                            if m >= 2:
                                dve.wait_ge(s_mxd, junk_free)
                            dve.tensor_tensor_reduce(out=junk[:, m % 2, 0:width], in0=mxp[m % MXB][:, 0:width],
                                                     in1=causal[:, T - width:T], scale=1.0, scalar=MASKED,
                                                     op0=ALU.add, op1=ALU.max,
                                                     accum_out=mx[:, s % 2, n:n + 1]).then_inc(s_mxd, 1)
                            if s + 1 < NPAIR and n % 2 == 1:
                                split_low(i, s + 1, n // 2)
                inverse_sums(i, HP - 1)
                p = NPAIR - 1
                dve.wait_ge(s_rb, i * (32 * HP) + 32 * HP)
                dve.wait_ge(s_att, i * NPAIR + NPAIR)
                dve.tensor_tensor(att[:, p, :], att[:, p, :], rbc[:, p % 2, :], ALU.mult).then_inc(s_nrmv, 1)
                b, u = pjn("wo0")
                dve.wait_ge(s_pjf[b], i * PB + u)
                dve.tensor_tensor(xacc[:, :, :], pj[b][:, :].rearrange("p (t d) -> p t d", t=NT), xb[:, :, :],
                                  ALU.add).then_inc(s_pje[b], 1)
                dve.wait_ge(s_pje[b], i * PB + u)
                ln_stats(i, 1, 0, xacc)
                ffn_dve(i, 0, 0)
                ffn_dve(i, 0, 1)
                ln_apply(i, 1, 0, xacc, xn1)
                ffn_dve(i, 0, 2)
                ffn_dve(i, 0, 3)
                for w in range(2):
                    n_rot, n_part = i * 4 + 2 * w, i * 6 + 3 * w
                    for tmp, c, name in ((rope_a, 0, "rq" if w == 0 else "rk"), (rope_b, 1, "rqs" if w == 0 else "rks")):
                        b, u = pjn(name)
                        dve.wait_ge(s_pjf[b], i * PB + u)
                        dve.tensor_tensor(tmp, pj[b][:, :], rope[:, c, :], ALU.mult).then_inc(s_pje[b], 1)
                    for name in (("rq", "rqs"), ("rk", "rks"))[w]:
                        b, u = pjn(name)
                        dve.wait_ge(s_pje[b], i * PB + u)
                    dve.tensor_tensor(rot, rope_a, rope_b, ALU.add).then_inc(s_rot, 1)
                    dve.wait_ge(s_rot, n_rot + 1)
                    dve.tensor_copy(parts[w][0], rot).then_inc(s_part, 1)
                    dve.wait_ge(s_part, n_part + 1)
                    dve.tensor_tensor(rest, rot, parts[w][0], ALU.subtract).then_inc(s_rot, 1)
                    dve.wait_ge(s_rot, n_rot + 2)
                    dve.tensor_copy(parts[w][1], rest).then_inc(s_part, 1)
                    dve.wait_ge(s_part, n_part + 2)
                    dve.tensor_tensor(parts[w][2], rest, parts[w][1], ALU.subtract).then_inc(s_part, 1)
                ffn_end(i, 0, xb, x_in)
                for t in range(L1_STEPS):
                    if t == LN_AT:
                        layer_norm(i, 1, 1, xn1, hn1)
                    if t == SPLIT_AT:
                        entry_split(i)
                    if (g := l1_rows(t)) is not None:
                        b, u = pjn(f"n{g}")
                        n = i * 2 * NG + 2 * g
                        dve.wait_ge(s_nth, i * NG + g + 1)
                        dve.scalar_tensor_tensor(out=nrest[:, :], in0=pj[b][0:16, 0:P], scalar=-1.0, in1=nrow[:, 0, :],
                                                 op0=ALU.mult, op1=ALU.subtract).then_inc(s_pje[b], 1)
                        dve.wait_ge(s_pje[b], i * PB + u)
                        dve.tensor_copy(nrow[:, 1, :], nrest[:, :]).then_inc(s_nt, 1)
                        dve.wait_ge(s_nt, n + 1)
                        dve.tensor_tensor(nrow[:, 2, :], nrest[:, :], nrow[:, 1, :], ALU.subtract).then_inc(s_nt, 1)
                    if (g := l1_heads(t, OUT_AT)) is not None:
                        head_norm_a(i, g)
                    if (g := l1_heads(t, OUT_AT + NORM_LAG)) is not None:
                        head_norm_b(i, g)
                    if t < NU:
                        g, n = divmod(t, GU)
                        m = L0N + t
                        dve.wait_ge(s_mxf, i * MXN + m + 1)
                        dve.reduce_max(mx[:, g % 2, n:n + 1], mxp[m % MXB][:, :], AXIS.X).then_inc(s_mxd, 1)
                ffn_dve(i, 1, 0)
                head_norm_a(i, NG - 1)
                ffn_dve(i, 1, 1)
                head_norm_b(i, NG - 1)
                ffn_dve(i, 1, 2)
                ffn_dve(i, 1, 3)
                ffn_end(i, 1, xacc, xacc)
                b, u = pjn("wo1")
                bf, uf = pjn("fb")
                dve.wait_ge(s_pjf[b], i * PB + u)
                dve.wait_ge(s_pje[bf], i * PB + uf)
                dve.tensor_tensor(xacc[:, :, :], pj[b][:, :].rearrange("p (t d) -> p t d", t=NT), xacc[:, :, :],
                                  ALU.add).then_inc(s_pje[b], 1)

        @block.tensor
        def _(pe):
            pe.wait_ge(s_ld, NLOAD)
            pe.wait_ge(s_pset, N_PSET)
            pe.wait_ge(s_vprep, N_VPREP)
            pe.wait_ge(s_aprep, 8)
            used = []

            def bank(i, name):
                used.append(name)
                b, n = entry(i, name)
                if i is not None or PJ_ENTRY[name] >= 2:
                    pe.wait_ge(s_pje[b], n - 1)
                return pj[b], s_pjf[b]

            def transpose4(i, name, src):
                t, full = bank(i, name)
                for k in range(NT):
                    last = pe.transpose(t[:, P * k:P * (k + 1)], src(k), ident[:, :])
                last.then_inc(full, 1)

            def project(i, name, w, x, pieces):
                t, full = bank(i, name)
                for k in range(pieces):
                    c = T // pieces
                    last = pe.matmul(t[:, c * k:c * (k + 1)], w(k), x(k), start=True, stop=True)
                last.then_inc(full, 1)

            def ffn_first(i, l, f):
                if f == 0:
                    b, n = entry(i, f"hT{l}")
                    pe.wait_ge(s_pje[b], n)
                project(i, f"y{'ab'[l]}{f}", lambda k: w1[:, l, P * f:P * (f + 1)], lambda k: hT[l][:, :], 1)

            def ffn_second(i, l):
                pe.wait_ge(s_y, before(i, l, NF) + NF)
                t, full = bank(i, "f" + "ab"[l])
                for k in range(NT):
                    for f in range(NF):
                        last = pe.matmul(t[:, D * k:D * (k + 1)], y[:, f, P * k:P * (k + 1)], w2[:, l, D * f:D * (f + 1)],
                                         start=f == 0, stop=f == NF - 1)
                last.then_inc(full, 1)

            def project_qk(i, p):
                project(i, f"q{p}", lambda k: wqkv[:, P * p:P * (p + 1)], lambda k: xnT[:, :], 1)
                project(i, f"k{p}", lambda k: wqkv[:, INNER + P * p:INNER + P * (p + 1)], lambda k: xnT[:, :], 1)

            def max_scores0(i, p, n):
                b = p % 3
                j, q = divmod(n, NT)
                m = 8 * p + n
                width = max(P * (q + 1), 2 * P)
                if n == 0:
                    pe.wait_ge(s_spv, i * L0N + 8 * p + 8)
                    pe.wait_ge(s_spa, i * (4 * NPAIR) + 4 * p + 4)
                if m >= MXB:
                    pe.wait_ge(s_mxd, i * MXN + m - MXB + 1)
                for x, y_, rows, first in ((QA, KA, P, True), (QB, KB, ROW_MAX, False)):
                    last = pe.matmul(mxp[m % MXB][:, 0:width], x[0:rows, b, j, P * q:P * (q + 1)],
                                     y_[0:rows, b, j, 0:width], start=first, stop=not first)
                last.then_inc(s_mxf, 1)

            def key_scores0(i, p, n):
                b = p % 3
                j, k = divmod(n, NT)
                m = 8 * p + n
                q0 = min(P * k, T - 2 * P)
                if n == 0:
                    pe.wait_ge(s_mdma[p % 2], i * (16 * NPAIR) + 32 * (p // 2 + 1))
                if m >= STB:
                    pe.wait_ge(s_exp, i * MXN + m - STB + 1)
                for x, y_, rows, first in ((KA, QA, P, True), (KB, QB, ROW_MAX + 2, False)):
                    last = pe.matmul(stp[m % STB][:, 0:T - q0], x[0:rows, b, j, P * k:P * (k + 1)],
                                     y_[0:rows, b, j, q0:T], start=first, stop=False, skip_group_check=True)
                c0 = P * k - q0
                last = pe.matmul(stp[m % STB][:, c0:c0 + P], identb[:, :], causalb[:, :], start=False, stop=True,
                                 skip_group_check=True)
                last.then_inc(s_st, 1)

            def pv0(i, p):
                pe.wait_ge(s_exp, i * MXN + 8 * p + 8)
                if p >= 1:
                    pe.wait_ge(s_att, i * NPAIR + p)
                for k in range(NT):
                    for j in range(2):
                        base = (2 * (p % 2) + j) * PT0 + OFFS[k]
                        last = pe.matmul(op[DH * j:DH * (j + 1), P * k:T], v0[:, k, DH * (2 * p + j):DH * (2 * p + j + 1)],
                                         pt[:, base:base + WIDTH[k]], start=k == 0, stop=k == NT - 1)
                last.then_inc(s_pv, 1)

            def pv1(i, g, k):
                pe.wait_ge(s_exp, i * MXN + L0N + GS * (NT * g + k) + GS)
                if k == 0 and g >= 1:
                    pe.wait_ge(s_or, i * NG + g)
                for j in range(GS):
                    last = pe.matmul(op[32 * j:32 * (j + 1), :], v1[:, k, (GS * g + j) // 2, :],
                                     pt[:, (GS * (k % 2) + j) * T:(GS * (k % 2) + j + 1) * T], start=k == 0, stop=k == NT - 1)
                last.then_inc(s_pv1, 1)

            def entry_transposes(i, part):
                pe.wait_ge(s_lnv, before(i, 0, 24) + 12 * (part + 1))
                if part == 0:
                    transpose4(i, "xnT0", lambda k: xn0[:, k, :])
                else:
                    transpose4(i, "hT0", lambda k: hn0[:, k, :])

            def entry_qk(i):
                b, n = entry(i, "xnT0")
                pe.wait_ge(s_pje[b], n)
                project_qk(i, 0)

            def entry_values(i, lo, hi):
                for n in range(lo, hi):
                    project(i, f"v{n}", lambda k: xnT[:, P * (n // 2):P * (n // 2 + 1)],
                            lambda k: wqkv[:, 2 * INNER + T * (n % 2):2 * INNER + T * (n % 2 + 1)], 1)

            entry_transposes(None, 0)
            entry_transposes(None, 1)
            entry_qk(None)
            entry_values(None, 0, 2 * NT)
            for f in range(NF):
                ffn_first(None, 0, f)
            ffn_second(None, 0)
            assert used == ENTRY_ALL
            with pe.Fori(0, NB) as i:
                used.clear()
                for s in range(NPAIR + 2):
                    if 1 <= s <= NPAIR:
                        pe.wait_ge(s_mxd, i * MXN + 8 * s)
                        t, full = bank(i, f"m{s - 1}")
                        pe.transpose(t[0:8, 0:P], mx[:, (s - 1) % 2, 0:8], ident[:, :]).then_inc(full, 1)
                    if s + 1 < NPAIR:
                        project_qk(i, s + 1)
                    early = MAX_EARLY if 1 <= s < NPAIR else 0
                    for n in range(early):
                        max_scores0(i, s, n)
                    if s >= 2:
                        pv0(i, s - 2)
                    if s == NPAIR:
                        entry_transposes(i, 0)
                    for n in range(8):
                        if s < NPAIR and n + early < 8:
                            max_scores0(i, s, n + early)
                        if 1 <= s <= NPAIR:
                            key_scores0(i, s - 1, n)
                        if s == NPAIR and n == HT0_AT:
                            entry_transposes(i, 1)
                        if s == NPAIR and n == QK_AT:
                            entry_qk(i)
                    if s == NPAIR + 1:
                        entry_values(i, 0, V_EARLY)
                    if s >= 3 and s % 2 == 1:
                        g = (s - 3) // 2
                        t, full = bank(i, f"l{g}")
                        pe.wait_ge(s_psum, i * PSN + min(16 * (g + 1), PSN))
                        if g == HP - 1:
                            pe.wait_ge(s_psv, i * NT + NT)
                        for c in range(4):
                            last = pe.matmul(t[32 * c:32 * (c + 1), :], ones[:, :], psums[:, c, :], start=True, stop=True)
                        last.then_inc(full, 1)
                entry_values(i, V_EARLY, 2 * NT)
                t, full = bank(i, "wo0")
                for p in range(NPAIR):
                    if p < NPAIR - 1:
                        pe.wait_ge(s_nrm, i * (NPAIR - 1) + p + 1)
                    else:
                        pe.wait_ge(s_nrmv, i + 1)
                    for k in range(NT):
                        last = pe.matmul(t[:, D * k:D * (k + 1)], att[:, p, P * k:P * (k + 1)], wout[:, p, :],
                                         start=p == 0 and k == 0, stop=p == NPAIR - 1, skip_group_check=True)
                last.then_inc(full, 1)
                for f in range(NF):
                    ffn_first(i, 0, f)
                pe.wait_ge(s_lnv, before(i, 1, 24) + 12)
                transpose4(i, "xnT1", lambda k: xn1[:, k, :])
                b, u = pjn("xnT1")
                pe.wait_ge(s_pje[b], i * PB + u)
                for c, name in enumerate(("rq", "rqs", "rk", "rks")):
                    project(i, name, lambda k: w_l1[:, c, :], lambda k: xnT1[:, :], 1)
                project(i, "vals", lambda k: xnT1[:, P * k:P * (k + 1)], lambda k: w_l1[:, 4, :], NT)
                ffn_second(i, 0)
                b, u = pjn("vals")
                pe.wait_ge(s_pje[b], i * PB + u)
                pe.wait_ge(s_stk, i * NSTK + NSTK)
                for t in range(L1_STEPS):
                    if (g := l1_rows(t)) is not None:
                        pe.wait_ge(s_mxd, i * MXN + L0N + GU * (g + 1))
                        rows, full = bank(i, f"n{g}")
                        pe.transpose(rows[0:16, 0:P], mx[:, g % 2, 0:16], ident[:, :]).then_inc(full, 1)
                    if (g := l1_heads(t, OUT_AT)) is not None:
                        pe.wait_ge(s_or, i * NG + g + 1)
                        transpose4(i, f"o{g}", lambda k: oraw[:, g % 2, P * k:P * (k + 1)])
                    if (n := t - KEY_LAG) >= 0:
                        g, r = divmod(n, GU)
                        k, j = divmod(r, GS)
                        if r == 0:
                            pe.wait_ge(s_nd[g % 2], i * 96 + 48 * (g // 2 + 1))
                        pe.wait_ge(s_exp, i * MXN + L0N + n - STB + 1)
                        pe.matmul(stp[(L0N + n) % STB][:, :], KS[0:ROW_MAX + 3, GS * g + j, P * k:P * (k + 1)],
                                  QS[0:ROW_MAX + 3, GS * g + j, :], start=True, stop=True).then_inc(s_st, 1)
                    if t < NU:
                        sub, q = divmod(t, NT)
                        m = L0N + t
                        pe.wait_ge(s_mxd, i * MXN + m - MXB + 1)
                        pe.matmul(mxp[m % MXB][:, :], QS[0:ROW_MAX, sub, P * q:P * (q + 1)],
                                  KS[0:ROW_MAX, sub, :], start=True, stop=True).then_inc(s_mxf, 1)
                    if n >= GS and n % GS == PV_AT:
                        pv1(i, *divmod(n // GS - 1, NT))
                    if t == HT_AT:
                        pe.wait_ge(s_lnv, before(i, 1, 24) + 24)
                        transpose4(i, "hT1", lambda k: hn1[:, k, :])
                ffn_first(i, 1, 0)
                pv1(i, NG - 1, NT - 1)
                ffn_first(i, 1, 1)
                pe.wait_ge(s_or, i * NG + NG)
                transpose4(i, f"o{NG - 1}", lambda k: oraw[:, (NG - 1) % 2, P * k:P * (k + 1)])
                ffn_first(i, 1, 2)
                ffn_first(i, 1, 3)
                pe.wait_ge(s_tl, i * 7 * NG + 7 * NG)
                transpose4(i, "oT", lambda k: o1[:, k, :])
                ffn_second(i, 1)
                b, u = pjn("oT")
                pe.wait_ge(s_pje[b], i * PB + u)
                project(i, "wo1", lambda k: o1T[:, P * k:P * (k + 1)], lambda k: w_l1[:, 5, :], NT)
                assert used == pj_order()


def kernel(**inputs):
    import concourse.bacc as bacc
    from concourse.bass_utils import run_bass_kernel_spmd

    nc = bacc.Bacc("TRN2", target_bir_lowering=False, num_devices=1)
    data = {k: np.ascontiguousarray(v) for k, v in inputs.items()}
    swap = np.arange(D) ^ 1
    for n in "qkvo":
        w = data.pop(f"L1_attn_W{n}")
        data[f"t_W{n}T"] = np.ascontiguousarray(w.T)
        if n in "qk":
            data[f"t_W{n}sT"] = np.ascontiguousarray(w[swap].T)
    data.update(tables())
    arrays, a = {}, {}
    for name, v in data.items():
        arrays[f"in_{name}"] = v
        a[name] = nc.dram_tensor(f"in_{name}", v.shape, mybir.dt.from_np(v.dtype), kind="ExternalInput").ap()
    out = nc.dram_tensor("out_x", (NB, T, D), F32, kind="ExternalOutput").ap()
    build_program(nc, a, out)
    r = run_bass_kernel_spmd(nc, [arrays], core_ids=[0])
    return r.results[0]["out_x"]
```
